# Optimizing a Trainium2 kernel written in Bass

```python
import numpy as np
import jax
import jax.numpy as jnp

def _softmax(x, axis=-1):
    return jax.nn.softmax(x, axis=axis)

def _gelu(x):
    return jax.nn.gelu(x, approximate=True)

def _silu(x):
    return jax.nn.silu(x)

def _sigmoid(x):
    return jax.nn.sigmoid(x)

def _layernorm(x, axis=-1, eps=1e-05):
    m = jnp.mean(x, axis=axis, keepdims=True)
    v = jnp.var(x, axis=axis, keepdims=True)
    return (x - m) / jnp.sqrt(v + eps)

def _scatter_add(tgt, idx, src, axis=0):
    return tgt.at[idx].add(src)

def _segment_sum(src, seg, n):
    return jax.ops.segment_sum(src, seg, n)
kernel_name = 'mk_xattn_ffn_d4_seqx_r8_09b288'

def setup_inputs(seed: int=0):
    np.random.seed(seed)
    _w = jnp.asarray

    def _rec_inputs():
        import jax
        import jax.numpy as jnp
        _rk = jax.random.key(seed)
        x = 7.22e-05 + 1 * jax.random.normal(jax.random.fold_in(_rk, 1), (4, 256, 256), jnp.float32)
        _lenS = 256 - jax.random.randint(jax.random.fold_in(_rk, 7), (4,), 0, max(1, 256 // 4) + 1, jnp.int32)
        _lenS2 = 512 - jax.random.randint(jax.random.fold_in(_rk, 8), (4,), 0, max(1, 512 // 4) + 1, jnp.int32)
        _ctx_1024P = jax.random.normal(jax.random.fold_in(_rk, 11), (4, 16, 128), jnp.float32)
        _ctx_1024c = jax.random.dirichlet(jax.random.fold_in(_rk, 511), 0.3 * jnp.ones((16,), jnp.float32), (4, 512))
        _ctx_1024t = jnp.einsum('bsk,bkd->bsd', _ctx_1024c, _ctx_1024P)
        _ctx_1024t = _ctx_1024t * jax.lax.rsqrt(jnp.mean(jnp.square(_ctx_1024t)) + 1e-12) * 0.953939
        ctx_1024 = -0.000673644 + 1.00013 * (_ctx_1024t + 0.3 * jax.random.normal(jax.random.fold_in(_rk, 611), (4, 512, 128), jnp.float32))
        _validS = jnp.arange(256)[None, :] < _lenS[:, None]
        _validS2 = jnp.arange(512)[None, :] < _lenS2[:, None]
        _causal = jnp.tril(jnp.ones((256, 256), dtype=bool))
        mask_BxS2_bf1 = jnp.ones((4, 512), dtype=bool)
        return (x, ctx_1024, mask_BxS2_bf1)
    x, ctx_1024, mask_BxS2_bf1 = _rec_inputs()

    def _L0_xattn_setup():
        import jax, jax.numpy as jnp
        import numpy as np
        B, S1, S2, DCA = (2, 256, 128, 16)
        QDIM, KDIM, H = (256, 128, 16)
        HD = QDIM // H
        SCALE = HD ** (-0.5)
        EPS = 1e-06
        DCA_WEIGHT = 1.0

        def _ln(t, w, b):
            m = jnp.mean(t, axis=-1, keepdims=True)
            v = jnp.var(t, axis=-1, keepdims=True)
            return (t - m) * jax.lax.rsqrt(v + EPS) * w + b

        def _attn(q, k, v):
            s = jnp.einsum('bhqd,bhkd->bhqk', q, k) * SCALE
            p = jax.nn.softmax(s, axis=-1)
            return jnp.einsum('bhqk,bhkd->bhqd', p, v)
        key = jax.random.key(seed)
        ks = jax.random.split(key, 8)
        w = lambda k, shape: jax.random.normal(k, shape, jnp.float32) * 0.02
        return {'x': jax.random.normal(ks[0], (B, S1, QDIM), jnp.float32), 'y': jax.random.normal(ks[1], (B, S2 + DCA, KDIM), jnp.float32), 'Wq': w(ks[2], (QDIM, QDIM)), 'bq': jnp.zeros((QDIM,), jnp.float32), 'Wk': w(ks[3], (KDIM, QDIM)), 'bk': jnp.zeros((QDIM,), jnp.float32), 'Wv': w(ks[4], (KDIM, QDIM)), 'bv': jnp.zeros((QDIM,), jnp.float32), 'Wkv_dca': w(ks[5], (KDIM, 2 * QDIM)), 'bkv_dca': jnp.zeros((2 * QDIM,), jnp.float32), 'qn_w': jnp.ones((HD,), jnp.float32), 'qn_b': jnp.zeros((HD,), jnp.float32), 'kn_w': jnp.ones((HD,), jnp.float32), 'kn_b': jnp.zeros((HD,), jnp.float32), 'kn_dca_w': jnp.ones((HD,), jnp.float32), 'kn_dca_b': jnp.zeros((HD,), jnp.float32), 'Wo': w(ks[6], (QDIM, QDIM)), 'bo': jnp.zeros((QDIM,), jnp.float32)}
    _L0_xattn_all = _L0_xattn_setup()
    _L0_xattn_in = {k: v for k, v in _L0_xattn_all.items() if k in ('Wq', 'bq', 'Wk', 'bk', 'Wv', 'bv', 'Wkv_dca', 'bkv_dca', 'qn_w', 'qn_b', 'kn_w', 'kn_b', 'kn_dca_w', 'kn_dca_b', 'Wo', 'bo')}
    del _L0_xattn_all

    def _L0_ffn_setup():
        import jax, jax.numpy as jnp
        import numpy as np

        def _sparsify_2to4(h):
            B, S, I = h.shape
            g = h.reshape(B, S, I // 4, 4)
            a = jnp.abs(g)
            _, idx = jax.lax.top_k(a, 2)
            pos = jnp.arange(4)
            mask = (pos == idx[..., 0:1]) | (pos == idx[..., 1:2])
            return (g * mask.astype(g.dtype)).reshape(B, S, I)
        key = jax.random.key(seed)
        k1, k2, k3, k4 = jax.random.split(key, 4)
        B, S, H, I = (4, 256, 256, 1024)
        x = jax.random.normal(k1, (B, S, H), dtype=jnp.float32)
        w_gate = jax.random.normal(k2, (H, I), dtype=jnp.float32) / np.sqrt(H)
        w_up = jax.random.normal(k3, (H, I), dtype=jnp.float32) / np.sqrt(H)
        w_down = jax.random.normal(k4, (I, H), dtype=jnp.float32) / np.sqrt(I)
        return {'x': x, 'w_gate': w_gate, 'w_up': w_up, 'w_down': w_down}
    _L0_ffn_all = _L0_ffn_setup()
    _L0_ffn_in = {k: v for k, v in _L0_ffn_all.items() if k in ('w_gate', 'w_up', 'w_down')}
    del _L0_ffn_all

    def _L1_xattn_setup():
        import jax, jax.numpy as jnp
        import numpy as np
        EPS = 1e-05

        def rmsnorm(x, g, eps=EPS):
            var = jnp.mean(jnp.square(x), axis=-1, keepdims=True)
            return x * jax.lax.rsqrt(var + eps) * g
        key = jax.random.key(seed)
        ks = jax.random.split(key, 8)
        B, Sq, Skv = (2, 512, 64)
        dim, cdim, H, D = (256, 128, 16, 128)
        inner = H * D
        s = lambda f: 1.0 / np.sqrt(f)
        return {'hidden_states': jax.random.normal(ks[0], (B, Sq, dim), jnp.float32), 'encoder_hidden_states': jax.random.normal(ks[1], (B, Skv, cdim), jnp.float32), 'Wq': jax.random.normal(ks[2], (dim, inner), jnp.float32) * s(dim), 'Wk': jax.random.normal(ks[3], (cdim, inner), jnp.float32) * s(cdim), 'Wv': jax.random.normal(ks[4], (cdim, inner), jnp.float32) * s(cdim), 'Wo': jax.random.normal(ks[5], (inner, dim), jnp.float32) * s(inner), 'gq': jnp.ones((D,), jnp.float32), 'gk': jnp.ones((D,), jnp.float32)}
    _L1_xattn_all = _L1_xattn_setup()
    _L1_xattn_in = {k: v for k, v in _L1_xattn_all.items() if k in ('Wq', 'Wk', 'Wv', 'Wo', 'gq', 'gk')}
    del _L1_xattn_all

    def _L1_ffn_setup():
        import jax, jax.numpy as jnp
        import numpy as np
        EPS = 1e-06
        K_STEPS = 4
        USE_GATING = True

        def layer_norm(x, gamma, beta):
            mu = jnp.mean(x, axis=-1, keepdims=True)
            var = jnp.mean(jnp.square(x - mu), axis=-1, keepdims=True)
            return (x - mu) * jax.lax.rsqrt(var + EPS) * gamma + beta
        key = jax.random.key(seed)
        B, L, D, H = (4, 512, 256, 1024)
        ks = jax.random.split(key, 16)
        s = 0.02
        return {'x': jax.random.normal(ks[0], (B, L, D), dtype=jnp.float32), 'in_gamma': jnp.ones((D,), jnp.float32), 'in_beta': jnp.zeros((D,), jnp.float32), 'agg_w': jax.random.normal(ks[1], (D, D), jnp.float32) * s, 'agg_b': jnp.zeros((D,), jnp.float32), 'pn_gamma': jnp.ones((D,), jnp.float32), 'pn_beta': jnp.zeros((D,), jnp.float32), 'd1_w': jax.random.normal(ks[2], (D, H), jnp.float32) * s, 'd1_b': jnp.zeros((H,), jnp.float32), 'd2_w': jax.random.normal(ks[3], (H, D), jnp.float32) * s, 'd2_b': jnp.zeros((D,), jnp.float32), 'bc_w': jax.random.normal(ks[4], (D, D), jnp.float32) * s, 'bc_b': jnp.zeros((D,), jnp.float32), 'gate_w': jax.random.normal(ks[5], (D, D), jnp.float32) * s, 'gate_b': jnp.zeros((D,), jnp.float32), 'out_gamma': jnp.ones((D,), jnp.float32), 'out_beta': jnp.zeros((D,), jnp.float32)}
    _L1_ffn_all = _L1_ffn_setup()
    _L1_ffn_in = {k: v for k, v in _L1_ffn_all.items() if k in ('in_gamma', 'in_beta', 'agg_w', 'agg_b', 'pn_gamma', 'pn_beta', 'd1_w', 'd1_b', 'd2_w', 'd2_b', 'bc_w', 'bc_b', 'gate_w', 'gate_b', 'out_gamma', 'out_beta')}
    del _L1_ffn_all

    def _L2_xattn_setup():
        import jax, jax.numpy as jnp
        import numpy as np
        N_HEADS = 16
        N_KV_HEADS = 8
        HEAD_DIM = 128
        D_TEXT = 256
        D_VISION = 128
        GROUPS = N_HEADS // N_KV_HEADS
        key = jax.random.key(seed)
        ks = jax.random.split(key, 6)
        B, T_text, T_vis = (4, 256, 72)
        text_hidden = jax.random.normal(ks[0], (B, T_text, D_TEXT), dtype=jnp.float32)
        vision_tokens = jax.random.normal(ks[1], (B, T_vis, D_VISION), dtype=jnp.float32)
        vision_mask = jnp.ones((B, T_vis), dtype=bool)
        s = 0.02
        Wq = jax.random.normal(ks[2], (D_TEXT, N_HEADS * HEAD_DIM), dtype=jnp.float32) * s
        Wk = jax.random.normal(ks[3], (D_VISION, N_KV_HEADS * HEAD_DIM), dtype=jnp.float32) * s
        Wv = jax.random.normal(ks[4], (D_VISION, N_KV_HEADS * HEAD_DIM), dtype=jnp.float32) * s
        Wo = jax.random.normal(ks[5], (N_HEADS * HEAD_DIM, D_TEXT), dtype=jnp.float32) * s
        return {'text_hidden': text_hidden, 'vision_tokens': vision_tokens, 'vision_mask': vision_mask, 'Wq': Wq, 'Wk': Wk, 'Wv': Wv, 'Wo': Wo}
    _L2_xattn_all = _L2_xattn_setup()
    _L2_xattn_in = {k: v for k, v in _L2_xattn_all.items() if k in ('Wq', 'Wk', 'Wv', 'Wo')}
    del _L2_xattn_all

    def _L2_ffn_setup():
        import jax, jax.numpy as jnp
        import numpy as np
        B, S, H = (2, 64, 256)
        E, I, K = (64, 176, 6)
        NS = 2
        SH_I = I * NS
        key = jax.random.key(seed)
        ks = jax.random.split(key, 6)
        s = 0.02
        return {'hidden_states': jax.random.normal(ks[0], (B, S, H), jnp.float32), 'gate_w': jax.random.normal(ks[1], (E, H), jnp.float32) * s, 'experts_w1': jax.random.normal(ks[2], (E, I, H), jnp.float32) * s, 'experts_w2': jax.random.normal(ks[3], (E, H, I), jnp.float32) * s, 'shared_gate_up': jax.random.normal(ks[4], (2 * SH_I, H), jnp.float32) * s, 'shared_down': jax.random.normal(ks[5], (H, SH_I), jnp.float32) * s}
    _L2_ffn_all = _L2_ffn_setup()
    _L2_ffn_in = {k: v for k, v in _L2_ffn_all.items() if k in ('gate_w', 'experts_w1', 'experts_w2', 'shared_gate_up', 'shared_down')}
    del _L2_ffn_all

    def _L3_xattn_setup():
        import jax, jax.numpy as jnp
        import numpy as np
        N_HEADS = 16
        N_KV_HEADS = 8
        HEAD_DIM = 128
        D_TEXT = 256
        D_VISION = 128
        GROUPS = N_HEADS // N_KV_HEADS
        key = jax.random.key(seed)
        ks = jax.random.split(key, 6)
        B, T_text, T_vis = (4, 256, 72)
        text_hidden = jax.random.normal(ks[0], (B, T_text, D_TEXT), dtype=jnp.float32)
        vision_tokens = jax.random.normal(ks[1], (B, T_vis, D_VISION), dtype=jnp.float32)
        vision_mask = jnp.ones((B, T_vis), dtype=bool)
        s = 0.02
        Wq = jax.random.normal(ks[2], (D_TEXT, N_HEADS * HEAD_DIM), dtype=jnp.float32) * s
        Wk = jax.random.normal(ks[3], (D_VISION, N_KV_HEADS * HEAD_DIM), dtype=jnp.float32) * s
        Wv = jax.random.normal(ks[4], (D_VISION, N_KV_HEADS * HEAD_DIM), dtype=jnp.float32) * s
        Wo = jax.random.normal(ks[5], (N_HEADS * HEAD_DIM, D_TEXT), dtype=jnp.float32) * s
        return {'text_hidden': text_hidden, 'vision_tokens': vision_tokens, 'vision_mask': vision_mask, 'Wq': Wq, 'Wk': Wk, 'Wv': Wv, 'Wo': Wo}
    _L3_xattn_all = _L3_xattn_setup()
    _L3_xattn_in = {k: v for k, v in _L3_xattn_all.items() if k in ('Wq', 'Wk', 'Wv', 'Wo')}
    del _L3_xattn_all

    def _L3_ffn_setup():
        import jax, jax.numpy as jnp
        import numpy as np
        HIDDEN = 256
        INTER = 96
        N_EXPERTS = 32
        TOP_K = 8
        key = jax.random.key(seed)
        k = jax.random.split(key, 5)
        s = 1.0 / np.sqrt(HIDDEN)
        return {'hidden_states': jax.random.normal(k[0], (1, 128, HIDDEN), jnp.float32), 'gate_w': jax.random.normal(k[1], (HIDDEN, N_EXPERTS), jnp.float32) * s, 'w_gate': jax.random.normal(k[2], (N_EXPERTS, HIDDEN, INTER), jnp.float32) * s, 'w_up': jax.random.normal(k[3], (N_EXPERTS, HIDDEN, INTER), jnp.float32) * s, 'w_down': jax.random.normal(k[4], (N_EXPERTS, INTER, HIDDEN), jnp.float32) * (1.0 / np.sqrt(INTER))}
    _L3_ffn_all = _L3_ffn_setup()
    _L3_ffn_in = {k: v for k, v in _L3_ffn_all.items() if k in ('gate_w', 'w_gate', 'w_up', 'w_down')}
    del _L3_ffn_all
    return {'x': x, 'ctx_1024': ctx_1024, 'mask_BxS2_bf1': mask_BxS2_bf1, 'L0_xattn_Wq': _L0_xattn_in['Wq'], 'L0_xattn_bq': _L0_xattn_in['bq'], 'L0_xattn_Wk': _L0_xattn_in['Wk'], 'L0_xattn_bk': _L0_xattn_in['bk'], 'L0_xattn_Wv': _L0_xattn_in['Wv'], 'L0_xattn_bv': _L0_xattn_in['bv'], 'L0_xattn_Wkv_dca': _L0_xattn_in['Wkv_dca'], 'L0_xattn_bkv_dca': _L0_xattn_in['bkv_dca'], 'L0_xattn_qn_w': _L0_xattn_in['qn_w'], 'L0_xattn_qn_b': _L0_xattn_in['qn_b'], 'L0_xattn_kn_w': _L0_xattn_in['kn_w'], 'L0_xattn_kn_b': _L0_xattn_in['kn_b'], 'L0_xattn_kn_dca_w': _L0_xattn_in['kn_dca_w'], 'L0_xattn_kn_dca_b': _L0_xattn_in['kn_dca_b'], 'L0_xattn_Wo': _L0_xattn_in['Wo'], 'L0_xattn_bo': _L0_xattn_in['bo'], 'L0_ffn_w_gate': _L0_ffn_in['w_gate'], 'L0_ffn_w_up': _L0_ffn_in['w_up'], 'L0_ffn_w_down': _L0_ffn_in['w_down'], 'L1_xattn_Wq': _L1_xattn_in['Wq'], 'L1_xattn_Wk': _L1_xattn_in['Wk'], 'L1_xattn_Wv': _L1_xattn_in['Wv'], 'L1_xattn_Wo': _L1_xattn_in['Wo'], 'L1_xattn_gq': _L1_xattn_in['gq'], 'L1_xattn_gk': _L1_xattn_in['gk'], 'L1_ffn_in_gamma': _L1_ffn_in['in_gamma'], 'L1_ffn_in_beta': _L1_ffn_in['in_beta'], 'L1_ffn_agg_w': _L1_ffn_in['agg_w'], 'L1_ffn_agg_b': _L1_ffn_in['agg_b'], 'L1_ffn_pn_gamma': _L1_ffn_in['pn_gamma'], 'L1_ffn_pn_beta': _L1_ffn_in['pn_beta'], 'L1_ffn_d1_w': _L1_ffn_in['d1_w'], 'L1_ffn_d1_b': _L1_ffn_in['d1_b'], 'L1_ffn_d2_w': _L1_ffn_in['d2_w'], 'L1_ffn_d2_b': _L1_ffn_in['d2_b'], 'L1_ffn_bc_w': _L1_ffn_in['bc_w'], 'L1_ffn_bc_b': _L1_ffn_in['bc_b'], 'L1_ffn_gate_w': _L1_ffn_in['gate_w'], 'L1_ffn_gate_b': _L1_ffn_in['gate_b'], 'L1_ffn_out_gamma': _L1_ffn_in['out_gamma'], 'L1_ffn_out_beta': _L1_ffn_in['out_beta'], 'L2_xattn_Wq': _L2_xattn_in['Wq'], 'L2_xattn_Wk': _L2_xattn_in['Wk'], 'L2_xattn_Wv': _L2_xattn_in['Wv'], 'L2_xattn_Wo': _L2_xattn_in['Wo'], 'L2_ffn_gate_w': _L2_ffn_in['gate_w'], 'L2_ffn_experts_w1': _L2_ffn_in['experts_w1'], 'L2_ffn_experts_w2': _L2_ffn_in['experts_w2'], 'L2_ffn_shared_gate_up': _L2_ffn_in['shared_gate_up'], 'L2_ffn_shared_down': _L2_ffn_in['shared_down'], 'L3_xattn_Wq': _L3_xattn_in['Wq'], 'L3_xattn_Wk': _L3_xattn_in['Wk'], 'L3_xattn_Wv': _L3_xattn_in['Wv'], 'L3_xattn_Wo': _L3_xattn_in['Wo'], 'L3_ffn_gate_w': _L3_ffn_in['gate_w'], 'L3_ffn_w_gate': _L3_ffn_in['w_gate'], 'L3_ffn_w_up': _L3_ffn_in['w_up'], 'L3_ffn_w_down': _L3_ffn_in['w_down']}

def reference(x, ctx_1024, mask_BxS2_bf1, L0_xattn_Wq, L0_xattn_bq, L0_xattn_Wk, L0_xattn_bk, L0_xattn_Wv, L0_xattn_bv, L0_xattn_Wkv_dca, L0_xattn_bkv_dca, L0_xattn_qn_w, L0_xattn_qn_b, L0_xattn_kn_w, L0_xattn_kn_b, L0_xattn_kn_dca_w, L0_xattn_kn_dca_b, L0_xattn_Wo, L0_xattn_bo, L0_ffn_w_gate, L0_ffn_w_up, L0_ffn_w_down, L1_xattn_Wq, L1_xattn_Wk, L1_xattn_Wv, L1_xattn_Wo, L1_xattn_gq, L1_xattn_gk, L1_ffn_in_gamma, L1_ffn_in_beta, L1_ffn_agg_w, L1_ffn_agg_b, L1_ffn_pn_gamma, L1_ffn_pn_beta, L1_ffn_d1_w, L1_ffn_d1_b, L1_ffn_d2_w, L1_ffn_d2_b, L1_ffn_bc_w, L1_ffn_bc_b, L1_ffn_gate_w, L1_ffn_gate_b, L1_ffn_out_gamma, L1_ffn_out_beta, L2_xattn_Wq, L2_xattn_Wk, L2_xattn_Wv, L2_xattn_Wo, L2_ffn_gate_w, L2_ffn_experts_w1, L2_ffn_experts_w2, L2_ffn_shared_gate_up, L2_ffn_shared_down, L3_xattn_Wq, L3_xattn_Wk, L3_xattn_Wv, L3_xattn_Wo, L3_ffn_gate_w, L3_ffn_w_gate, L3_ffn_w_up, L3_ffn_w_down):
    import jax
    import jax.numpy as jnp

    def _L0_xattn_ref(x, y, Wq, bq, Wk, bk, Wv, bv, Wkv_dca, bkv_dca, qn_w, qn_b, kn_w, kn_b, kn_dca_w, kn_dca_b, Wo, bo):
        import jax, jax.numpy as jnp
        import numpy as np
        B, S1, S2, DCA = (2, 256, 128, 16)
        QDIM, KDIM, H = (256, 128, 16)
        HD = QDIM // H
        SCALE = HD ** (-0.5)
        EPS = 1e-06
        DCA_WEIGHT = 1.0

        def _ln(t, w, b):
            m = jnp.mean(t, axis=-1, keepdims=True)
            v = jnp.var(t, axis=-1, keepdims=True)
            return (t - m) * jax.lax.rsqrt(v + EPS) * w + b

        def _attn(q, k, v):
            s = jnp.einsum('bhqd,bhkd->bhqk', q, k) * SCALE
            p = jax.nn.softmax(s, axis=-1)
            return jnp.einsum('bhqk,bhkd->bhqd', p, v)
        b, s1, _ = x.shape
        y_dca = y[:, -DCA:, :]
        y_main = y[:, :-DCA, :]
        kv_dca = (y_dca @ Wkv_dca + bkv_dca).reshape(b, DCA, 2, H, HD)
        k_dca = _ln(kv_dca[:, :, 0], kn_dca_w, kn_dca_b)
        v_dca = kv_dca[:, :, 1]
        s2 = y_main.shape[1]
        q = _ln((x @ Wq + bq).reshape(b, s1, H, HD), qn_w, qn_b)
        kv = jnp.concatenate([y_main @ Wk + bk, y_main @ Wv + bv], axis=-1)
        kv = kv.reshape(b, s2, H, 2 * HD)
        k = _ln(kv[..., :HD], kn_w, kn_b)
        v = kv[..., HD:]
        qT = q.transpose(0, 2, 1, 3)
        ctx = _attn(qT, k.transpose(0, 2, 1, 3), v.transpose(0, 2, 1, 3))
        ctx = ctx.transpose(0, 2, 1, 3).reshape(b, s1, QDIM)
        ctx_dca = _attn(qT, k_dca.transpose(0, 2, 1, 3), v_dca.transpose(0, 2, 1, 3))
        ctx_dca = ctx_dca.transpose(0, 2, 1, 3).reshape(b, s1, QDIM)
        ctx = ctx + DCA_WEIGHT * ctx_dca
        return ctx @ Wo + bo

    def _L0_ffn_ref(x, w_gate, w_up, w_down):
        import jax, jax.numpy as jnp
        import numpy as np

        def _sparsify_2to4(h):
            B, S, I = h.shape
            g = h.reshape(B, S, I // 4, 4)
            a = jnp.abs(g)
            _, idx = jax.lax.top_k(a, 2)
            pos = jnp.arange(4)
            mask = (pos == idx[..., 0:1]) | (pos == idx[..., 1:2])
            return (g * mask.astype(g.dtype)).reshape(B, S, I)
        h = jax.nn.silu(jnp.einsum('bsh,hi->bsi', x, w_gate)) * jnp.einsum('bsh,hi->bsi', x, w_up)
        h_sparse = _sparsify_2to4(h)
        return jnp.einsum('bsi,ih->bsh', h_sparse, w_down)

    def _L1_xattn_ref(hidden_states, encoder_hidden_states, Wq, Wk, Wv, Wo, gq, gk):
        import jax, jax.numpy as jnp
        import numpy as np
        EPS = 1e-05

        def rmsnorm(x, g, eps=EPS):
            var = jnp.mean(jnp.square(x), axis=-1, keepdims=True)
            return x * jax.lax.rsqrt(var + eps) * g
        B, Sq, _ = hidden_states.shape
        Skv = encoder_hidden_states.shape[1]
        D = gq.shape[0]
        H = Wq.shape[1] // D
        scale = 1.0 / np.sqrt(D)
        q = (hidden_states @ Wq).reshape(B, Sq, H, D)
        k = (encoder_hidden_states @ Wk).reshape(B, Skv, H, D)
        v = (encoder_hidden_states @ Wv).reshape(B, Skv, H, D)
        q = rmsnorm(q, gq)
        k = rmsnorm(k, gk)
        scores = jnp.einsum('bqhd,bkhd->bhqk', q, k) * scale
        attn = jax.nn.softmax(scores, axis=-1)
        out = jnp.einsum('bhqk,bkhd->bqhd', attn, v)
        out = out.reshape(B, Sq, H * D)
        return out @ Wo

    def _L1_ffn_ref(x, in_gamma, in_beta, agg_w, agg_b, pn_gamma, pn_beta, d1_w, d1_b, d2_w, d2_b, bc_w, bc_b, gate_w, gate_b, out_gamma, out_beta):
        import jax, jax.numpy as jnp
        import numpy as np
        EPS = 1e-06
        K_STEPS = 4
        USE_GATING = True

        def layer_norm(x, gamma, beta):
            mu = jnp.mean(x, axis=-1, keepdims=True)
            var = jnp.mean(jnp.square(x - mu), axis=-1, keepdims=True)
            return (x - mu) * jax.lax.rsqrt(var + EPS) * gamma + beta
        x_norm = layer_norm(x, in_gamma, in_beta)
        thought = x_norm[:, -1, :] @ agg_w + agg_b
        for _ in range(K_STEPS):
            t = layer_norm(thought, pn_gamma, pn_beta)
            t = jax.nn.gelu(t @ d1_w + d1_b, approximate=False)
            thought = thought + (t @ d2_w + d2_b)
        broadcast = (thought @ bc_w + bc_b)[:, None, :]
        if USE_GATING:
            gate = jax.nn.sigmoid(x @ gate_w + gate_b)
            out = x + gate * broadcast
        else:
            out = x + broadcast
        return layer_norm(out, out_gamma, out_beta)

    def _L2_xattn_ref(text_hidden, vision_tokens, vision_mask, Wq, Wk, Wv, Wo):
        import jax, jax.numpy as jnp
        import numpy as np
        N_HEADS = 16
        N_KV_HEADS = 8
        HEAD_DIM = 128
        D_TEXT = 256
        D_VISION = 128
        GROUPS = N_HEADS // N_KV_HEADS
        B, T_text, _ = text_hidden.shape
        T_vis = vision_tokens.shape[1]
        scale = jnp.float32(np.sqrt(HEAD_DIM))
        q = (text_hidden @ Wq).reshape(B, T_text, N_HEADS, HEAD_DIM).transpose(0, 2, 1, 3)
        k = (vision_tokens @ Wk).reshape(B, T_vis, N_KV_HEADS, HEAD_DIM).transpose(0, 2, 1, 3)
        v = (vision_tokens @ Wv).reshape(B, T_vis, N_KV_HEADS, HEAD_DIM).transpose(0, 2, 1, 3)
        k = jnp.repeat(k, GROUPS, axis=1)
        v = jnp.repeat(v, GROUPS, axis=1)
        scores = jnp.einsum('bhtd,bhsd->bhts', q, k) / scale
        mask = vision_mask[:, None, None, :]
        scores = jnp.where(mask, scores, -jnp.inf)
        attn = jax.nn.softmax(scores, axis=-1)
        attn = jnp.nan_to_num(attn, nan=0.0)
        out = jnp.einsum('bhts,bhsd->bhtd', attn, v)
        out = out.transpose(0, 2, 1, 3).reshape(B, T_text, N_HEADS * HEAD_DIM)
        return out @ Wo

    def _L2_ffn_ref(hidden_states, gate_w, experts_w1, experts_w2, shared_gate_up, shared_down):
        import jax, jax.numpy as jnp
        import numpy as np
        B, S, H = (2, 64, 256)
        E, I, K = (64, 176, 6)
        NS = 2
        SH_I = I * NS
        orig_shape = hidden_states.shape
        x = hidden_states.reshape(-1, orig_shape[-1])
        router_logits = x @ gate_w.T
        probs = jax.nn.softmax(router_logits, axis=-1)
        topk_w, topk_idx = jax.lax.top_k(probs, K)
        topk_w = topk_w / jnp.sum(topk_w, axis=-1, keepdims=True)
        combine = jnp.sum(jax.nn.one_hot(topk_idx, E, dtype=x.dtype) * topk_w[..., None], axis=1)
        h = jax.nn.silu(jnp.einsum('th,eih->tei', x, experts_w1))
        y = jnp.einsum('tei,ehi->teh', h, experts_w2)
        routed_out = jnp.einsum('teh,te->th', y, combine)
        gu = x @ shared_gate_up.T
        g, u = jnp.split(gu, 2, axis=-1)
        shared_out = jax.nn.silu(g) * u @ shared_down.T
        return (routed_out + shared_out).reshape(orig_shape)

    def _L3_xattn_ref(text_hidden, vision_tokens, vision_mask, Wq, Wk, Wv, Wo):
        import jax, jax.numpy as jnp
        import numpy as np
        N_HEADS = 16
        N_KV_HEADS = 8
        HEAD_DIM = 128
        D_TEXT = 256
        D_VISION = 128
        GROUPS = N_HEADS // N_KV_HEADS
        B, T_text, _ = text_hidden.shape
        T_vis = vision_tokens.shape[1]
        scale = jnp.float32(np.sqrt(HEAD_DIM))
        q = (text_hidden @ Wq).reshape(B, T_text, N_HEADS, HEAD_DIM).transpose(0, 2, 1, 3)
        k = (vision_tokens @ Wk).reshape(B, T_vis, N_KV_HEADS, HEAD_DIM).transpose(0, 2, 1, 3)
        v = (vision_tokens @ Wv).reshape(B, T_vis, N_KV_HEADS, HEAD_DIM).transpose(0, 2, 1, 3)
        k = jnp.repeat(k, GROUPS, axis=1)
        v = jnp.repeat(v, GROUPS, axis=1)
        scores = jnp.einsum('bhtd,bhsd->bhts', q, k) / scale
        mask = vision_mask[:, None, None, :]
        scores = jnp.where(mask, scores, -jnp.inf)
        attn = jax.nn.softmax(scores, axis=-1)
        attn = jnp.nan_to_num(attn, nan=0.0)
        out = jnp.einsum('bhts,bhsd->bhtd', attn, v)
        out = out.transpose(0, 2, 1, 3).reshape(B, T_text, N_HEADS * HEAD_DIM)
        return out @ Wo

    def _L3_ffn_ref(hidden_states, gate_w, w_gate, w_up, w_down):
        import jax, jax.numpy as jnp
        import numpy as np
        HIDDEN = 256
        INTER = 96
        N_EXPERTS = 32
        TOP_K = 8
        B, S, H = hidden_states.shape
        E = gate_w.shape[1]
        x = hidden_states.reshape(-1, H)
        T = x.shape[0]
        K = TOP_K
        P = T * K
        C = 2 * (P // E)
        probs = jax.nn.softmax(x @ gate_w, axis=-1)
        w, sel = jax.lax.top_k(probs, K)
        w = w / jnp.sum(w, axis=-1, keepdims=True)
        flat_e = sel.reshape(-1)
        flat_t = jnp.repeat(jnp.arange(T), K)
        flat_w = w.reshape(-1)
        order = jnp.argsort(flat_e)
        se = flat_e[order]
        start = jnp.searchsorted(se, jnp.arange(E))
        pos = jnp.arange(P) - start[se]
        slot = jnp.where(pos < C, se * C + pos, E * C)
        slot_pair = jnp.full((E * C,), P, dtype=jnp.int32).at[slot].set(order.astype(jnp.int32), mode='drop')
        t_slot = jnp.concatenate([flat_t, jnp.array([T])])[slot_pair]
        w_slot = jnp.concatenate([flat_w, jnp.zeros((1,), flat_w.dtype)])[slot_pair]
        x_pad = jnp.concatenate([x, jnp.zeros((1, H), x.dtype)], axis=0)
        xg = x_pad[t_slot].reshape(E, C, H)
        g = jnp.einsum('ech,ehi->eci', xg, w_gate)
        u = jnp.einsum('ech,ehi->eci', xg, w_up)
        y = jnp.einsum('eci,eih->ech', jax.nn.silu(g) * u, w_down).reshape(E * C, H)
        out = jnp.zeros((T + 1, H), x.dtype).at[t_slot].add(w_slot[:, None] * y)
        return out[:T].reshape(B, S, H)
    x = x + _L0_xattn_ref(_layernorm(x, axis=-1), ctx_1024, L0_xattn_Wq, L0_xattn_bq, L0_xattn_Wk, L0_xattn_bk, L0_xattn_Wv, L0_xattn_bv, L0_xattn_Wkv_dca, L0_xattn_bkv_dca, L0_xattn_qn_w, L0_xattn_qn_b, L0_xattn_kn_w, L0_xattn_kn_b, L0_xattn_kn_dca_w, L0_xattn_kn_dca_b, L0_xattn_Wo, L0_xattn_bo)
    x = x + _L0_ffn_ref(_layernorm(x, axis=-1), L0_ffn_w_gate, L0_ffn_w_up, L0_ffn_w_down)
    x = x + _L1_xattn_ref(_layernorm(x, axis=-1), ctx_1024, L1_xattn_Wq, L1_xattn_Wk, L1_xattn_Wv, L1_xattn_Wo, L1_xattn_gq, L1_xattn_gk)
    x = x + _L1_ffn_ref(_layernorm(x, axis=-1), L1_ffn_in_gamma, L1_ffn_in_beta, L1_ffn_agg_w, L1_ffn_agg_b, L1_ffn_pn_gamma, L1_ffn_pn_beta, L1_ffn_d1_w, L1_ffn_d1_b, L1_ffn_d2_w, L1_ffn_d2_b, L1_ffn_bc_w, L1_ffn_bc_b, L1_ffn_gate_w, L1_ffn_gate_b, L1_ffn_out_gamma, L1_ffn_out_beta)
    x = x + _L2_xattn_ref(_layernorm(x, axis=-1), ctx_1024, mask_BxS2_bf1, L2_xattn_Wq, L2_xattn_Wk, L2_xattn_Wv, L2_xattn_Wo)
    x = x + _L2_ffn_ref(_layernorm(x, axis=-1), L2_ffn_gate_w, L2_ffn_experts_w1, L2_ffn_experts_w2, L2_ffn_shared_gate_up, L2_ffn_shared_down)
    x = x + _L3_xattn_ref(_layernorm(x, axis=-1), ctx_1024, mask_BxS2_bf1, L3_xattn_Wq, L3_xattn_Wk, L3_xattn_Wv, L3_xattn_Wo)
    x = x + _L3_ffn_ref(_layernorm(x, axis=-1), L3_ffn_gate_w, L3_ffn_w_gate, L3_ffn_w_up, L3_ffn_w_down)
    return x

_drawn_inputs = setup_inputs


def setup_inputs(seed=0):
    import zlib

    import numpy as np

    out = dict(_drawn_inputs(seed))
    spreads = {'L0_xattn_bq': (0.0, 0.442),
     'L0_xattn_bk': (0.0, 0.1),
     'L0_xattn_bv': (0.0, 0.1),
     'L0_xattn_bkv_dca': (0.0, 0.1),
     'L0_xattn_qn_w': (1.0, 0.6),
     'L0_xattn_qn_b': (0.0, 0.773),
     'L0_xattn_kn_w': (1.0, 0.6),
     'L0_xattn_kn_b': (0.0, 0.8),
     'L0_xattn_kn_dca_w': (1.0, 0.6),
     'L0_xattn_kn_dca_b': (0.0, 0.8),
     'L0_xattn_bo': (0.0, 0.1),
     'L1_xattn_gq': (1.0, 0.2),
     'L1_xattn_gk': (1.0, 0.2),
     'L1_ffn_in_gamma': (1.0, 0.6),
     'L1_ffn_in_beta': (0.0, 0.8),
     'L1_ffn_agg_b': (0.0, 0.499),
     'L1_ffn_pn_gamma': (1.0, 0.6),
     'L1_ffn_pn_beta': (0.0, 0.8),
     'L1_ffn_d1_b': (0.0, 0.586),
     'L1_ffn_d2_b': (0.0, 0.1),
     'L1_ffn_bc_b': (0.0, 0.326),
     'L1_ffn_gate_b': (0.0, 0.8),
     'L1_ffn_out_gamma': (1.0, 0.2),
     'L1_ffn_out_beta': (0.0, 0.1)}
    factors = {'L1_ffn_gate_w': 5.838,
     'L2_xattn_Wq': 8.0,
     'L2_xattn_Wk': 8.0,
     'L2_ffn_gate_w': 6.328,
     'L2_ffn_experts_w1': 5.719,
     'L2_ffn_experts_w2': 5.597,
     'L2_ffn_shared_gate_up': 5.846,
     'L2_ffn_shared_down': 5.835,
     'L3_xattn_Wq': 8.0,
     'L3_xattn_Wk': 8.0}
    for name, (base, spread) in spreads.items():
        noise = np.random.default_rng([zlib.crc32(name.encode()), seed]).standard_normal(out[name].shape)
        drawn = base * np.exp(spread * noise) if base else spread * noise
        out[name] = jnp.asarray(drawn.astype(out[name].dtype))
    for name, factor in factors.items():
        out[name] = (out[name] * factor).astype(out[name].dtype)
    return out
```

```python
from contextlib import ExitStack

import concourse.bass as bass
from concourse import mybir
from concourse.alu_op_type import AluOpType as ALU

ACT = mybir.ActivationFunctionType
AX_X = mybir.AxisListType.X
F32 = mybir.dt.float32
BF16 = mybir.dt.bfloat16
U8 = mybir.dt.uint8

P = 128
BATCH = 4
TOKENS = 1024
TT = TOKENS // P
D = 256
DC = D // P
KEYS = 512
KT = KEYS // P
CW = 128
HEADS = 16
BANK = 512
LOWEST = -3.0e38
MASKED = 1.0e30
PAIRS = HEADS * BATCH
AHEAD = 3
RMS_EPS = 1e-5


def wait_for(engine, semaphore, count):
    if not isinstance(count, int) or count > 0:
        engine.wait_ge(semaphore, count)


class Stage:

    def __init__(self, nc, m, name):
        self.nc, self.m, self.name, self.stack, self.free_banks = nc, m, name, ExitStack(), list(m.banks)
        self.semaphores = []

    def __enter__(self):
        return self

    def __exit__(self, *error):
        self.stack.close()
        self.m.used_semaphores = self.semaphores

    def sbuf(self, name, shape, dtype=F32):
        return self.stack.enter_context(self.nc.sbuf_tensor(f"{self.name}_{name}", shape, dtype))

    def banks(self, name, count):
        given, self.free_banks = self.free_banks[:count], self.free_banks[count:]
        assert len(given) == count, name
        return given

    def sem(self, name):
        self.semaphores.append(self.nc.alloc_semaphore(name=f"{self.name}_{name}"))
        return self.semaphores[-1]

    def sems(self, *names):
        return [self.sem(n) for n in names]

    def block(self):
        if self.m.used_semaphores:
            self.nc.clear_and_free_semaphores(self.m.used_semaphores)
        return self.nc.Block()


def load_stage(nc, m, dram):
    with Stage(nc, m, "load") as st:
        loaded, set_up = st.sems("loaded", "set_up")
        with st.block() as block:

            @block.sync
            def _(sp):
                sp.dma_start(m.x[:], dram["x"].rearrange("(t p) d -> p t d", p=P)).then_inc(loaded, 16)
                sp.dma_start(m.ctx_t[:], dram["ctx_t"]).then_inc(loaded, 16)
                sp.dma_start(m.ctx[:], dram["ctx"].rearrange("(t p) c -> p t c", p=P)).then_inc(loaded, 16)
                sp.dma_start(m.ident[:], dram["ident"]).then_inc(loaded, 16)
                sp.wait_ge(loaded, 64)

            @block.gpsimd
            def _(pool):
                pool.memset(m.minus_half[:], -0.5).then_inc(set_up, 1)
                pool.memset(m.ones[:], 1.0).then_inc(set_up, 1)
                pool.wait_ge(set_up, 2)


def store_stage(nc, m, dram):
    with Stage(nc, m, "store") as st:
        stored = st.sem("stored")
        with st.block() as block:

            @block.sync
            def _(sp):
                sp.dma_start(dram["out"].rearrange("(t p) d -> p t d", p=P), m.x[:]).then_inc(stored, 16)
                sp.wait_ge(stored, 16)


def norm_stage(nc, m, name, keep=False):
    eps = 1e-5
    with Stage(nc, m, name) as st:
        stats = st.sbuf("stats", [P, TT, 6])
        moments = st.sbuf("moments", [P, TT, 2])
        spread = st.sbuf("spread", [P, TT])
        rstd = st.sbuf("rstd", [P, TT])
        xn = st.sbuf("xn", [P, 2, D])
        turned = st.banks("turned", 2)
        stats_done, moments_done, spread_done, rstd_done, xn_done, turned_ready, kept, copied = st.sems(
            "stats_done", "moments_done", "spread_done", "rstd_done", "xn_done", "turned_ready", "kept", "copied")
        with st.block() as block:

            @block.vector
            def _(dve):
                with dve.Fori(0, TT) as t:
                    dve.bn_stats(stats[:, t, :], m.x[:, t, :]).then_inc(stats_done, 1)
                dve.wait_ge(stats_done, TT)
                for t in range(TT):
                    last = dve.bn_aggr(moments[:, t, :], stats[:, t, :])
                last.then_inc(moments_done, 1)
                dve.wait_ge(moments_done, 1)
                dve.tensor_scalar(spread[:], moments[:, :, 1], eps, None, ALU.add).then_inc(spread_done, 1)
                dve.wait_ge(rstd_done, 1)

                def normalise(t, slot):
                    dve.tensor_scalar(xn[:, slot, :], m.x[:, t, :], moments[:, t, 0:1], rstd[:, bass.ds(t, 1)],
                                      ALU.subtract, ALU.mult).then_inc(xn_done, 1)

                for slot in range(2):
                    normalise(slot, slot)
                with dve.Fori(1, TT // 2) as i:
                    for slot in range(2):
                        dve.wait_ge(turned_ready, 2 * i + (slot - 1))
                        if keep:
                            dve.wait_ge(copied, 2 * i + (slot - 1))
                        normalise(2 * i + slot, slot)

            @block.gpsimd
            def _(pool):
                pool.wait_ge(spread_done, 1)
                pool.tensor_tensor(rstd[:], spread[:], m.minus_half[:, 0:TT], ALU.pow).then_inc(rstd_done, 1)
                if keep:
                    for t in range(TT):
                        pool.wait_ge(xn_done, t + 1)
                        pool.tensor_copy(m.x_n[:, t, :], xn[:, t % 2, :]).then_inc(copied, 1)

            @block.tensor
            def _(pe):
                def turn(t, slot):
                    pe.wait_ge(xn_done, t + 1)
                    for c in range(DC):
                        last = pe.transpose(turned[slot][:, c * P:(c + 1) * P], xn[:, slot, c * P:(c + 1) * P],
                                            m.ident[:])
                    last.then_inc(turned_ready, 1)

                for slot in range(2):
                    turn(slot, slot)
                with pe.Fori(1, TT // 2) as i:
                    for slot in range(2):
                        pe.wait_ge(kept, 2 * i + (slot - 1))
                        turn(2 * i + slot, slot)

            @block.scalar
            def _(act):
                with act.Fori(0, TT // 2) as i:
                    for slot in range(2):
                        act.wait_ge(turned_ready, 2 * i + (slot + 1))
                        act.copy(m.x_t[:, :, bass.ds((2 * i + slot) * P, P)],
                                 turned[slot][:, 0:D].rearrange("p (c q) -> p c q", c=DC)).then_inc(kept, 1)


def heads_stage(nc, m, dram, name, qk_norm):
    scale = float(P) ** -0.5
    n_k = BATCH * KEYS // BANK
    rows = BATCH * KT
    if qk_norm:
        quarters = [["k0", "k1", "k2", "k3"], ["kk", "q0"], ["row", "q1"], ["qq", "wvo"]]
    else:
        quarters = [["a"], ["q0"], ["q1"], ["wvo"]]
    pieces = [piece for quarter in quarters for piece in quarter]
    n_pieces = len(pieces)
    last_q, k_pieces = pieces.index("q1"), n_k
    with Stage(nc, m, name) as st:
        wq = st.sbuf("wq", [P, 2, D])
        wk = st.sbuf("wk", [P, 2, CW])
        wv_t = st.sbuf("wv_t", [P, 2, CW])
        wo = st.sbuf("wo", [P, 2, D])
        a_h = st.sbuf("a_h", [P, 2, D])
        wvo = st.sbuf("wvo", [P, 2, D])
        q_t = st.sbuf("q_t", [P, 2, TOKENS])
        side = st.sbuf("side", [P, 2, BATCH * KEYS])
        valid = st.sbuf("valid", [P, BATCH])
        masked = st.sbuf("masked", [P, 4, KEYS])
        top = st.sbuf("top", [P, 4])
        shift = st.sbuf("shift", [P, 4])
        prob = st.sbuf("prob", [P, 4, KEYS])
        total = st.sbuf("total", [P, 8])
        inverse = st.sbuf("inverse", [P, 4])
        woken = st.sbuf("woken", [P, 1])
        prob_t = st.sbuf("prob_t", [P, 2, KT, 2 * P])
        o_t = st.sbuf("o_t", [P, 2, 2 * P])
        if qk_norm:
            k_t = st.sbuf("k_t", [P, 2, BATCH * KEYS])
            q_squares = st.sbuf("q_squares", [P, TOKENS])
            k_squares = st.sbuf("k_squares", [P, BATCH * KEYS])
            gain = st.sbuf("gain", [P, 2])
            gains = st.sbuf("gains", [P, 1])
            q_means = st.sbuf("q_means", [P, TT])
            k_means = st.sbuf("k_means", [P, rows])
            k_rms = st.sbuf("k_rms", [P, rows])
            q_scale = st.sbuf("q_scale", [P, 2, TT])
            rms_row = st.sbuf("rms_row", [rows, P])
        else:
            mask_u8 = st.sbuf("mask_u8", [P, BATCH * KEYS], U8)
        score_bank = st.banks("score", 2)
        turn_bank = st.banks("turn", 2)
        o_bank, = st.banks("o", 1)
        y_bank, = st.banks("y", 1)
        prep_bank = st.banks("prep", 2)
        w_loaded = st.sems("w_loaded0", "w_loaded1")
        rms_loaded = st.sems("rms_loaded0", "rms_loaded1")
        (side_loaded, scores_ready, top_done, shift_done, exp_done, inverse_done, turn_ready,
         turn_kept, pv_ready, o_kept, y_ready, x_added, prep_ready, prep_kept) = st.sems(
            "side_loaded", "scores_ready", "top_done", "shift_done", "exp_done", "inverse_done",
            "turn_ready", "turn_kept", "pv_ready", "o_kept", "y_ready", "x_added", "prep_ready",
            "prep_kept")
        (set_up, k_rms_done, q_scale_done, row_stored, gain_loaded) = st.sems(
            "set_up", "k_rms_done", "q_scale_done", "row_stored", "gain_loaded")

        def walk(engine, prepare, step):
            def two_heads(i, last=False):
                for k in range(2 * BATCH):
                    after, ahead = quarters[k % BATCH], k // BATCH + 1
                    if last and ahead == 2:
                        after = []
                    head = (i * 2 + k // BATCH, i, k // BATCH)
                    following = (i * 2 + ahead, i + ahead // 2, ahead % 2)
                    step(i * (2 * BATCH) + k, k, head, after, following)

            for piece in pieces:
                prepare(piece, (0, 0, 0))
            two_heads(0)
            with engine.Fori(1, HEADS // 2 - 1) as i:
                two_heads(i)
            two_heads(HEADS // 2 - 1, True)
            for k in range(AHEAD):
                step(PAIRS + k, k, None, [], None)

        def exists(pair, back):
            return not isinstance(pair, int) or 0 <= pair - back < PAIRS

        with st.block() as block:

            @block.sync
            def _(sp):
                if qk_norm:
                    sp.dma_start(gain[:, 0:1], dram["gq"]).then_inc(gain_loaded, 16)
                    sp.dma_start(gain[:, 1:2], dram["gk"]).then_inc(gain_loaded, 16)
                else:
                    sp.dma_start(mask_u8[:], dram["mask"].partition_broadcast(P)).then_inc(side_loaded, 16)

                def load(h, g, slot):
                    sp.dma_start(wq[:, slot, :], dram["wq"][h]).then_inc(w_loaded[slot], 16)
                    sp.dma_start(wk[:, slot, :], dram["wk"][g]).then_inc(w_loaded[slot], 16)
                    sp.dma_start(wv_t[:, slot, :], dram["wv_t"][g]).then_inc(w_loaded[slot], 16)
                    sp.dma_start(wo[:, slot, :], dram["wo"][h]).then_inc(w_loaded[slot], 16)

                def spread_rms(h, slot):
                    rows_kept, free, stored = (known(count) for count in (
                        h * n_pieces + (pieces.index("row") + 1), h * (2 * BATCH) - 2 * BATCH, h * 16 + 16))
                    sp.wait_ge(prep_kept, rows_kept)
                    wait_for(sp, top_done, free)
                    sp.dma_start(dram["rms"][slot], rms_row[:]).then_inc(row_stored, 16)
                    sp.wait_ge(row_stored, stored)
                    sp.dma_start(side[:, slot, :],
                                 dram["rms"][slot].rearrange("t p -> (t p)").partition_broadcast(P)
                                 ).then_inc(rms_loaded[slot], 16)

                def known(count):
                    return count if isinstance(count, int) else sp.snap(count)

                for h in range(2):
                    load(h, h if qk_norm else 0, h)
                if qk_norm:
                    spread_rms(0, 0)
                with sp.Fori(1, HEADS // 2) as i:
                    for slot in range(2):
                        sp.wait_ge(prep_kept, i * (2 * n_pieces) + (slot - 1) * n_pieces)
                        load(i * 2 + slot, i * 2 + slot if qk_norm else i, slot)
                        if qk_norm:
                            spread_rms(i * 2 + (slot - 1), 1 - slot)
                if qk_norm:
                    spread_rms(HEADS - 1, 1)

            @block.tensor
            def _(pe):
                def prepare(piece, head):
                    h, turn, slot = head
                    n = pieces.index(piece)
                    if n == 0:
                        pe.wait_ge(w_loaded[slot], turn * 64 + 64)
                    bank = prep_bank[n % 2]
                    wait_for(pe, prep_kept, h * n_pieces + (n - 1))
                    if piece == "a":
                        for c in range(DC):
                            last = pe.matmul(bank[:, c * P:(c + 1) * P], wq[:, slot, c * P:(c + 1) * P],
                                             wk[:, slot, :], start=True, stop=True)
                    elif piece in ("q0", "q1"):
                        chunk = int(piece[1])
                        if not qk_norm:
                            pe.wait_ge(prep_kept, h * n_pieces + 1)
                        left = wq if qk_norm else a_h
                        for c in range(DC):
                            last = pe.matmul(bank[:], left[:, slot, c * P:(c + 1) * P],
                                             m.x_t[:, c, chunk * BANK:(chunk + 1) * BANK],
                                             start=(c == 0), stop=(c == DC - 1))
                    elif piece == "wvo":
                        last = pe.matmul(bank[:, 0:D], wv_t[:, slot, :], wo[:, slot, :], start=True, stop=True)
                    elif piece in ("kk", "qq"):
                        of, tiles = (k_squares, rows) if piece == "kk" else (q_squares, TT)
                        pe.wait_ge(prep_kept, h * n_pieces + (k_pieces if piece == "kk" else last_q + 1))
                        for t in range(tiles):
                            last = pe.matmul(bank[:, t:t + 1], of[:, t * P:(t + 1) * P], m.ones[:, 0:1],
                                             start=True, stop=True)
                    elif piece == "row":
                        pe.wait_ge(k_rms_done, h + 1)
                        last = pe.transpose(bank[0:rows, 0:P], k_rms[:], m.ident[:])
                    else:
                        chunk = int(piece[1])
                        last = pe.matmul(bank[:], wk[:, slot, :], m.ctx_t[:, chunk * BANK:(chunk + 1) * BANK],
                                         start=True, stop=True)
                    last.then_inc(prep_ready, 1)

                def step(pair, k, head, after, following):
                    b = k % BATCH
                    if exists(pair, 0):
                        h, _, slot = head
                        if b == 0:
                            pe.wait_ge(prep_kept, h * n_pieces + n_pieces)
                        keys = k_t[:, slot, :] if qk_norm else m.ctx_t[:, :]
                        for q in range(2):
                            wait_for(pe, top_done, pair * 2 + (q - 1))
                            t = 2 * b + q
                            pe.matmul(score_bank[q][:], q_t[:, slot, t * P:(t + 1) * P],
                                      keys[:, b * KEYS:(b + 1) * KEYS], start=True, stop=True).then_inc(scores_ready, 1)
                    for piece in after:
                        prepare(piece, following)
                    if exists(pair, 1):
                        for q in range(2):
                            pe.wait_ge(exp_done, pair * 2 + (q - 1))
                            wait_for(pe, turn_kept, pair * 2 + (q - 3))
                            for n in range(KT):
                                last = pe.transpose(turn_bank[q][:, n * P:(n + 1) * P],
                                                    prob[:, (2 * k - 2 + q) % 4, n * P:(n + 1) * P], m.ident[:])
                            last.then_inc(turn_ready, 1)
                    if exists(pair, 2):
                        pe.wait_ge(turn_kept, pair * 2 - 2)
                        wait_for(pe, o_kept, pair - 2)
                        for n in range(KT):
                            last = pe.matmul(o_bank[:, 0:2 * P], m.ctx[:, (k - 2) % BATCH * KT + n, :],
                                             prob_t[:, k % 2, n, :], start=(n == 0), stop=(n == KT - 1))
                        last.then_inc(pv_ready, 1)
                    if exists(pair, 3):
                        pe.wait_ge(o_kept, pair - 2)
                        wait_for(pe, x_added, pair * 2 - 6)
                        for q in range(2):
                            last = pe.matmul(y_bank[:, q * D:(q + 1) * D], o_t[:, (k - 3) % 2, q * P:(q + 1) * P],
                                             wvo[:, (k - 3) // BATCH % 2, :], start=True, stop=True)
                        last.then_inc(y_ready, 1)

                walk(pe, prepare, step)

            @block.scalar
            def _(act):
                def prepare(piece, head):
                    h, turn, slot = head
                    n = pieces.index(piece)
                    bank = prep_bank[n % 2]
                    act.wait_ge(prep_ready, h * n_pieces + (n + 1))
                    if piece == "a":
                        last = act.copy(a_h[:, slot, :], bank[:, 0:D])
                    elif piece in ("q0", "q1"):
                        chunk = int(piece[1])
                        columns = slice(chunk * BANK, (chunk + 1) * BANK)
                        if qk_norm:
                            act.activation(q_squares[:, columns], bank[:], ACT.Square)
                        last = act.copy(q_t[:, slot, columns], bank[:])
                    elif piece == "wvo":
                        last = act.copy(wvo[:, slot, :], bank[:, 0:D])
                    elif piece == "kk":
                        wait_for(act, k_rms_done, h)
                        last = act.activation(k_means[:], bank[:, 0:rows], ACT.Copy, bias=RMS_EPS, scale=1.0 / P)
                    elif piece == "qq":
                        wait_for(act, q_scale_done, h)
                        last = act.activation(q_means[:], bank[:, 0:TT], ACT.Copy, bias=RMS_EPS * P)
                    elif piece == "row":
                        wait_for(act, row_stored, h * 16)
                        last = act.copy(rms_row[:], bank[0:rows, 0:P])
                    else:
                        chunk = int(piece[1])
                        columns = slice(chunk * BANK, (chunk + 1) * BANK)
                        act.activation(k_squares[:, columns], bank[:], ACT.Square)
                        last = act.activation(k_t[:, slot, columns], bank[:], ACT.Copy, scale=gains[:, 0:1])
                    last.then_inc(prep_kept, 1)

                def step(pair, k, head, after, following):
                    if exists(pair, 0):
                        h, _, slot = head
                        for q in range(2):
                            unit, t = (2 * k + q) % 4, 2 * (k % BATCH) + q
                            act.wait_ge(shift_done, pair * 2 + (q + 1))
                            wait_for(act, turn_ready, pair * 2 + (q - 3))
                            wait_for(act, inverse_done, pair - 3)
                            act.activation(prob[:, unit, :], masked[:, unit, :], ACT.Exp, bias=shift[:, unit:unit + 1],
                                           scale=q_scale[:, slot, t:t + 1] if qk_norm else scale,
                                           accum_out=total[:, 2 * (k % 4) + q:2 * (k % 4) + q + 1]).then_inc(exp_done, 1)
                    for piece in after:
                        prepare(piece, following)
                    if exists(pair, 2):
                        act.wait_ge(pv_ready, pair - 1)
                        wait_for(act, y_ready, pair - 3)
                        if qk_norm:
                            last = act.copy(o_t[:, k % 2, :], o_bank[:, 0:2 * P])
                        else:
                            b = (k - 2) % BATCH
                            last = act.activation(o_t[:, k % 2, :], o_bank[:, 0:2 * P], ACT.Copy, scale=valid[:, b:b + 1])
                        last.then_inc(o_kept, 1)

                act.wait_ge(set_up, 1)
                walk(act, prepare, step)

            @block.vector
            def _(dve):
                def prepare(piece, head):
                    pass

                def step(pair, k, head, after, following):
                    b = k % BATCH
                    if exists(pair, 0):
                        h, turn, slot = head
                        if qk_norm and b == 0:
                            dve.wait_ge(rms_loaded[slot], turn * 16 + 16)
                            dve.wait_ge(q_scale_done, h + 1)
                        for q in range(2):
                            unit, t = (2 * k + q) % 4, 2 * b + q
                            dve.wait_ge(scores_ready, pair * 2 + (q + 1))
                            wait_for(dve, exp_done, pair * 2 + (q - 3))
                            dve.memset(woken[:], 0.0)
                            dve.tensor_tensor_reduce(masked[:, unit, :], score_bank[q][:],
                                                     side[:, slot if qk_norm else 0, b * KEYS:(b + 1) * KEYS], 1.0, LOWEST,
                                                     ALU.mult if qk_norm else ALU.add, ALU.max,
                                                     top[:, unit:unit + 1]).then_inc(top_done, 1)
                            dve.wait_ge(top_done, pair * 2 + (q + 1))
                            if qk_norm:
                                dve.scalar_tensor_tensor(shift[:, unit:unit + 1], top[:, unit:unit + 1], -1.0,
                                                         q_scale[:, slot, t:t + 1], ALU.mult,
                                                         ALU.mult).then_inc(shift_done, 1)
                            else:
                                dve.tensor_scalar(shift[:, unit:unit + 1], top[:, unit:unit + 1], -scale, None,
                                                  ALU.mult).then_inc(shift_done, 1)
                    if exists(pair, 1):
                        for q in range(2):
                            dve.wait_ge(turn_ready, pair * 2 + (q - 1))
                            wait_for(dve, pv_ready, pair - 2)
                            dve.tensor_copy(prob_t[:, (k - 1) % 2, :, q * P:(q + 1) * P],
                                            turn_bank[q][:].rearrange("p (n t) -> p n t", n=KT)).then_inc(turn_kept, 1)
                    if exists(pair, 3):
                        old, at = (k - 3) % BATCH, k % 2 * 2
                        wait_for(dve, x_added, pair * 2 - 8)
                        dve.wait_ge(exp_done, pair * 2 - 4)
                        dve.reciprocal(inverse[:, at:at + 2], total[:, (k - 3) % 4 * 2:(k - 3) % 4 * 2 + 2]
                                       ).then_inc(inverse_done, 1)
                        dve.wait_ge(y_ready, pair - 2)
                        dve.wait_ge(inverse_done, pair - 2)
                        for q in range(2):
                            tile = m.x[:, 2 * old + q, :]
                            dve.scalar_tensor_tensor(tile, y_bank[:, q * D:(q + 1) * D], inverse[:, at + q:at + q + 1], tile,
                                                     ALU.mult, ALU.add).then_inc(x_added, 1)

                if qk_norm:
                    dve.wait_ge(gain_loaded, 32)
                    dve.tensor_tensor(gains[:], gain[:, 0:1], gain[:, 1:2], ALU.mult).then_inc(set_up, 1)
                else:
                    dve.wait_ge(side_loaded, 16)
                    dve.tensor_scalar(side[:, 0, :], mask_u8[:], 1.0, MASKED, ALU.subtract, ALU.mult)
                    dve.tensor_reduce(valid[:], mask_u8[:].rearrange("p (b s) -> p b s", b=BATCH), AX_X,
                                      ALU.max).then_inc(set_up, 1)
                walk(dve, prepare, step)

            @block.gpsimd
            def _(pool):
                if not qk_norm:
                    return

                def prepare(piece, head):
                    h, _, slot = head
                    if piece == "kk":
                        pool.wait_ge(prep_kept, h * n_pieces + (pieces.index("kk") + 1))
                        wait_for(pool, prep_ready, h * n_pieces + (pieces.index("row") + 1 - n_pieces))
                        pool.tensor_tensor(k_rms[:], k_means[:], m.minus_half[:, 0:rows], ALU.pow).then_inc(k_rms_done, 1)
                    elif piece == "qq":
                        pool.wait_ge(prep_kept, h * n_pieces + (pieces.index("qq") + 1))
                        wait_for(pool, exp_done, h * (2 * BATCH) - 2 * BATCH)
                        pool.tensor_tensor(q_scale[:, slot, :], q_means[:], m.minus_half[:, 0:TT],
                                           ALU.pow).then_inc(q_scale_done, 1)

                def step(pair, k, head, after, following):
                    for piece in after:
                        prepare(piece, following)

                walk(pool, prepare, step)


H0 = 16
GROUP = 4
GROUPS = HEADS // GROUP
LAST_KEYS = 16


def small_project_stage(nc, m, dram):
    tiles = TT + BATCH * KT
    eps = 1e-6
    with Stage(nc, m, "l0p") as st:
        wq = st.sbuf("wq", [P, DC, D])
        wkv = st.sbuf("wkv", [CW, 2 * D])
        wkv_last = st.sbuf("wkv_last", [CW, 2 * D])
        bq = st.sbuf("bq", [P, D])
        bkv = st.sbuf("bkv", [P, 2, 2 * D])
        gain = st.sbuf("gain", [P, 3, H0])
        offset = st.sbuf("offset", [P, 3, H0])
        ctx_common = st.sbuf("ctx_common", [CW, BATCH, P])
        ctx_last = st.sbuf("ctx_last", [CW, BATCH, P])
        raw = st.sbuf("raw", [P, 2, 2 * D])
        centred = st.sbuf("centred", [P, 2, D])
        squares = st.sbuf("squares", [P, 2, D])
        sums = st.sbuf("sums", [P, 2, HEADS])
        means = st.sbuf("means", [P, 2, HEADS])
        variance = st.sbuf("variance", [P, 2, HEADS])
        rstd = st.sbuf("rstd", [P, 2, HEADS])
        padded = st.sbuf("padded", [P, 2, HEADS, 2 * H0])
        project_bank = st.banks("project", 2)
        turn_bank = st.banks("turn", 2)
        (loaded, cleared, shares_set, projected, raw_done, sums_done, means_done, centred_done, squares_done,
         variance_done, spread_done, rstd_done, scaled, gained, padded_done, turned, kept, v_done) = st.sems(
            "loaded", "cleared", "shares_set", "projected", "raw_done", "sums_done", "means_done", "centred_done",
            "squares_done", "variance_done", "spread_done", "rstd_done", "scaled", "gained", "padded_done", "turned",
            "kept", "v_done")
        n_loads = 15

        with st.block() as block:

            @block.sync
            def _(sp):
                common = P - LAST_KEYS
                sp.dma_start(wq[:], dram["wq"].rearrange("(c p) n -> p c n", p=P)).then_inc(loaded, 16)
                sp.dma_start(wkv[:], dram["wkv"]).then_inc(loaded, 16)
                sp.dma_start(wkv_last[:], dram["wkv_last"]).then_inc(loaded, 16)
                sp.dma_start(bq[:], dram["bq"].partition_broadcast(P)).then_inc(loaded, 16)
                sp.dma_start(bkv[:, 0, :], dram["bkv"].partition_broadcast(P)).then_inc(loaded, 16)
                sp.dma_start(bkv[0:common, 1, :], dram["bkv"].partition_broadcast(common)).then_inc(loaded, 16)
                sp.dma_start(bkv[common:P, 1, :], dram["bkv_last"].partition_broadcast(LAST_KEYS)).then_inc(loaded, 16)
                for n, (w, b) in enumerate((("qn_w", "qn_b"), ("kn_w", "kn_b"))):
                    sp.dma_start(gain[:, n, :], dram[w].partition_broadcast(P)).then_inc(loaded, 16)
                    sp.dma_start(offset[:, n, :], dram[b].partition_broadcast(P)).then_inc(loaded, 16)
                for to, w in ((gain, "kn_{}w"), (offset, "kn_{}b")):
                    sp.dma_start(to[0:common, 2, :], dram[w.format("")].partition_broadcast(common)).then_inc(loaded, 16)
                    sp.dma_start(to[common:P, 2, :],
                                 dram[w.format("dca_")].partition_broadcast(LAST_KEYS)).then_inc(loaded, 16)

            @block.gpsimd
            def _(pool):
                pool.memset(ctx_common[:], 0.0).then_inc(cleared, 1)
                pool.memset(ctx_last[:], 0.0).then_inc(cleared, 1)
                pool.memset(padded[:], 0.0).then_inc(cleared, 1)
                pool.wait_ge(cleared, 3)
                last_tiles = m.ctx_t[:].rearrange("c (b n q) -> c b n q", b=BATCH, n=KT)[:, :, KT - 1, :]
                cut = P - LAST_KEYS
                pool.tensor_copy(ctx_common[:, :, 0:cut], last_tiles[:, :, 0:cut]).then_inc(shares_set, 1)
                pool.tensor_copy(ctx_last[:, :, cut:P], last_tiles[:, :, cut:P]).then_inc(shares_set, 1)
                for i in range(tiles):
                    slot = i % 2
                    pool.wait_ge(spread_done, i + 1)
                    wait_for(pool, scaled, i - 1)
                    pool.tensor_tensor(rstd[:, slot, :], variance[:, slot, :], m.minus_half[:, 0:HEADS],
                                       ALU.pow).then_inc(rstd_done, 1)

            @block.tensor
            def _(pe):
                pe.wait_ge(loaded, 16 * n_loads)
                pe.wait_ge(shares_set, 2)

                def project(i):
                    bank = project_bank[i % 2]
                    wait_for(pe, raw_done, i - 1)
                    if i < TT:
                        for c in range(DC):
                            last = pe.matmul(bank[:, 0:D], m.x_t[:, c, i * P:(i + 1) * P], wq[:, c, :],
                                             start=(c == 0), stop=(c == DC - 1))
                    else:
                        b, n = divmod(i - TT, KT)
                        if n == KT - 1:
                            pe.matmul(bank[:], ctx_common[:, b, :], wkv[:], start=True, stop=False)
                            last = pe.matmul(bank[:], ctx_last[:, b, :], wkv_last[:], start=False, stop=True)
                        else:
                            last = pe.matmul(bank[:], m.ctx_t[:, (i - TT) * P:(i - TT + 1) * P], wkv[:],
                                             start=True, stop=True)
                    last.then_inc(projected, 1)

                def turn(i):
                    pe.wait_ge(padded_done, i + 1)
                    wait_for(pe, kept, i - 1)
                    for g in range(GROUPS):
                        last = pe.transpose(turn_bank[i % 2][:, g * P:(g + 1) * P],
                                            padded[:, i % 2, g * GROUP:(g + 1) * GROUP, :].rearrange("p h d -> p (h d)"),
                                            m.ident[:])
                    last.then_inc(turned, 1)

                for i in range(tiles + 1):
                    if i < tiles:
                        project(i)
                    if i >= 1:
                        turn(i - 1)

            @block.scalar
            def _(act):
                def keep_tile(i):
                    to, per_batch, at = (m.q0_t, TT // BATCH, i) if i < TT else (m.k0_t, KT, i - TT)
                    b, n = divmod(at, per_batch)
                    act.wait_ge(turned, i + 1)
                    act.copy(to[:, b * GROUPS:(b + 1) * GROUPS, n * P:(n + 1) * P],
                             turn_bank[i % 2][:].rearrange("p (g q) -> p g q", g=GROUPS)).then_inc(kept, 1)

                for i in range(tiles):
                    slot = i % 2
                    act.wait_ge(centred_done, i + 1)
                    wait_for(act, variance_done, i - 1)
                    act.activation(squares[:, slot, :], centred[:, slot, :], ACT.Square).then_inc(squares_done, 1)
                    if i >= 1:
                        keep_tile(i - 1)
                keep_tile(tiles - 1)

            @block.vector
            def _(dve):
                def spread(a):
                    return a.rearrange("p (h a) -> p h a", a=1).broadcast_to([P, HEADS, H0])

                def of_heads(a):
                    return a.rearrange("p (a d) -> p a d", a=1).broadcast_to([P, HEADS, H0])

                dve.wait_ge(loaded, 16 * n_loads)
                dve.wait_ge(cleared, 3)
                for i in range(tiles):
                    slot, query = i % 2, i < TT
                    last_tile = not query and (i - TT) % KT == KT - 1
                    kind = 0 if query else 2 if last_tile else 1
                    width = D if query else 2 * D
                    bias = bq[:] if query else bkv[:, int(last_tile), :]
                    dve.wait_ge(projected, i + 1)
                    dve.tensor_tensor(raw[:, slot, 0:width], project_bank[slot][:, 0:width], bias, ALU.add).then_inc(raw_done, 1)
                    dve.wait_ge(raw_done, i + 1)
                    if query:
                        values = raw[:, slot, 0:D].rearrange("p (h d) -> p h d", h=HEADS)
                    else:
                        pairs = raw[:, slot, :].rearrange("p (h a d) -> p h a d", h=HEADS, a=2)
                        values = pairs[:, :, 0, :]
                        b, n = divmod(i - TT, KT)
                        dve.tensor_copy(m.v0[:, b * GROUPS:(b + 1) * GROUPS, n, :].rearrange("p g (j d) -> p g j d", j=GROUP),
                                        pairs[:, :, 1, :].rearrange("p (g j) d -> p g j d", j=GROUP)).then_inc(v_done, 1)
                    c3 = centred[:, slot, :].rearrange("p (h d) -> p h d", h=HEADS)
                    dve.tensor_reduce(sums[:, slot, :], values, AX_X, ALU.add).then_inc(sums_done, 1)
                    dve.wait_ge(sums_done, i + 1)
                    dve.tensor_scalar(means[:, slot, :], sums[:, slot, :], 1.0 / H0, None, ALU.mult).then_inc(means_done, 1)
                    dve.wait_ge(means_done, i + 1)
                    dve.tensor_tensor(c3, values, spread(means[:, slot, :]), ALU.subtract).then_inc(centred_done, 1)
                    dve.wait_ge(squares_done, i + 1)
                    dve.tensor_reduce(sums[:, slot, :], squares[:, slot, :].rearrange("p (h d) -> p h d", h=HEADS),
                                      AX_X, ALU.add).then_inc(variance_done, 1)
                    dve.wait_ge(variance_done, i + 1)
                    wait_for(dve, rstd_done, i - 1)
                    dve.tensor_scalar(variance[:, slot, :], sums[:, slot, :], 1.0 / H0, eps, ALU.mult,
                                      ALU.add).then_inc(spread_done, 1)
                    dve.wait_ge(rstd_done, i + 1)
                    dve.tensor_tensor(c3, c3, spread(rstd[:, slot, :]), ALU.mult).then_inc(scaled, 1)
                    dve.wait_ge(scaled, i + 1)
                    dve.tensor_tensor(c3, c3, of_heads(gain[:, kind, :]), ALU.mult).then_inc(gained, 1)
                    dve.wait_ge(gained, i + 1)
                    wait_for(dve, turned, i - 1)
                    dve.tensor_tensor(padded[:, slot, :, 0:H0], c3, of_heads(offset[:, kind, :]),
                                      ALU.add).then_inc(padded_done, 1)


def small_attention_stage(nc, m):
    scale = float(H0) ** -0.5
    cut = KEYS - LAST_KEYS
    parts = ((0, cut), (cut, KEYS))
    lag = 2
    turns = BATCH * GROUPS // 2
    with Stage(nc, m, "l0a") as st:
        q_t = st.sbuf("q_t", [P, 2, 2 * P])
        k_t = st.sbuf("k_t", [P, 2, KEYS])
        v = st.sbuf("v", [P, 2, KT, GROUP * H0])
        top = st.sbuf("top", [P, 4, 2])
        shift = st.sbuf("shift", [P, 4, 2])
        prob = st.sbuf("prob", [P, 4, KEYS])
        total = st.sbuf("total", [P, 4, 2])
        inverse = st.sbuf("inverse", [P, 2, 2, GROUP, 2])
        prob_t = st.sbuf("prob_t", [P, 2, 2, KT, P])
        score_bank = st.banks("score", 4)
        turn_bank = st.banks("turn", 2)
        o_bank = st.banks("o", 2)
        (staged, scores_ready, top_done, shift_done, exp_done, inverse_done, prob_done, turn_ready, pv_ready,
         o_kept) = st.sems("staged", "scores_ready", "top_done", "shift_done", "exp_done", "inverse_done", "prob_done",
                           "turn_ready", "pv_ready", "o_kept")
        turn_kept = st.sems("turn0_kept", "turn1_kept")

        def walk(engine, step):
            def two_groups(i, last=False):
                for k in range(2 * GROUP):
                    slot = k // GROUP
                    following = None if last and slot else (i + slot, 1 - slot)
                    step(i * (2 * GROUP) + k, k, i, following)

            two_groups(0)
            with engine.Fori(1, turns - 1) as i:
                two_groups(i)
            two_groups(turns - 1, True)
            for k in range(lag):
                step(PAIRS + k, k, None, None)

        def exists(pair, back):
            return not isinstance(pair, int) or 0 <= pair - back < PAIRS

        with st.block() as block:

            @block.gpsimd
            def _(pool):
                def stage(turn, slot):
                    group = turn * 2 + slot
                    wait_for(pool, scores_ready, turn * (4 * GROUP) + (slot - 1) * (2 * GROUP))
                    wait_for(pool, pv_ready, turn * (2 * GROUP) + (slot - 1) * GROUP)
                    pool.tensor_copy(q_t[:, slot, :], m.q0_t[:, group, :]).then_inc(staged, 1)
                    pool.tensor_copy(k_t[:, slot, :], m.k0_t[:, group, :]).then_inc(staged, 1)
                    pool.tensor_copy(v[:, slot, :, :], m.v0[:, group, :, :]).then_inc(staged, 1)

                def step(pair, k, turn, following):
                    if exists(pair, 0):
                        if k % GROUP == lag and following is not None:
                            stage(*following)

                stage(0, 0)
                walk(pool, step)

            @block.tensor
            def _(pe):
                def step(pair, k, turn, following):
                    slot, j = k // GROUP, k % GROUP
                    if exists(pair, 0):
                        if j == 0:
                            pe.wait_ge(staged, turn * 6 + (3 * slot + 3))
                        rows = slice(2 * H0 * j, 2 * H0 * j + H0)
                        for q in range(2):
                            wait_for(pe, exp_done, pair * 2 + (q - 3))
                            pe.matmul(score_bank[(2 * k + q) % 4][:], q_t[rows, slot, q * P:(q + 1) * P], k_t[rows, slot, :],
                                      start=True, stop=True).then_inc(scores_ready, 1)
                    if exists(pair, 1):
                        for q in range(2):
                            pe.wait_ge(prob_done, pair * 2 + (q - 1))
                            wait_for(pe, turn_kept[q], pair - 1)
                            for n in range(KT):
                                last = pe.transpose(turn_bank[q][:, n * P:(n + 1) * P],
                                                    prob[:, (2 * k - 2 + q) % 4, n * P:(n + 1) * P], m.ident[:])
                            last.then_inc(turn_ready, 1)
                    if exists(pair, 2):
                        old = (k - 2) % (2 * GROUP)
                        old_slot, old_j = old // GROUP, old % GROUP
                        if old_j == 0:
                            wait_for(pe, o_kept, turn * 2 + (old_slot - 1))
                        for q in range(2):
                            pe.wait_ge(turn_kept[q], pair - 1)
                        for q in range(2):
                            to = q * GROUP * H0 + old_j * H0
                            for n in range(KT):
                                last = pe.matmul(o_bank[old_slot][:, to:to + H0], prob_t[:, k % 2, q, n, :],
                                                 v[:, old_slot, n, old_j * H0:(old_j + 1) * H0],
                                                 start=(n == 0), stop=(n == KT - 1))
                        last.then_inc(pv_ready, 1)

                walk(pe, step)

            @block.scalar
            def _(act):
                def step(pair, k, turn, following):
                    if exists(pair, 0):
                        for q in range(2):
                            unit = (2 * k + q) % 4
                            act.wait_ge(shift_done, pair * 2 + (q + 1))
                            wait_for(act, turn_ready, pair * 2 + (q - 3))
                            wait_for(act, prob_done, pair * 2 + (q - 3))
                            for part, (first, end) in enumerate(parts):
                                last = act.activation(prob[:, unit, first:end], score_bank[unit][:, first:end], ACT.Exp,
                                                      bias=shift[:, unit, part:part + 1], scale=scale,
                                                      accum_out=total[:, unit, part:part + 1])
                            last.then_inc(exp_done, 1)
                    if exists(pair, 1):
                        act.wait_ge(turn_ready, pair * 2)
                        wait_for(act, pv_ready, pair - 2)
                        act.copy(prob_t[:, (k - 1) % 2, 1, :, :],
                                 turn_bank[1][:].rearrange("p (n t) -> p n t", n=KT)).then_inc(turn_kept[1], 1)

                walk(act, step)

            @block.vector
            def _(dve):
                def step(pair, k, turn, following):
                    if exists(pair, 0):
                        for q in range(2):
                            unit = (2 * k + q) % 4
                            dve.wait_ge(scores_ready, pair * 2 + (q + 1))
                            wait_for(dve, exp_done, pair * 2 + (q - 3))
                            for part, (first, end) in enumerate(parts):
                                last = dve.tensor_reduce(top[:, unit, part:part + 1], score_bank[unit][:, first:end],
                                                         AX_X, ALU.max)
                            last.then_inc(top_done, 1)
                            dve.wait_ge(top_done, pair * 2 + (q + 1))
                            dve.tensor_scalar(shift[:, unit, :], top[:, unit, :], -scale, None, ALU.mult).then_inc(shift_done, 1)
                    if exists(pair, 1):
                        dve.wait_ge(turn_ready, pair * 2 - 1)
                        wait_for(dve, pv_ready, pair - 2)
                        dve.tensor_copy(prob_t[:, (k - 1) % 2, 0, :, :],
                                        turn_bank[0][:].rearrange("p (n t) -> p n t", n=KT)).then_inc(turn_kept[0], 1)
                    if exists(pair, 0):
                        for q in range(2):
                            unit = (2 * k + q) % 4
                            slot, j = k // GROUP, k % GROUP
                            if j == 0:
                                wait_for(dve, o_kept, turn * 2 + (slot - 1))
                            dve.wait_ge(exp_done, pair * 2 + (q + 1))
                            dve.reciprocal(inverse[:, slot, q, j, :], total[:, unit, :]).then_inc(inverse_done, 1)
                            dve.wait_ge(inverse_done, pair * 2 + (q + 1))
                            dve.tensor_scalar(prob[:, unit, cut:], prob[:, unit, cut:], total[:, unit, 0:1],
                                              inverse[:, slot, q, j, 1:2], ALU.mult, ALU.mult).then_inc(prob_done, 1)
                    if exists(pair, 2) and (k - 2) % GROUP == GROUP - 1:
                        old_slot = (k - 2) // GROUP % 2
                        group = BATCH * GROUPS - 1 if turn is None else turn * 2 + (0 if k >= GROUP else -1)
                        dve.wait_ge(pv_ready, pair - 1)
                        dve.tensor_tensor(m.o0[:, :, group, :].rearrange("p q (j d) -> p q j d", j=GROUP),
                                          o_bank[old_slot][:, 0:2 * GROUP * H0].rearrange(
                                              "p (q j d) -> p q j d", q=2, j=GROUP),
                                          inverse[:, old_slot, :, :, 0:1].broadcast_to([P, 2, GROUP, H0]),
                                          ALU.mult).then_inc(o_kept, 1)

                walk(dve, step)


def small_output_stage(nc, m, dram):
    with Stage(nc, m, "l0o") as st:
        wo = st.sbuf("wo", [P, DC, D])
        bo = st.sbuf("bo", [P, D])
        o_t = st.sbuf("o_t", [P, 2, DC, P])
        part = st.sbuf("part", [P, 2, D])
        turn_bank = st.banks("turn", 2)
        y_bank = st.banks("y", 2)
        loaded, turned, kept, y_ready, part_done, x_added = st.sems("loaded", "turned", "kept", "y_ready", "part_done",
                                                                     "x_added")
        half = GROUPS // DC

        with st.block() as block:

            @block.sync
            def _(sp):
                sp.dma_start(wo[:], dram["wo"].rearrange("(c p) n -> p c n", p=P)).then_inc(loaded, 16)
                sp.dma_start(bo[:], dram["bo"].partition_broadcast(P)).then_inc(loaded, 16)

            @block.tensor
            def _(pe):
                pe.wait_ge(loaded, 32)
                for t in range(TT + 1):
                    if t < TT:
                        b, q = divmod(t, TT // BATCH)
                        wait_for(pe, kept, t - 1)
                        for c in range(DC):
                            first = b * GROUPS + c * half
                            last = pe.transpose(turn_bank[t % 2][:, c * P:(c + 1) * P],
                                                m.o0[:, q, first:first + half, :].rearrange("p g n -> p (g n)"), m.ident[:])
                        last.then_inc(turned, 1)
                    if t >= 1:
                        pe.wait_ge(kept, t)
                        wait_for(pe, part_done, t - 2)
                        for c in range(DC):
                            last = pe.matmul(y_bank[(t - 1) % 2][:, 0:D], o_t[:, (t - 1) % 2, c, :], wo[:, c, :],
                                             start=(c == 0), stop=(c == DC - 1))
                        last.then_inc(y_ready, 1)

            @block.scalar
            def _(act):
                for t in range(TT):
                    act.wait_ge(turned, t + 1)
                    wait_for(act, y_ready, t - 1)
                    act.copy(o_t[:, t % 2, :, :],
                             turn_bank[t % 2][:, 0:D].rearrange("p (c q) -> p c q", c=DC)).then_inc(kept, 1)

            @block.vector
            def _(dve):
                dve.wait_ge(loaded, 32)
                for t in range(TT):
                    dve.wait_ge(y_ready, t + 1)
                    wait_for(dve, x_added, t - 1)
                    dve.tensor_tensor(part[:, t % 2, :], y_bank[t % 2][:, 0:D], bo[:], ALU.add).then_inc(part_done, 1)
                    dve.wait_ge(part_done, t + 1)
                    dve.tensor_tensor(m.x[:, t, :], m.x[:, t, :], part[:, t % 2, :], ALU.add).then_inc(x_added, 1)


HIDDEN0 = 1024


def sparse_ffn_stage(nc, m, dram):
    halves = HIDDEN0 // BANK
    chunks = HIDDEN0 // P
    fours = HIDDEN0 // 4
    lag = 1
    with Stage(nc, m, "l0f") as st:
        wg = st.sbuf("wg", [P, DC, HIDDEN0])
        wu = st.sbuf("wu", [P, DC, HIDDEN0])
        wd = st.sbuf("wd", [P, chunks, D])
        x_t = st.sbuf("x_t", [P, 2, DC, P])
        gate = st.sbuf("gate", [P, 2, HIDDEN0])
        h = st.sbuf("h", [P, 2, HIDDEN0])
        size = st.sbuf("size", [P, HIDDEN0])
        beats_near = st.sbuf("beats_near", [P, fours, 2], BF16)
        beats_far = st.sbuf("beats_far", [P, fours, 2], BF16)
        beats_across = st.sbuf("beats_across", [P, fours, 2], BF16)
        front = st.sbuf("front", [P, fours, 2], BF16)
        back = st.sbuf("back", [P, fours, 2], BF16)
        wins = st.sbuf("wins", [P, fours, 4], BF16)
        kept = st.sbuf("kept", [P, 2, HIDDEN0])
        h_t = st.sbuf("h_t", [P, 2, chunks, P])
        gate_bank = st.banks("gate", halves)
        up_bank = st.banks("up", halves)
        turn_bank = st.banks("turn", 2)
        y_bank = st.banks("y", 2)
        (loaded, staged, gate_ready, up_ready, gate_done, h_done, size_done, near_done, far_done, across_done, front_done, back_done,
         wins_done, kept_done, turned, turn_kept, y_ready, x_added) = st.sems(
            "loaded", "staged", "gate_ready", "up_ready", "gate_done", "h_done", "size_done", "near_done", "far_done", "across_done",
            "front_done", "back_done", "wins_done", "kept_done", "turned", "turn_kept", "y_ready", "x_added")

        def walk(engine, step):
            for k in range(2):
                step(k, k)
            with engine.Fori(1, TT // 2) as i:
                for k in range(2):
                    step(i * 2 + k, k)
            for k in range(lag):
                step(TT + k, k)

        def exists(t, behind):
            return not isinstance(t, int) or 0 <= t - behind < TT

        with st.block() as block:

            @block.sync
            def _(sp):
                sp.dma_start(wg[:], dram["w_gate"].rearrange("(c p) n -> p c n", p=P)).then_inc(loaded, 16)
                sp.dma_start(wu[:], dram["w_up"].rearrange("(c p) n -> p c n", p=P)).then_inc(loaded, 16)
                sp.dma_start(wd[:], dram["w_down"].rearrange("(c p) n -> p c n", p=P)).then_inc(loaded, 16)

            @block.gpsimd
            def _(pool):
                def step(t, k):
                    if exists(t, 0):
                        wait_for(pool, up_ready, t * halves - halves)
                        pool.tensor_copy(x_t[:, k, :, :], m.x_t[:, :, bass.ds(t * P, P)]).then_inc(staged, 1)

                walk(pool, step)

            @block.tensor
            def _(pe):
                def step(t, k):
                    if exists(t, 0):
                        pe.wait_ge(staged, t + 1)
                        for n in range(halves):
                            columns = slice(n * BANK, (n + 1) * BANK)
                            for bank, w, ready, used in ((gate_bank[n], wg, gate_ready, gate_done),
                                                         (up_bank[n], wu, up_ready, h_done)):
                                wait_for(pe, used, t * halves + (n + 1 - halves))
                                for c in range(DC):
                                    last = pe.matmul(bank[:], x_t[:, k, c, :], w[:, c, columns],
                                                     start=(c == 0), stop=(c == DC - 1))
                                last.then_inc(ready, 1)
                    if exists(t, 1):
                        old = 1 - k
                        for half in range(2):
                            pe.wait_ge(kept_done, t)
                            wait_for(pe, turn_kept, t * 2 + (half - 3))
                            for n in range(chunks // 2):
                                c = half * (chunks // 2) + n
                                last = pe.transpose(turn_bank[half][:, n * P:(n + 1) * P], kept[:, old, c * P:(c + 1) * P],
                                                    m.ident[:])
                            last.then_inc(turned, 1)
                        pe.wait_ge(turn_kept, t * 2)
                        wait_for(pe, x_added, t - 2)
                        for c in range(chunks):
                            last = pe.matmul(y_bank[old][:, 0:D], h_t[:, old, c, :], wd[:, c, :],
                                             start=(c == 0), stop=(c == chunks - 1))
                        last.then_inc(y_ready, 1)

                pe.wait_ge(loaded, 48)
                walk(pe, step)

            @block.scalar
            def _(act):
                def step(t, k):
                    if exists(t, 0):
                        for n in range(halves):
                            act.wait_ge(gate_ready, t * halves + (n + 1))
                            wait_for(act, h_done, t * halves + (n + 1 - 2 * halves))
                            act.activation(gate[:, k, n * BANK:(n + 1) * BANK], gate_bank[n][:], ACT.Silu).then_inc(gate_done, 1)
                        act.wait_ge(h_done, t * halves + halves)
                        wait_for(act, across_done, t * 2)
                        act.activation(size[:], h[:, k, :], ACT.Abs).then_inc(size_done, 1)
                    if exists(t, 1):
                        old = 1 - k
                        for half in range(2):
                            act.wait_ge(turned, t * 2 + (half - 1))
                            wait_for(act, y_ready, t - 2)
                            act.copy(h_t[:, old, half * (chunks // 2):(half + 1) * (chunks // 2), :],
                                     turn_bank[half][:].rearrange("p (n t) -> p n t", n=chunks // 2)).then_inc(turn_kept, 1)

                walk(act, step)

            @block.vector
            def _(dve):
                s4 = size[:].rearrange("p (f e) -> p f e", e=4)

                def step(t, k):
                    if exists(t, 0):
                        for n in range(halves):
                            columns = slice(n * BANK, (n + 1) * BANK)
                            dve.wait_ge(gate_done, t * halves + (n + 1))
                            dve.wait_ge(up_ready, t * halves + (n + 1))
                            wait_for(dve, kept_done, t - 1)
                            dve.tensor_tensor(h[:, k, columns], gate[:, k, columns], up_bank[n][:], ALU.mult).then_inc(h_done, 1)
                        h4 = h[:, k, :].rearrange("p (f e) -> p f e", e=4)
                        k4 = kept[:, k, :].rearrange("p (f e) -> p f e", e=4)
                        dve.wait_ge(size_done, t + 1)
                        wait_for(dve, kept_done, t)
                        dve.tensor_tensor(beats_near[:], s4[:, :, 0:4:2], s4[:, :, 1:4:2], ALU.is_ge).then_inc(near_done, 1)
                        dve.tensor_tensor(beats_far[:], s4[:, :, 0:2], s4[:, :, 2:4], ALU.is_ge).then_inc(far_done, 1)
                        for e in range(2):
                            dve.tensor_tensor(beats_across[:, :, e], s4[:, :, e], s4[:, :, 3 - e], ALU.is_ge).then_inc(across_done, 1)
                        dve.wait_ge(near_done, t + 1)
                        dve.wait_ge(far_done, t + 1)
                        dve.wait_ge(across_done, t * 2 + 2)
                        dve.tensor_tensor(front[:], beats_far[:], beats_across[:], ALU.add).then_inc(front_done, 1)
                        for e in range(2):
                            dve.tensor_tensor(back[:, :, e], beats_far[:, :, e], beats_across[:, :, 1 - e], ALU.add).then_inc(back_done, 1)
                        dve.wait_ge(front_done, t + 1)
                        dve.wait_ge(back_done, t * 2 + 2)
                        dve.tensor_tensor(wins[:, :, 0], front[:, :, 0], beats_near[:, :, 0], ALU.add).then_inc(wins_done, 1)
                        dve.tensor_tensor(wins[:, :, 1], front[:, :, 1], beats_near[:, :, 0], ALU.subtract).then_inc(wins_done, 1)
                        dve.tensor_tensor(wins[:, :, 2], beats_near[:, :, 1], back[:, :, 0], ALU.subtract).then_inc(wins_done, 1)
                        dve.tensor_tensor(wins[:, :, 3], beats_near[:, :, 1], back[:, :, 1], ALU.add).then_inc(wins_done, 1)
                        dve.wait_ge(wins_done, t * 4 + 4)
                        dve.wait_ge(h_done, t * halves + halves)
                        wait_for(dve, turned, t * 2 - 2)
                        for e, (least, test) in enumerate(((2.0, ALU.is_ge), (1.0, ALU.is_ge), (0.0, ALU.is_ge), (1.0, ALU.is_le))):
                            last = dve.scalar_tensor_tensor(k4[:, :, e], wins[:, :, e], least, h4[:, :, e], test, ALU.mult)
                        last.then_inc(kept_done, 1)
                    if exists(t, 1):
                        dve.wait_ge(y_ready, t)
                        dve.tensor_tensor(m.x[:, t - 1, :], m.x[:, t - 1, :], y_bank[1 - k][:, 0:D], ALU.add).then_inc(x_added, 1)

                walk(dve, step)


STEPS1 = 4
HIDDEN1 = 1024


def thought_stage(nc, m, dram):
    eps = 1e-6
    chunks = HIDDEN1 // P
    B = BATCH
    IN_GAMMA, IN_BETA, AGG_B, PN_GAMMA, PN_BETA, D2_B, BC_B = range(7)
    small_names = ("in_gamma", "in_beta", "agg_b", "pn_gamma", "pn_beta", "d2_b", "bc_b")
    GATE_B, OUT_GAMMA, OUT_BETA = range(3)
    wide_names = ("gate_b", "out_gamma", "out_beta")
    with Stage(nc, m, "l1f") as st:
        weights = {"agg_w": st.sbuf("agg_w", [P, DC, D]), "d1_w": st.sbuf("d1_w", [P, DC, HIDDEN1]),
                   "d2_w": st.sbuf("d2_w", [P, chunks, D]), "bc_w": st.sbuf("bc_w", [P, DC, D]),
                   "gate_w": st.sbuf("gate_w", [P, DC, D])}
        d1_b = st.sbuf("d1_b", [P, chunks])
        small = st.sbuf("small", [B, len(small_names), D])
        wide = st.sbuf("wide", [P, len(wide_names), D])
        pick = st.sbuf("pick", [B, B, P])
        last_x = st.sbuf("last_x", [B, D])
        thought = st.sbuf("thought", [B, D])
        stats = st.sbuf("stats", [B, 6])
        moments = st.sbuf("moments", [B, 2])
        spread = st.sbuf("spread", [B, 1])
        rstd = st.sbuf("rstd", [B, 1])
        rows = st.sbuf("rows", [B, D])
        rows_t = st.sbuf("rows_t", [P, DC, B])
        hidden = st.sbuf("hidden", [P, chunks, B])
        active = st.sbuf("active", [P, chunks, B])
        delta = st.sbuf("delta", [B, D])
        said = st.sbuf("said", [P, B, D])
        raw = st.sbuf("raw", [P, TT, D])
        gate = st.sbuf("gate", [P, TT, D])
        out = st.sbuf("out", [P, TT, D])
        out_stats = st.sbuf("out_stats", [P, TT, 6])
        out_moments = st.sbuf("out_moments", [P, TT, 2])
        out_spread = st.sbuf("out_spread", [P, TT])
        out_rstd = st.sbuf("out_rstd", [P, TT])
        turn_bank, = st.banks("turn", 1)
        hidden_bank, = st.banks("hidden", 1)
        row_bank, = st.banks("row", 1)
        said_bank = st.banks("said", 2)
        gate_bank = st.banks("gate", 2)
        n_loads = len(weights) + len(small_names) + len(wide_names) + 2
        (loaded, last_loaded, own, spread_done, rstd_done, rows_set, turned, turn_kept, product_ready, product_read,
         hidden_ready, hidden_set, active_done, said_ready, said_kept, gate_ready, raw_done, gate_done, gated, added, offset_done,
         out_spread_done, out_rstd_done, scaled, gained) = st.sems(
            "loaded", "last_loaded", "own", "spread_done", "rstd_done", "rows_set", "turned", "turn_kept", "product_ready",
            "product_read", "hidden_ready", "hidden_set", "active_done", "said_ready", "said_kept", "gate_ready",
            "raw_done", "gate_done", "gated", "added", "offset_done", "out_spread_done", "out_rstd_done", "scaled", "gained")

        with st.block() as block:

            @block.sync
            def _(sp):
                sp.dma_start(last_x[:], m.x_n[P - 1:P, 1:TT:2, :]).then_inc(last_loaded, 16)
                for name, to in weights.items():
                    sp.dma_start(to[:], dram[name].rearrange("(c p) n -> p c n", p=P)).then_inc(loaded, 16)
                for n, name in enumerate(wide_names):
                    sp.dma_start(wide[:, n, :], dram[name].partition_broadcast(P)).then_inc(loaded, 16)
                for n, name in enumerate(small_names):
                    sp.dma_start(small[:, n, :], dram[name].partition_broadcast(B)).then_inc(loaded, 16)
                sp.dma_start(d1_b[:], dram["d1_b"]).then_inc(loaded, 16)
                sp.dma_start(pick[:], dram["pick"]).then_inc(loaded, 16)

            @block.gpsimd
            def _(pool):
                for n in range(1 + STEPS1):
                    pool.wait_ge(spread_done, n + 1)
                    pool.tensor_tensor(rstd[:], spread[:], m.minus_half[0:B, 0:1], ALU.pow).then_inc(rstd_done, 1)
                pool.wait_ge(said_kept, 2)
                for t in range(TT):
                    pool.wait_ge(gate_done, t + 1)
                    pool.tensor_tensor(gate[:, t, :], gate[:, t, :], said[:, t * B // TT, :], ALU.mult).then_inc(gated, 1)
                pool.wait_ge(out_spread_done, 1)
                pool.tensor_tensor(out_rstd[:], out_spread[:], m.minus_half[:, 0:TT], ALU.pow).then_inc(out_rstd_done, 1)
                for t in range(TT):
                    pool.wait_ge(scaled, t + 1)
                    pool.tensor_tensor(out[:, t, :], out[:, t, :], wide[:, OUT_GAMMA, :], ALU.mult).then_inc(gained, 1)

            @block.tensor
            def _(pe):
                products = 0

                def turn(n):
                    pe.wait_ge(rows_set, n + 1)
                    for c in range(DC):
                        last = pe.transpose(turn_bank[:, c * B:(c + 1) * B], rows[:, c * P:(c + 1) * P], m.ident[0:B, 0:B])
                    last.then_inc(turned, 1)
                    pe.wait_ge(turn_kept, n + 1)

                def project(w):
                    for c in range(DC):
                        last = pe.matmul(row_bank[0:B, 0:D], rows_t[:, c, :], w[:, c, :], start=(c == 0), stop=(c == DC - 1))
                    last.then_inc(product_ready, 1)

                pe.wait_ge(loaded, 16 * n_loads)
                for t in range(TT):
                    wait_for(pe, raw_done, t - 1)
                    for c in range(DC):
                        last = pe.matmul(gate_bank[t % 2][:, 0:D], m.x_t[:, c, t * P:(t + 1) * P], weights["gate_w"][:, c, :],
                                         start=(c == 0), stop=(c == DC - 1))
                    last.then_inc(gate_ready, 1)
                turn(0)
                project(weights["agg_w"])
                for n in range(STEPS1):
                    turn(1 + n)
                    for j in range(chunks):
                        for c in range(DC):
                            last = pe.matmul(hidden_bank[:, j * B:(j + 1) * B], weights["d1_w"][:, c, j * P:(j + 1) * P],
                                             rows_t[:, c, :], start=(c == 0), stop=(c == DC - 1))
                    last.then_inc(hidden_ready, 1)
                    pe.wait_ge(active_done, n + 1)
                    pe.wait_ge(product_read, n + 1)
                    for j in range(chunks):
                        last = pe.matmul(row_bank[0:B, 0:D], active[:, j, :], weights["d2_w"][:, j, :],
                                         start=(j == 0), stop=(j == chunks - 1))
                    last.then_inc(product_ready, 1)
                turn(1 + STEPS1)
                project(weights["bc_w"])
                pe.wait_ge(rows_set, 3 + STEPS1)
                for b in range(B):
                    last = pe.matmul(said_bank[b // 2][:, b % 2 * D:(b % 2 + 1) * D], pick[:, b, :], rows[:], start=True, stop=True)
                last.then_inc(said_ready, 1)

            @block.scalar
            def _(act):
                def keep_turn(n):
                    act.wait_ge(turned, n + 1)
                    act.copy(rows_t[:], turn_bank[:, 0:DC * B].rearrange("p (c b) -> p c b", c=DC)).then_inc(turn_kept, 1)

                for t in range(TT):
                    act.wait_ge(raw_done, t + 1)
                    act.activation(gate[:, t, :], raw[:, t, :], ACT.Sigmoid).then_inc(gate_done, 1)
                keep_turn(0)
                for n in range(STEPS1):
                    keep_turn(1 + n)
                    act.wait_ge(hidden_set, n + 1)
                    act.activation(active[:], hidden[:], ACT.Gelu).then_inc(active_done, 1)
                keep_turn(1 + STEPS1)
                act.wait_ge(said_ready, 1)
                for n in range(2):
                    act.copy(said[:, 2 * n:2 * n + 2, :], said_bank[n][:].rearrange("p (b d) -> p b d", b=2)).then_inc(said_kept, 1)

            @block.vector
            def _(dve):
                links = 0

                def link(instruction):
                    nonlocal links
                    links += 1
                    instruction.then_inc(own, 1)
                    dve.wait_ge(own, links)

                def norm(n, of, gamma, beta):
                    link(dve.bn_stats(stats[:], of[:]))
                    link(dve.bn_aggr(moments[:], stats[:]))
                    dve.tensor_scalar(spread[:], moments[:, 1:2], eps, None, ALU.add).then_inc(spread_done, 1)
                    dve.wait_ge(rstd_done, n + 1)
                    link(dve.tensor_scalar(rows[:], of[:], moments[:, 0:1], rstd[:], ALU.subtract, ALU.mult))
                    link(dve.tensor_tensor(rows[:], rows[:], small[:, gamma, :], ALU.mult))
                    dve.tensor_tensor(rows[:], rows[:], small[:, beta, :], ALU.add).then_inc(rows_set, 1)

                dve.wait_ge(loaded, 16 * n_loads)
                for t in range(TT):
                    dve.wait_ge(gate_ready, t + 1)
                    dve.tensor_tensor(raw[:, t, :], gate_bank[t % 2][:, 0:D], wide[:, GATE_B, :], ALU.add).then_inc(raw_done, 1)
                dve.wait_ge(last_loaded, 16)
                norm(0, last_x, IN_GAMMA, IN_BETA)
                dve.wait_ge(product_ready, 1)
                product = dve.tensor_tensor(thought[:], row_bank[0:B, 0:D], small[:, AGG_B, :], ALU.add)
                product.then_inc(product_read, 1)
                dve.wait_ge(product_read, 1)
                for n in range(STEPS1):
                    norm(1 + n, thought, PN_GAMMA, PN_BETA)
                    dve.wait_ge(hidden_ready, n + 1)
                    dve.tensor_tensor(hidden[:], hidden_bank[:, 0:chunks * B].rearrange("p (j b) -> p j b", j=chunks),
                                      d1_b[:].rearrange("p (j a) -> p j a", a=1).broadcast_to([P, chunks, B]),
                                      ALU.add).then_inc(hidden_set, 1)
                    dve.wait_ge(product_ready, n + 2)
                    dve.tensor_tensor(delta[:], row_bank[0:B, 0:D], small[:, D2_B, :], ALU.add).then_inc(product_read, 1)
                    dve.wait_ge(product_read, n + 2)
                    link(dve.tensor_tensor(thought[:], thought[:], delta[:], ALU.add))
                dve.tensor_copy(rows[:], thought[:]).then_inc(rows_set, 1)
                dve.wait_ge(product_ready, 2 + STEPS1)
                dve.tensor_tensor(rows[:], row_bank[0:B, 0:D], small[:, BC_B, :], ALU.add).then_inc(rows_set, 1)
                for t in range(TT):
                    dve.wait_ge(gated, t + 1)
                    dve.tensor_tensor(out[:, t, :], gate[:, t, :], m.x_n[:, t, :], ALU.add).then_inc(added, 1)
                    dve.wait_ge(added, t + 1)
                    link(dve.bn_stats(out_stats[:, t, :], out[:, t, :]))
                    link(dve.bn_aggr(out_moments[:, t, :], out_stats[:, t, :]))
                dve.tensor_scalar(out_spread[:], out_moments[:, :, 1], eps, None, ALU.add).then_inc(out_spread_done, 1)
                dve.wait_ge(out_rstd_done, 1)
                for t in range(TT):
                    dve.tensor_scalar(out[:, t, :], out[:, t, :], out_moments[:, t, 0:1], out_rstd[:, t:t + 1],
                                      ALU.subtract, ALU.mult).then_inc(scaled, 1)
                for t in range(TT):
                    dve.wait_ge(gained, t + 1)
                    dve.tensor_tensor(raw[:, t, :], out[:, t, :], wide[:, OUT_BETA, :], ALU.add).then_inc(offset_done, 1)
                    dve.wait_ge(offset_done, t + 1)
                    dve.tensor_tensor(m.x[:, t, :], m.x[:, t, :], raw[:, t, :], ALU.add)


def route_stage(nc, m, dram, name, experts, chosen, capacity):
    with Stage(nc, m, name) as st:
        pad = 8 - chosen
        gate_w = st.sbuf("gate_w", [P, DC, experts])
        before = st.sbuf("before", [P, 2, P], BF16)
        before_raw = st.sbuf("before_raw", [P, P])
        top = st.sbuf("top", [P, TT])
        total = st.sbuf("total", [P, TT])
        inverse = st.sbuf("inverse", [P, TT])
        logit = st.sbuf("logit", [P, TT, experts])
        prob = st.sbuf("prob", [P, TT, experts + pad])
        best = st.sbuf("best", [P, TT, 8])
        rest = st.sbuf("rest", [P, TT, experts + pad])
        mask = st.sbuf("mask", [P, TT, experts])
        mask_b = st.sbuf("mask_b", [P, TT, experts], BF16)
        share = st.sbuf("share", [P, TT, experts])
        left = st.sbuf("left", [experts, TOKENS])
        logit_bank, = st.banks("logit", 1)
        place_bank, = st.banks("place", 1)
        turn_bank = st.banks("turn", 2)
        loaded, logits_ready, own, shifted, exp_done, masked, places_ready, shares_done, turned = st.sems(
            "loaded", "logits_ready", "own", "shifted", "exp_done", "masked", "places_ready", "shares_done", "turned")
        wide = [P, TT, experts]

        def by_tile(a):
            return a.rearrange("p (t a) -> p t a", a=1).broadcast_to(wide)

        with st.block() as block:

            @block.sync
            def _(sp):
                sp.dma_start(gate_w[:], dram["gate_w"].rearrange("(c p) n -> p c n", p=P)).then_inc(loaded, 16)
                sp.dma_start(before_raw[:], dram["before"]).then_inc(loaded, 16)

            @block.tensor
            def _(pe):
                pe.wait_ge(loaded, 32)
                for t in range(TT):
                    for c in range(DC):
                        last = pe.matmul(logit_bank[:, t * experts:(t + 1) * experts], m.x_t[:, c, t * P:(t + 1) * P],
                                         gate_w[:, c, :], start=(c == 0), stop=(c == DC - 1))
                last.then_inc(logits_ready, 1)
                if capacity is not None:
                    pe.wait_ge(masked, 1)
                    for t in range(TT):
                        for s in range(t + 1):
                            last = pe.matmul(place_bank[:, t * experts:(t + 1) * experts], before[:, int(s < t), :],
                                             mask_b[:, s, :], start=(s == 0), stop=(s == t))
                    last.then_inc(places_ready, 1)
                pe.wait_ge(shares_done, 1)
                for t in range(TT):
                    bank, at = turn_bank[t * 2 // TT], t % (TT // 2) * P
                    last = pe.transpose(bank[0:experts, at:at + P], share[:, t, :], m.ident[:])
                last.then_inc(turned, 1)

            @block.scalar
            def _(act):
                act.wait_ge(shifted, 1)
                act.activation(prob[:, :, 0:experts], logit[:], ACT.Exp).then_inc(exp_done, 1)

            @block.vector
            def _(dve):
                links = 0

                def link(instruction):
                    nonlocal links
                    links += 1
                    instruction.then_inc(own, 1)
                    dve.wait_ge(own, links)

                dve.wait_ge(loaded, 32)
                dve.tensor_copy(before[:, 0, :], before_raw[:])
                link(dve.memset(before[:, 1, :], 1.0))
                dve.wait_ge(logits_ready, 1)
                logits = logit_bank[:, 0:TT * experts].rearrange("p (t e) -> p t e", t=TT)
                link(dve.tensor_reduce(top[:], logits, AX_X, ALU.max))
                dve.tensor_tensor(logit[:], logits, by_tile(top[:]), ALU.subtract).then_inc(shifted, 1)
                dve.wait_ge(exp_done, 1)
                p = prob[:, :, 0:experts]
                link(dve.tensor_reduce(total[:], p, AX_X, ALU.add))
                link(dve.reciprocal(inverse[:], total[:]))
                link(dve.tensor_tensor(p, p, by_tile(inverse[:]), ALU.mult))
                for t in range(TT):
                    last = dve.max(best[:, t, :], prob[:, t, 0:experts])
                link(last)
                for n in range(pad):
                    dve.memset(best[:, :, chosen + n], -1.0 - n)
                    last = dve.memset(prob[:, :, experts + n], -1.0 - n)
                if pad:
                    link(last)
                for t in range(TT):
                    last = dve.match_replace(rest[:, t, :], best[:, t, :], prob[:, t, :], -9.0)
                link(last)
                link(dve.tensor_tensor(mask[:], rest[:, :, 0:experts], p, ALU.not_equal))
                link(dve.tensor_tensor(share[:], p, mask[:], ALU.mult))
                dve.tensor_copy(mask_b[:], mask[:]).then_inc(masked, 1)
                link(dve.tensor_reduce(total[:], share[:], AX_X, ALU.add))
                link(dve.reciprocal(inverse[:], total[:]))
                last = dve.tensor_tensor(share[:], share[:], by_tile(inverse[:]), ALU.mult)
                if capacity is not None:
                    link(last)
                    dve.wait_ge(places_ready, 1)
                    places = place_bank[:, 0:TT * experts].rearrange("p (t e) -> p t e", t=TT)
                    last = dve.scalar_tensor_tensor(share[:], places, float(capacity), share[:], ALU.is_lt, ALU.mult)
                last.then_inc(shares_done, 1)
                dve.wait_ge(turned, 1)
                halves = [(turn_bank[n][0:experts, :], slice(n * BANK, (n + 1) * BANK)) for n in range(2)]
                for bank, at in halves:
                    last = dve.tensor_copy(m.mix[0:experts, 0, at], bank)
                link(last)
                for bank, at in halves:
                    last = dve.tensor_tensor(left[:, at], bank, m.mix[0:experts, 0, at], ALU.subtract)
                link(last)
                link(dve.tensor_copy(m.mix[0:experts, 1, :], left[:]))
                link(dve.tensor_tensor(left[:], left[:], m.mix[0:experts, 1, :], ALU.subtract))
                dve.tensor_copy(m.mix[0:experts, 2, :], left[:])


def experts_stage(nc, m, dram, name, experts, tiles, gated, shared):
    halves = TOKENS // BANK
    with Stage(nc, m, name) as st:
        w1 = st.sbuf("w1", [P, 2, DC, P])
        wu = st.sbuf("wu", [P, 2, DC, P])
        w2 = st.sbuf("w2", [P, 2, D])
        spread = st.sbuf("spread", [experts, 2, P], BF16)
        gate = st.sbuf("gate", [P, 2, BANK])
        upped = st.sbuf("upped", [P, 2, BANK])
        h = st.sbuf("h", [P, 2, TOKENS])
        y_t = st.sbuf("y_t", [P, DC, TOKENS])
        y_bank = st.banks("y", 2 * halves)
        work = st.banks("work", 4)
        w_loaded = st.sems("w_loaded0", "w_loaded1")
        shared_loaded = [st.sem(f"shared_loaded{j}") for j in range(shared)]
        hidden_ready, up_ready, mix_ready, gate_done, up_done, h_done, y_ready, y_kept, turned, x_added = st.sems(
            "hidden_ready", "up_ready", "mix_ready", "gate_done", "up_done", "h_done", "y_ready", "y_kept", "turned",
            "x_added")
        n_tiles = shared + tiles
        mix_bank = [work[2], work[2]] if gated else [work[1], work[2]]
        per_tile = 64 if gated else 48

        def walk(engine, step):
            for j in range(shared + 2):
                step(j, j % 2, None if j < shared else 0)
            with engine.Fori(1, tiles // 2) as i:
                for k in range(2):
                    step(i * 2 + (shared + k), (shared + k) % 2, i)
            step(n_tiles, n_tiles % 2, None)

        def exists(j, behind):
            return not isinstance(j, int) or 0 <= j - behind < n_tiles

        with st.block() as block:

            @block.sync
            def _(sp):
                def load(j, slot, expert_tile):
                    wait_for(sp, y_ready, j - 1)
                    sp.dma_start(w1[:, slot, :, :], dram["w1"][expert_tile]).then_inc(w_loaded[slot], 16)
                    sp.dma_start(w2[:, slot, :], dram["w2"][expert_tile]).then_inc(w_loaded[slot], 16)
                    sp.dma_start(spread[:, slot, :], dram["spread"][expert_tile]).then_inc(w_loaded[slot], 16)
                    if gated:
                        sp.dma_start(wu[:, slot, :, :], dram["wu"][expert_tile]).then_inc(w_loaded[slot], 16)

                for j in range(shared):
                    wait_for(sp, y_ready, j - 1)
                    sp.dma_start(w1[:, j % 2, :, :], dram["shared_w1"][j]).then_inc(shared_loaded[j], 16)
                    sp.dma_start(wu[:, j % 2, :, :], dram["shared_wu"][j]).then_inc(shared_loaded[j], 16)
                    sp.dma_start(w2[:, j % 2, :], dram["shared_w2"][j]).then_inc(shared_loaded[j], 16)
                for j in range(2):
                    load(shared + j, (shared + j) % 2, j)
                with sp.Fori(1, tiles // 2) as i:
                    for k in range(2):
                        load(i * 2 + (shared + k), (shared + k) % 2, i * 2 + k)

            @block.tensor
            def _(pe):
                def step(j, slot, turn):
                    is_shared = turn is None
                    if exists(j, 0):
                        if is_shared:
                            pe.wait_ge(shared_loaded[j], 48)
                        else:
                            pe.wait_ge(w_loaded[slot], turn * per_tile + per_tile)
                        for n in range(halves):
                            columns = slice(n * BANK, (n + 1) * BANK)
                            half = j * halves + n
                            wait_for(pe, gate_done, half - 1)
                            for c in range(DC):
                                last = pe.matmul(work[3 * n][:], w1[:, slot, c, :], m.x_t[:, c, columns],
                                                 start=(c == 0), stop=(c == DC - 1))
                            last.then_inc(hidden_ready, 1)
                            if gated or is_shared:
                                wait_for(pe, up_done if gated else h_done, half)
                                for c in range(DC):
                                    last = pe.matmul(work[1][:], wu[:, slot, c, :], m.x_t[:, c, columns],
                                                     start=(c == 0), stop=(c == DC - 1))
                                last.then_inc(up_ready, 1)
                            if not is_shared:
                                after_shared = isinstance(j, int) and j == shared
                                wait_for(pe, h_done, half if gated or after_shared else half - 1)
                                for part in range(3):
                                    last = pe.matmul(mix_bank[n][:], spread[:, slot, :], m.mix[0:experts, part, columns],
                                                     start=(part == 0), stop=(part == 2))
                                last.then_inc(mix_ready, 1)
                    if exists(j, 1):
                        old = 1 - slot
                        first = isinstance(j, int) and j == 1
                        final = isinstance(j, int) and j == n_tiles
                        for n in range(halves):
                            pe.wait_ge(h_done, j * halves + (n + 1 - halves))
                            for o in range(DC):
                                last = pe.matmul(y_bank[o * halves + n][:], w2[:, old, o * P:(o + 1) * P],
                                                 h[:, old, n * BANK:(n + 1) * BANK], start=first, stop=final,
                                                 skip_group_check=True)
                        last.then_inc(y_ready, 1)

                walk(pe, step)
                for t in range(TT):
                    bank = work[t % 2]
                    if t == 0:
                        pe.wait_ge(y_kept, DC * halves)
                    wait_for(pe, x_added, t - 1)
                    for o in range(DC):
                        last = pe.transpose(bank[:, o * P:(o + 1) * P], y_t[:, o, t * P:(t + 1) * P], m.ident[:])
                    last.then_inc(turned, 1)

            @block.scalar
            def _(act):
                def step(j, slot, turn):
                    if exists(j, 0):
                        for n in range(halves):
                            half = j * halves + n
                            act.wait_ge(hidden_ready, half + 1)
                            wait_for(act, h_done, half - 1)
                            act.activation(gate[:, n, :], work[3 * n][:], ACT.Silu).then_inc(gate_done, 1)

                walk(act, step)
                act.wait_ge(y_ready, n_tiles)
                for o in range(DC):
                    for n in range(halves):
                        act.copy(y_t[:, o, n * BANK:(n + 1) * BANK], y_bank[o * halves + n][:]).then_inc(y_kept, 1)

            @block.vector
            def _(dve):
                def step(j, slot, turn):
                    if exists(j, 0):
                        for n in range(halves):
                            half = j * halves + n
                            to = h[:, slot, n * BANK:(n + 1) * BANK]
                            dve.wait_ge(gate_done, half + 1)
                            wait_for(dve, y_ready, j - 1)
                            if turn is None:
                                dve.wait_ge(up_ready, half + 1)
                                dve.tensor_tensor(to, gate[:, n, :], work[1][:], ALU.mult).then_inc(h_done, 1)
                            elif gated:
                                dve.wait_ge(up_ready, half + 1)
                                dve.tensor_tensor(upped[:, n, :], gate[:, n, :], work[1][:], ALU.mult).then_inc(up_done, 1)
                                dve.wait_ge(up_done, half + 1)
                                dve.wait_ge(mix_ready, half + 1)
                                dve.tensor_tensor(to, upped[:, n, :], mix_bank[n][:], ALU.mult).then_inc(h_done, 1)
                            else:
                                dve.wait_ge(mix_ready, half + (1 - shared * halves))
                                dve.tensor_tensor(to, gate[:, n, :], mix_bank[n][:], ALU.mult).then_inc(h_done, 1)

                walk(dve, step)
                for t in range(TT):
                    dve.wait_ge(turned, t + 1)
                    dve.tensor_tensor(m.x[:, t, :], m.x[:, t, :], work[t % 2][:, 0:D], ALU.add).then_inc(x_added, 1)


class Memory:

    def __init__(self, nc, stack):
        def sbuf(name, shape, dtype=F32):
            return stack.enter_context(nc.sbuf_tensor(name, shape, dtype))

        self.banks = [stack.enter_context(nc.psum_tensor(f"bank{n}", [P, BANK], F32)) for n in range(8)]
        self.used_semaphores = []
        self.x = sbuf("x", [P, TT, D])
        self.x_t = sbuf("x_t", [P, DC, TOKENS])
        self.x_n = sbuf("x_n", [P, TT, D])
        self.ctx = sbuf("ctx", [P, BATCH * KT, CW])
        self.ctx_t = sbuf("ctx_t", [CW, BATCH * KEYS])
        self.ident = sbuf("ident", [P, P])
        self.ones = sbuf("ones", [P, 2])
        self.minus_half = sbuf("minus_half", [P, HEADS])
        self.mix = sbuf("mix", [64, 3, TOKENS], BF16)
        self.q0_t = sbuf("q0_t", [P, BATCH * GROUPS, 2 * P])
        self.k0_t = sbuf("k0_t", [P, BATCH * GROUPS, KEYS])
        self.v0 = sbuf("v0", [P, BATCH * GROUPS, KT, GROUP * H0])
        self.o0 = sbuf("o0", [P, 2, BATCH * GROUPS, GROUP * H0])


CAPACITY3 = 2 * (TOKENS * 8 // 32)


def build(nc, dram, stages=99):
    def of(prefix):
        return {k[len(prefix):]: v for k, v in dram.items() if k.startswith(prefix)} | {
            k: dram[k] for k in ("mask", "rms", "before", "pick")}

    with ExitStack() as stack:
        m = Memory(nc, stack)
        load_stage(nc, m, dram)
        order = [
            lambda: (norm_stage(nc, m, "l0n"), small_project_stage(nc, m, of("l0a_")),
                     small_attention_stage(nc, m), small_output_stage(nc, m, of("l0a_"))),
            lambda: (norm_stage(nc, m, "l0g"), sparse_ffn_stage(nc, m, of("l0f_"))),
            lambda: (norm_stage(nc, m, "l1n"), heads_stage(nc, m, of("l1a_"), "l1a", True)),
            lambda: (norm_stage(nc, m, "l1t", True), thought_stage(nc, m, of("l1f_"))),
            lambda: (norm_stage(nc, m, "l2n"), heads_stage(nc, m, of("l2a_"), "l2a", False)),
            lambda: (norm_stage(nc, m, "l2g"), route_stage(nc, m, of("l2f_"), "l2r", 64, 6, None),
                     experts_stage(nc, m, of("l2f_"), "l2f", 64, 88, False, 3)),
            lambda: (norm_stage(nc, m, "l3n"), heads_stage(nc, m, of("l3a_"), "l3a", False)),
            lambda: (norm_stage(nc, m, "l3g"), route_stage(nc, m, of("l3f_"), "l3r", 32, 8, CAPACITY3),
                     experts_stage(nc, m, of("l3f_"), "l3f", 32, 24, True, 0)),
        ]
        for stage in (order[n] for n in (range(stages) if isinstance(stages, int) and stages < 99 else
                                         range(len(order)) if stages == 99 else stages)):
            stage()
        store_stage(nc, m, dram)


def layouts(i):
    import numpy as _np

    def row_tiles(w):
        return w.reshape(-1, P, w.shape[-1])

    def in_tiles(w):
        return w.reshape(DC, P, -1, P).transpose(2, 1, 0, 3)

    def spread(experts, width):
        owner = _np.arange(experts * width) // width
        return (owner[None, :] == _np.arange(experts)[:, None]).reshape(experts, -1, P).transpose(1, 0, 2).astype(_np.dtype("bfloat16"))

    def heads_in(w):
        return w.reshape(DC, P, HEADS, P).transpose(2, 1, 0, 3).reshape(HEADS, P, DC * P)

    ctx = i["ctx_1024"].reshape(BATCH * KEYS, CW)
    a = {
        "x": i["x"].reshape(TOKENS, D), "ctx": ctx, "ctx_t": ctx.T, "mask": i["mask_BxS2_bf1"].reshape(-1).view(_np.uint8),
        "ident": _np.eye(P, dtype=_np.float32), "before": _np.triu(_np.ones((P, P), _np.float32), 1),
        "pick": _np.repeat(_np.eye(BATCH, dtype=_np.float32)[:, :, None], P, 2),
    }
    p = "L0_xattn_"
    a |= {f"l0a_{n}": i[p + w] for n, w in (
        ("wq", "Wq"), ("bq", "bq"), ("wo", "Wo"), ("bo", "bo"), ("qn_w", "qn_w"), ("qn_b", "qn_b"), ("kn_w", "kn_w"), ("kn_b", "kn_b"),
        ("kn_dca_w", "kn_dca_w"), ("kn_dca_b", "kn_dca_b"))}
    a["l0a_wkv"] = _np.concatenate([i[p + "Wk"], i[p + "Wv"]], 1)
    a["l0a_bkv"] = _np.concatenate([i[p + "bk"], i[p + "bv"]])
    a["l0a_wkv_last"] = i[p + "Wkv_dca"].reshape(CW, 2, HEADS, H0).transpose(0, 2, 1, 3).reshape(CW, 2 * D)
    a["l0a_bkv_last"] = i[p + "bkv_dca"].reshape(2, HEADS, H0).transpose(1, 0, 2).reshape(2 * D)
    a |= {f"l0f_{n}": i["L0_ffn_" + n] for n in ("w_gate", "w_up", "w_down")}
    p = "L1_xattn_"
    a |= {"l1a_wq": heads_in(i[p + "Wq"]), "l1a_wk": i[p + "Wk"].reshape(CW, HEADS, P).transpose(1, 0, 2),
          "l1a_wv_t": row_tiles(i[p + "Wv"].T), "l1a_wo": row_tiles(i[p + "Wo"]),
          "l1a_gq": i[p + "gq"][:, None], "l1a_gk": i[p + "gk"][:, None]}
    a |= {f"l1f_{n}": i["L1_ffn_" + n] for n in ("in_gamma", "in_beta", "agg_w", "agg_b", "pn_gamma", "pn_beta", "d1_w", "d2_w", "d2_b",
                                                "bc_w", "bc_b", "gate_w", "gate_b", "out_gamma", "out_beta")}
    a["l1f_d1_b"] = i["L1_ffn_d1_b"].reshape(-1, P).T
    for n in (2, 3):
        p = f"L{n}_xattn_"
        a |= {f"l{n}a_wq": row_tiles(i[p + "Wq"].T), f"l{n}a_wk": row_tiles(i[p + "Wk"].T), f"l{n}a_wv_t": row_tiles(i[p + "Wv"].T),
              f"l{n}a_wo": row_tiles(i[p + "Wo"])}
    p = "L2_ffn_"
    inner = i[p + "shared_down"].shape[1]
    short = -inner % P
    gate, up = (_np.pad(w.T, ((0, 0), (0, short))) for w in (i[p + "shared_gate_up"][:inner], i[p + "shared_gate_up"][inner:]))
    a |= {"l2f_gate_w": i[p + "gate_w"].T, "l2f_w1": in_tiles(i[p + "experts_w1"].reshape(-1, D).T),
          "l2f_w2": row_tiles(i[p + "experts_w2"].transpose(0, 2, 1).reshape(-1, D)), "l2f_spread": spread(64, 176),
          "l2f_shared_w1": in_tiles(gate), "l2f_shared_wu": in_tiles(up),
          "l2f_shared_w2": row_tiles(_np.pad(i[p + "shared_down"].T, ((0, short), (0, 0))))}
    p = "L3_ffn_"
    a |= {"l3f_gate_w": i[p + "gate_w"], "l3f_w1": in_tiles(i[p + "w_gate"].transpose(1, 0, 2).reshape(D, -1)),
          "l3f_wu": in_tiles(i[p + "w_up"].transpose(1, 0, 2).reshape(D, -1)), "l3f_w2": row_tiles(i[p + "w_down"].reshape(-1, D)),
          "l3f_spread": spread(32, 96)}
    return {n: _np.ascontiguousarray(v) for n, v in a.items()}


def kernel(_stages=99, **inputs):
    import numpy as _np
    import concourse.bacc as _bacc
    from concourse.bass_utils import run_bass_kernel_spmd as _run

    arrays = layouts({n: _np.asarray(v) for n, v in inputs.items()})
    nc = _bacc.Bacc("TRN2", target_bir_lowering=False, num_devices=1)
    dram = {n: nc.dram_tensor(f"in_{n}", v.shape, mybir.dt.from_np(v.dtype), kind="ExternalInput").ap() for n, v in arrays.items()}
    dram["rms"] = nc.dram_tensor("rms", (2, BATCH * KT, P), F32, kind="Internal").ap()
    dram["out"] = nc.dram_tensor("out", (TOKENS, D), F32, kind="ExternalOutput").ap()
    build(nc, dram, _stages)
    r = _run(nc, [{f"in_{n}": v for n, v in arrays.items()}], core_ids=[0])
    return r.results[0]["out"].reshape(BATCH, TOKENS // BATCH, D)
```

```python
from contextlib import ExitStack

import concourse.bass as bass
from concourse import mybir
from concourse.alu_op_type import AluOpType as ALU

ACT = mybir.ActivationFunctionType
AX_X = mybir.AxisListType.X
F32 = mybir.dt.float32
F32R = mybir.dt.float32r
BF16 = mybir.dt.bfloat16
U8 = mybir.dt.uint8

P = 128
BATCH = 4
TOKENS = 1024
TT = TOKENS // P
D = 256
DC = D // P
KEYS = 512
KT = KEYS // P
CW = 128
HEADS = 16
BANK = 512
LOWEST = -3.0e38
MASKED = 1.0e30
PAIRS = HEADS * BATCH
AHEAD = 4
RMS_EPS = 1e-5


def wait_for(engine, semaphore, count):
    if not isinstance(count, int) or count > 0:
        engine.wait_ge(semaphore, count)


class Stage:

    def __init__(self, nc, m, name):
        self.nc, self.m, self.name, self.stack, self.free_banks = nc, m, name, ExitStack(), list(m.banks)
        self.semaphores = []

    def __enter__(self):
        return self

    def __exit__(self, *error):
        self.stack.close()
        self.m.used_semaphores = self.semaphores

    def sbuf(self, name, shape, dtype=F32):
        return self.stack.enter_context(self.nc.sbuf_tensor(f"{self.name}_{name}", shape, dtype))

    def banks(self, name, count):
        given, self.free_banks = self.free_banks[:count], self.free_banks[count:]
        assert len(given) == count, name
        return given

    def sem(self, name):
        self.semaphores.append(self.nc.alloc_semaphore(name=f"{self.name}_{name}"))
        return self.semaphores[-1]

    def sems(self, *names):
        return [self.sem(n) for n in names]

    def block(self):
        if self.m.used_semaphores:
            self.nc.clear_and_free_semaphores(self.m.used_semaphores)
        return self.nc.Block()


def load_stage(nc, m, dram):
    with Stage(nc, m, "load") as st:
        loaded, set_up = st.sems("loaded", "set_up")
        with st.block() as block:

            @block.sync
            def _(sp):
                sp.dma_start(m.x[:], dram["x"].rearrange("(t p) d -> p t d", p=P)).then_inc(loaded, 16)
                sp.dma_start(m.ident[:], dram["ident"]).then_inc(loaded, 16)
                sp.wait_ge(loaded, 32)

            @block.gpsimd
            def _(pool):
                pool.memset(m.minus_half[:], -0.5).then_inc(set_up, 1)
                pool.memset(m.ones[:], 1.0).then_inc(set_up, 1)
                pool.wait_ge(set_up, 2)


def context_stage(nc, m, dram):
    with Stage(nc, m, "ctx") as st:
        ctx = st.sbuf("ctx", [P, BATCH * KT, CW])
        ctx_t = st.sbuf("ctx_t", [CW, BATCH * KEYS])
        ctx_loaded, ctx_t_loaded, high_done = st.sems("ctx_loaded", "ctx_t_loaded", "high_done")
        with st.block() as block:

            @block.sync
            def _(sp):
                sp.dma_start(ctx[:], dram["ctx"].rearrange("(t p) c -> p t c", p=P)).then_inc(ctx_loaded, 16)

            @block.scalar
            def _(act):
                act.dma_start(ctx_t[:], dram["ctx_t"]).then_inc(ctx_t_loaded, 16)
                act.wait_ge(ctx_loaded, 16)
                act.copy(m.ctx_high[:], ctx[:]).then_inc(high_done, 1)
                act.wait_ge(ctx_t_loaded, 16)
                act.copy(m.ctx_t_high[:], ctx_t[:]).then_inc(high_done, 1)

            @block.vector
            def _(dve):
                dve.wait_ge(high_done, 1)
                dve.tensor_tensor(m.ctx_low[:], ctx[:], m.ctx_high[:].bitcast(F32), ALU.subtract)
                dve.wait_ge(high_done, 2)
                dve.tensor_tensor(m.ctx_t_low[:], ctx_t[:], m.ctx_t_high[:].bitcast(F32), ALU.subtract)


def store_stage(nc, m, dram):
    with Stage(nc, m, "store") as st:
        stored = st.sem("stored")
        with st.block() as block:

            @block.sync
            def _(sp):
                sp.dma_start(dram["out"].rearrange("(t p) d -> p t d", p=P), m.x[:]).then_inc(stored, 16)
                sp.wait_ge(stored, 16)


def norm_stage(nc, m, name, whole, parts, keep):
    eps = 1e-5
    with Stage(nc, m, name) as st:
        stats = st.sbuf("stats", [P, TT, 6])
        moments = st.sbuf("moments", [P, TT, 2])
        spread = st.sbuf("spread", [P, TT])
        rstd = st.sbuf("rstd", [P, TT])
        xn = st.sbuf("xn", [P, 2, D])
        turned = st.banks("turned", 2)
        stats_done, moments_done, spread_done, rstd_done, xn_done, turned_ready, high_done, low_done, copied = st.sems(
            "stats_done", "moments_done", "spread_done", "rstd_done", "xn_done", "turned_ready", "high_done", "low_done", "copied")
        with st.block() as block:

            @block.vector
            def _(dve):
                with dve.Fori(0, TT) as t:
                    dve.bn_stats(stats[:, t, :], m.x[:, t, :]).then_inc(stats_done, 1)
                dve.wait_ge(stats_done, TT)
                for t in range(TT):
                    last = dve.bn_aggr(moments[:, t, :], stats[:, t, :])
                last.then_inc(moments_done, 1)
                dve.wait_ge(moments_done, 1)
                dve.tensor_scalar(spread[:], moments[:, :, 1], eps, None, ALU.add).then_inc(spread_done, 1)
                dve.wait_ge(rstd_done, 1)

                def normalise(t, slot):
                    dve.tensor_scalar(xn[:, slot, :], m.x[:, t, :], moments[:, t, 0:1], rstd[:, bass.ds(t, 1)],
                                      ALU.subtract, ALU.mult).then_inc(xn_done, 1)

                def keep_low(t, slot):
                    dve.wait_ge(high_done, t + 1)
                    at = bass.ds(t * P, P)
                    dve.tensor_tensor(m.x_low[:, :, at], turned[slot][:, 0:D].rearrange("p (c q) -> p c q", c=DC),
                                      m.x_high[:, :, at].bitcast(F32), ALU.subtract).then_inc(low_done, 1)

                for slot in range(2):
                    normalise(slot, slot)
                with dve.Fori(1, TT // 2) as i:
                    for slot in range(2):
                        dve.wait_ge(turned_ready, 2 * i + (slot - 1))
                        if keep:
                            dve.wait_ge(copied, 2 * i + (slot - 1))
                        normalise(2 * i + slot, slot)
                        if parts:
                            keep_low(2 * i + (slot - 2), slot)
                for slot in range(2 if parts else 0):
                    keep_low(TT - 2 + slot, slot)

            @block.gpsimd
            def _(pool):
                pool.wait_ge(spread_done, 1)
                pool.tensor_tensor(rstd[:], spread[:], m.minus_half[:, 0:TT], ALU.pow).then_inc(rstd_done, 1)
                if keep:
                    for t in range(TT):
                        pool.wait_ge(xn_done, t + 1)
                        pool.tensor_copy(m.x_n[:, t, :], xn[:, t % 2, :]).then_inc(copied, 1)

            @block.tensor
            def _(pe):
                def turn(t, slot):
                    pe.wait_ge(xn_done, t + 1)
                    for c in range(DC):
                        last = pe.transpose(turned[slot][:, c * P:(c + 1) * P], xn[:, slot, c * P:(c + 1) * P],
                                            m.ident[:])
                    last.then_inc(turned_ready, 1)

                for slot in range(2):
                    turn(slot, slot)
                with pe.Fori(1, TT // 2) as i:
                    for slot in range(2):
                        pe.wait_ge(low_done if parts else high_done, 2 * i + (slot - 1))
                        turn(2 * i + slot, slot)

            @block.scalar
            def _(act):
                with act.Fori(0, TT // 2) as i:
                    for slot in range(2):
                        act.wait_ge(turned_ready, 2 * i + (slot + 1))
                        tile = turned[slot][:, 0:D].rearrange("p (c q) -> p c q", c=DC)
                        at = bass.ds((2 * i + slot) * P, P)
                        for to in ([m.x_t] if whole else []) + ([m.x_high] if parts else []):
                            last = act.copy(to[:, :, at], tile)
                        last.then_inc(high_done, 1)


def heads_stage(nc, m, dram, name, qk_norm):
    scale = float(P) ** -0.5
    n_k = BATCH * KEYS // BANK
    rows = BATCH * KT
    if qk_norm:
        quarters = [["k0", "k1", "k2", "k3"], ["q0", "kk"], ["q1", "row"], ["qq", "wvo"]]
    else:
        quarters = [["a"], ["q0"], ["q1"], ["wvo"]]
    pieces = [piece for quarter in quarters for piece in quarter]
    n_pieces = len(pieces)
    last_q, k_pieces = pieces.index("q1"), n_k
    n_splits = 2 if qk_norm else 4
    with Stage(nc, m, name) as st:
        wq = st.sbuf("wq", [P, 2, D])
        wk = st.sbuf("wk", [P, 2, CW])
        wv_t = st.sbuf("wv_t", [P, 2, CW])
        wo = st.sbuf("wo", [P, 2, D])
        wvo = st.sbuf("wvo", [P, 2, D])
        wvo_high = st.sbuf("wvo_high", [P, 2, D], F32R)
        wvo_low = st.sbuf("wvo_low", [P, 2, D], F32R)
        q_t = st.sbuf("q_t", [P, 2, TOKENS])
        side = st.sbuf("side", [P, 2, BATCH * KEYS])
        valid = st.sbuf("valid", [P, BATCH])
        masked = st.sbuf("masked", [P, 4, KEYS])
        top = st.sbuf("top", [P, 4])
        shift = st.sbuf("shift", [P, 4])
        prob = st.sbuf("prob", [P, 4, KEYS])
        total = st.sbuf("total", [P, 16])
        inverse = st.sbuf("inverse", [P, 4])
        woken = st.sbuf("woken", [P, 1])
        pool_woken = st.sbuf("pool_woken", [P, 1])
        prob_high = st.sbuf("prob_high", [P, 2, KT, 2 * P], F32R)
        prob_low = st.sbuf("prob_low", [P, 2, KT, 2 * P], F32R)
        o_high = st.sbuf("o_high", [P, 2, 2 * P], F32R)
        o_low = st.sbuf("o_low", [P, 2, 2 * P], F32R)
        if qk_norm:
            wq_high = st.sbuf("wq_high", [P, 2, D], F32R)
            wq_low = st.sbuf("wq_low", [P, 2, D], F32R)
            wk_high = st.sbuf("wk_high", [P, 2, CW], F32R)
            wk_low = st.sbuf("wk_low", [P, 2, CW], F32R)
            k_t = st.sbuf("k_t", [P, 2, BATCH * KEYS])
            q_squares = st.sbuf("q_squares", [P, TOKENS])
            k_squares = st.sbuf("k_squares", [P, BATCH * KEYS])
            gain = st.sbuf("gain", [P, 2])
            gains = st.sbuf("gains", [P, 1])
            q_means = st.sbuf("q_means", [P, TT])
            k_means = st.sbuf("k_means", [P, rows])
            k_rms = st.sbuf("k_rms", [P, rows])
            q_scale = st.sbuf("q_scale", [P, 2, TT])
            rms_row = st.sbuf("rms_row", [rows, P])
        else:
            a_h = st.sbuf("a_h", [P, 2, D])
            a_high = st.sbuf("a_high", [P, 2, D], F32R)
            a_low = st.sbuf("a_low", [P, 2, D], F32R)
            q_high = st.sbuf("q_high", [P, 2, TOKENS], F32R)
            q_low = st.sbuf("q_low", [P, 2, TOKENS], F32R)
            mask_u8 = st.sbuf("mask_u8", [P, BATCH * KEYS], U8)
        score_bank = st.banks("score", 2)
        turn_bank = st.banks("turn", 2)
        o_bank, = st.banks("o", 1)
        y_bank, = st.banks("y", 1)
        prep_bank = st.banks("prep", 2)
        w_loaded = st.sems("w_loaded0", "w_loaded1")
        rms_loaded = st.sems("rms_loaded0", "rms_loaded1")
        (side_loaded, scores_ready, top_done, shift_done, exp_done, inverse_done, turn_ready,
         high_done, turn_kept, pv_ready, o_high_done, o_kept, own_high, squared, split_done, y_ready, x_added, prep_ready, prep_kept) = st.sems(
            "side_loaded", "scores_ready", "top_done", "shift_done", "exp_done", "inverse_done",
            "turn_ready", "high_done", "turn_kept", "pv_ready", "o_high_done", "o_kept", "own_high", "squared", "split_done", "y_ready", "x_added", "prep_ready",
            "prep_kept")
        (set_up, k_rms_done, q_scale_done, row_stored, gain_loaded) = st.sems(
            "set_up", "k_rms_done", "q_scale_done", "row_stored", "gain_loaded")

        def walk(engine, prepare, step):
            def two_heads(i, last=False):
                for k in range(2 * BATCH):
                    after, ahead = quarters[k % BATCH], k // BATCH + 1
                    if last and ahead == 2:
                        after = []
                    head = (i * 2 + k // BATCH, i, k // BATCH)
                    following = (i * 2 + ahead, i + ahead // 2, ahead % 2)
                    step(i * (2 * BATCH) + k, k, head, after, following)

            for piece in pieces:
                prepare(piece, (0, 0, 0))
            two_heads(0)
            with engine.Fori(1, HEADS // 2 - 1) as i:
                two_heads(i)
            two_heads(HEADS // 2 - 1, True)
            for k in range(AHEAD):
                step(PAIRS + k, k, None, [], None)

        def exists(pair, back):
            return not isinstance(pair, int) or 0 <= pair - back < PAIRS

        with st.block() as block:

            @block.sync
            def _(sp):
                if qk_norm:
                    sp.dma_start(gain[:, 0:1], dram["gq"]).then_inc(gain_loaded, 16)
                    sp.dma_start(gain[:, 1:2], dram["gk"]).then_inc(gain_loaded, 16)
                else:
                    sp.dma_start(mask_u8[:], dram["mask"].partition_broadcast(P)).then_inc(side_loaded, 16)

                def load(h, g, slot):
                    sp.dma_start(wq[:, slot, :], dram["wq"][h]).then_inc(w_loaded[slot], 16)
                    sp.dma_start(wk[:, slot, :], dram["wk"][g]).then_inc(w_loaded[slot], 16)
                    sp.dma_start(wv_t[:, slot, :], dram["wv_t"][g]).then_inc(w_loaded[slot], 16)
                    sp.dma_start(wo[:, slot, :], dram["wo"][h]).then_inc(w_loaded[slot], 16)

                def spread_rms(h, slot):
                    rows_kept, free, stored = (known(count) for count in (
                        h * n_pieces + (pieces.index("row") + 1), h * (2 * BATCH) - 2 * BATCH, h * 16 + 16))
                    sp.wait_ge(prep_kept, rows_kept)
                    wait_for(sp, top_done, free)
                    sp.dma_start(dram["rms"][slot], rms_row[:]).then_inc(row_stored, 16)
                    sp.wait_ge(row_stored, stored)
                    sp.dma_start(side[:, slot, :],
                                 dram["rms"][slot].rearrange("t p -> (t p)").partition_broadcast(P)
                                 ).then_inc(rms_loaded[slot], 16)

                def known(count):
                    return count if isinstance(count, int) else sp.snap(count)

                for h in range(2):
                    load(h, h if qk_norm else 0, h)
                if qk_norm:
                    spread_rms(0, 0)
                with sp.Fori(1, HEADS // 2) as i:
                    for slot in range(2):
                        sp.wait_ge(prep_kept, i * (2 * n_pieces) + (slot - 1) * n_pieces)
                        load(i * 2 + slot, i * 2 + slot if qk_norm else i, slot)
                        if qk_norm:
                            spread_rms(i * 2 + (slot - 1), 1 - slot)
                if qk_norm:
                    spread_rms(HEADS - 1, 1)

            @block.tensor
            def _(pe):
                def product(to, left, right, start, stop):
                    pe.matmul(to, left[0], right[0], start=start, stop=False)
                    pe.matmul(to, left[0], right[1], start=False, stop=False)
                    return pe.matmul(to, left[1], right[0], start=False, stop=stop)

                def prepare(piece, head):
                    h, turn, slot = head
                    n = pieces.index(piece)
                    if n == 0:
                        pe.wait_ge(w_loaded[slot], turn * 64 + 64)
                        if qk_norm:
                            pe.wait_ge(split_done, h * n_splits + 1)
                    bank = prep_bank[n % 2]
                    wait_for(pe, prep_kept, h * n_pieces + (n - 1))
                    if piece == "a":
                        for c in range(DC):
                            last = pe.matmul(bank[:, c * P:(c + 1) * P], wq[:, slot, c * P:(c + 1) * P],
                                             wk[:, slot, :], start=True, stop=True)
                    elif piece in ("q0", "q1"):
                        chunk = int(piece[1])
                        if not qk_norm:
                            pe.wait_ge(split_done, h * n_splits + 1)
                        left = (wq_high, wq_low) if qk_norm else (a_high, a_low)
                        for c in range(DC):
                            last = product(bank[:], [of[:, slot, c * P:(c + 1) * P] for of in left],
                                           [of[:, c, chunk * BANK:(chunk + 1) * BANK] for of in (m.x_high, m.x_low)],
                                           c == 0, c == DC - 1)
                    elif piece == "wvo":
                        last = pe.matmul(bank[:, 0:D], wv_t[:, slot, :], wo[:, slot, :], start=True, stop=True)
                    elif piece in ("kk", "qq"):
                        of, tiles = (k_squares, rows) if piece == "kk" else (q_squares, TT)
                        if piece == "kk":
                            pe.wait_ge(squared, h * k_pieces + k_pieces)
                        else:
                            pe.wait_ge(prep_kept, h * n_pieces + (last_q + 1))
                        for t in range(tiles):
                            last = pe.matmul(bank[:, t:t + 1], of[:, t * P:(t + 1) * P], m.ones[:, 0:1],
                                             start=True, stop=True)
                    elif piece == "row":
                        pe.wait_ge(k_rms_done, h + 1)
                        last = pe.transpose(bank[0:rows, 0:P], k_rms[:], m.ident[:])
                    else:
                        chunk = int(piece[1])
                        last = product(bank[:], (wk_high[:, slot, :], wk_low[:, slot, :]),
                                       [of[:, chunk * BANK:(chunk + 1) * BANK] for of in (m.ctx_t_high, m.ctx_t_low)],
                                       True, True)
                    last.then_inc(prep_ready, 1)

                def step(pair, k, head, after, following):
                    b = k % BATCH
                    if exists(pair, 0):
                        h, _, slot = head
                        if b == 0:
                            pe.wait_ge(prep_kept, h * n_pieces + n_pieces)
                            if not qk_norm:
                                pe.wait_ge(split_done, h * n_splits + 3)
                        keys = slice(b * KEYS, (b + 1) * KEYS)
                        for q in range(2):
                            wait_for(pe, top_done, pair * 2 + (q - 1))
                            at = slice((2 * b + q) * P, (2 * b + q + 1) * P)
                            if qk_norm:
                                last = pe.matmul(score_bank[q][:], q_t[:, slot, at], k_t[:, slot, keys], start=True, stop=True)
                            else:
                                last = product(score_bank[q][:], (q_high[:, slot, at], q_low[:, slot, at]),
                                               (m.ctx_t_high[:, keys], m.ctx_t_low[:, keys]), True, True)
                            last.then_inc(scores_ready, 1)
                    if exists(pair, 3):
                        pe.wait_ge(turn_kept, pair * 2 - 4)
                        wait_for(pe, o_kept, pair - 3)
                        for n in range(KT):
                            tile = (k - 3) % BATCH * KT + n
                            last = product(o_bank[:, 0:2 * P], (m.ctx_high[:, tile, :], m.ctx_low[:, tile, :]),
                                           (prob_high[:, (k - 3) % 2, n, :], prob_low[:, (k - 3) % 2, n, :]), n == 0, n == KT - 1)
                        last.then_inc(pv_ready, 1)
                    if exists(pair, 4):
                        pe.wait_ge(o_kept, pair - 3)
                        wait_for(pe, x_added, pair * 2 - 8)
                        if k % BATCH == 0:
                            h = HEADS if head is None else head[0]
                            pe.wait_ge(split_done, h * n_splits)
                        old = (k - 4) // BATCH % 2
                        for q in range(2):
                            at = slice(q * P, (q + 1) * P)
                            last = product(y_bank[:, q * D:(q + 1) * D], [of[:, k % 2, at] for of in (o_high, o_low)],
                                           (wvo_high[:, old, :], wvo_low[:, old, :]), True, True)
                        last.then_inc(y_ready, 1)
                    for piece in after:
                        prepare(piece, following)
                    if exists(pair, 1):
                        for q in range(2):
                            pe.wait_ge(exp_done, pair * 2 + (q - 1))
                            wait_for(pe, turn_kept, pair * 2 + (q - 3))
                            for n in range(KT):
                                last = pe.transpose(turn_bank[q][:, n * P:(n + 1) * P],
                                                    prob[:, (2 * k - 2 + q) % 4, n * P:(n + 1) * P], m.ident[:])
                            last.then_inc(turn_ready, 1)

                walk(pe, prepare, step)

            @block.scalar
            def _(act):
                def prepare(piece, head):
                    h, turn, slot = head
                    n = pieces.index(piece)
                    bank = prep_bank[n % 2]
                    act.wait_ge(prep_ready, h * n_pieces + (n + 1))
                    if piece == "a":
                        last = act.copy(a_h[:, slot, :], bank[:, 0:D])
                    elif piece in ("q0", "q1"):
                        chunk = int(piece[1])
                        columns = slice(chunk * BANK, (chunk + 1) * BANK)
                        if qk_norm:
                            act.activation(q_squares[:, columns], bank[:], ACT.Square)
                            last = act.activation(q_t[:, slot, columns], bank[:], ACT.Copy, scale=gains[:, 0:1])
                        else:
                            last = act.copy(q_t[:, slot, columns], bank[:])
                    elif piece == "wvo":
                        last = act.copy(wvo[:, slot, :], bank[:, 0:D])
                    elif piece == "kk":
                        wait_for(act, k_rms_done, h)
                        last = act.activation(k_means[:], bank[:, 0:rows], ACT.Copy, bias=RMS_EPS, scale=1.0 / P)
                    elif piece == "qq":
                        wait_for(act, q_scale_done, h)
                        last = act.activation(q_means[:], bank[:, 0:TT], ACT.Copy, bias=RMS_EPS * P)
                    elif piece == "row":
                        wait_for(act, row_stored, h * 16)
                        last = act.copy(rms_row[:], bank[0:rows, 0:P])
                    else:
                        chunk = int(piece[1])
                        columns = slice(chunk * BANK, (chunk + 1) * BANK)
                        last = act.copy(k_t[:, slot, columns], bank[:])
                    last.then_inc(prep_kept, 1)

                def step(pair, k, head, after, following):
                    if exists(pair, 2):
                        for q in range(2):
                            act.wait_ge(turn_ready, pair * 2 + (q - 3))
                            wait_for(act, pv_ready, pair - 3)
                            act.copy(prob_high[:, k % 2, :, q * P:(q + 1) * P],
                                     turn_bank[q][:].rearrange("p (n t) -> p n t", n=KT)).then_inc(high_done, 1)
                    if exists(pair, 0):
                        h, _, slot = head
                        for q in range(2):
                            unit, t = (2 * k + q) % 4, 2 * (k % BATCH) + q
                            act.wait_ge(shift_done, pair * 2 + (q + 1))
                            wait_for(act, turn_ready, pair * 2 + (q - 3))
                            wait_for(act, inverse_done, pair - 7)
                            act.activation(prob[:, unit, :], masked[:, unit, :], ACT.Exp, bias=shift[:, unit:unit + 1],
                                           scale=q_scale[:, slot, t:t + 1] if qk_norm else scale,
                                           accum_out=total[:, 2 * (k % 8) + q:2 * (k % 8) + q + 1]).then_inc(exp_done, 1)
                    if exists(pair, 3):
                        act.wait_ge(pv_ready, pair - 2)
                        wait_for(act, y_ready, pair - 4)
                        of = (k - 3) % BATCH
                        if qk_norm:
                            last = act.copy(o_high[:, (k - 3) % 2, :], o_bank[:, 0:2 * P])
                        else:
                            last = act.activation(o_high[:, (k - 3) % 2, :], o_bank[:, 0:2 * P], ACT.Copy,
                                                  scale=valid[:, of:of + 1])
                        last.then_inc(o_high_done, 1)
                    for piece in after:
                        prepare(piece, following)

                act.wait_ge(set_up, 1)
                walk(act, prepare, step)

            @block.vector
            def _(dve):
                def prepare(piece, head):
                    pass

                def step(pair, k, head, after, following):
                    b = k % BATCH
                    if exists(pair, 0):
                        h, turn, slot = head
                        if qk_norm and b == 0:
                            dve.wait_ge(rms_loaded[slot], turn * 16 + 16)
                            dve.wait_ge(q_scale_done, h + 1)
                        for q in range(2):
                            unit, t = (2 * k + q) % 4, 2 * b + q
                            dve.wait_ge(scores_ready, pair * 2 + (q + 1))
                            wait_for(dve, exp_done, pair * 2 + (q - 3))
                            dve.memset(woken[:], 0.0)
                            dve.tensor_tensor_reduce(masked[:, unit, :], score_bank[q][:],
                                                     side[:, slot if qk_norm else 0, b * KEYS:(b + 1) * KEYS], 1.0, LOWEST,
                                                     ALU.mult if qk_norm else ALU.add, ALU.max,
                                                     top[:, unit:unit + 1]).then_inc(top_done, 1)
                            dve.wait_ge(top_done, pair * 2 + (q + 1))
                            if qk_norm:
                                dve.scalar_tensor_tensor(shift[:, unit:unit + 1], top[:, unit:unit + 1], -1.0,
                                                         q_scale[:, slot, t:t + 1], ALU.mult,
                                                         ALU.mult).then_inc(shift_done, 1)
                            else:
                                dve.tensor_scalar(shift[:, unit:unit + 1], top[:, unit:unit + 1], -scale, None,
                                                  ALU.mult).then_inc(shift_done, 1)
                    if exists(pair, 4):
                        old, at = k % BATCH, k % 2 * 2
                        wait_for(dve, x_added, pair * 2 - 10)
                        dve.wait_ge(exp_done, pair * 2 - 6)
                        dve.reciprocal(inverse[:, at:at + 2], total[:, (k - 4) % 8 * 2:(k - 4) % 8 * 2 + 2]
                                       ).then_inc(inverse_done, 1)
                    if exists(pair, 2):
                        for q in range(2):
                            dve.wait_ge(high_done, pair * 2 + (q - 3))
                            part = (slice(None), k % 2, slice(None), slice(q * P, (q + 1) * P))
                            dve.tensor_tensor(prob_low[part], turn_bank[q][:].rearrange("p (n t) -> p n t", n=KT),
                                              prob_high[part].bitcast(F32), ALU.subtract).then_inc(turn_kept, 1)
                    if exists(pair, 3):
                        dve.wait_ge(o_high_done, pair - 2)
                        held, of = (k - 3) % 2, (k - 3) % BATCH
                        high = o_high[:, held, :].bitcast(F32)
                        if qk_norm:
                            last = dve.tensor_tensor(o_low[:, held, :], o_bank[:, 0:2 * P], high, ALU.subtract)
                        else:
                            last = dve.scalar_tensor_tensor(o_low[:, held, :], o_bank[:, 0:2 * P], valid[:, of:of + 1], high,
                                                            ALU.mult, ALU.subtract)
                        last.then_inc(o_kept, 1)
                    if exists(pair, 4):
                        dve.wait_ge(y_ready, pair - 3)
                        dve.wait_ge(inverse_done, pair - 3)
                        for q in range(2):
                            tile = m.x[:, 2 * old + q, :]
                            dve.scalar_tensor_tensor(tile, y_bank[:, q * D:(q + 1) * D], inverse[:, at + q:at + q + 1], tile,
                                                     ALU.mult, ALU.add).then_inc(x_added, 1)

                if qk_norm:
                    dve.wait_ge(gain_loaded, 32)
                    dve.tensor_tensor(gains[:], gain[:, 0:1], gain[:, 1:2], ALU.mult).then_inc(set_up, 1)
                else:
                    dve.wait_ge(side_loaded, 16)
                    dve.tensor_scalar(side[:, 0, :], mask_u8[:], 1.0, MASKED, ALU.subtract, ALU.mult)
                    dve.tensor_reduce(valid[:], mask_u8[:].rearrange("p (b s) -> p b s", b=BATCH), AX_X,
                                      ALU.max).then_inc(set_up, 1)
                walk(dve, prepare, step)

            @block.gpsimd
            def _(pool):
                part_of = {"wvo": (n_splits - 1, (wvo_high, wvo_low, wvo))}
                if not qk_norm:
                    part_of |= {"a": (0, (a_high, a_low, a_h)), "q0": (1, (q_high, q_low, q_t)),
                                "q1": (2, (q_high, q_low, q_t))}

                def split(number, *operands):
                    pool.tensor_tensor(pool_woken[:], m.ones[:, 0:1], m.ones[:, 0:1], ALU.mult)
                    for high, low, whole in operands:
                        last = pool.tensor_copy(high, whole)
                    last.then_inc(own_high, 1)
                    pool.wait_ge(own_high, number + 1)
                    for high, low, whole in operands:
                        last = pool.tensor_tensor(low, whole, high.bitcast(F32), ALU.subtract)
                    last.then_inc(split_done, 1)

                def split_weights(h, turn, slot):
                    pool.wait_ge(w_loaded[slot], turn * 64 + 64)
                    split(h * n_splits, *((high[:, slot, :], low[:, slot, :], whole[:, slot, :]) for high, low, whole in (
                        (wq_high, wq_low, wq), (wk_high, wk_low, wk))))

                def prepare(piece, head):
                    h, turn, slot = head
                    if piece in ("k0", "k1", "k2", "k3"):
                        pool.wait_ge(prep_kept, h * n_pieces + (pieces.index(piece) + 1))
                        chunk = int(piece[1])
                        keys = k_t[:, slot, chunk * BANK:(chunk + 1) * BANK]
                        pool.tensor_tensor(k_squares[:, chunk * BANK:(chunk + 1) * BANK], keys, keys, ALU.mult).then_inc(squared, 1)
                    elif piece == "kk":
                        pool.wait_ge(prep_kept, h * n_pieces + (pieces.index("kk") + 1))
                        wait_for(pool, prep_ready, h * n_pieces + (pieces.index("row") + 1 - n_pieces))
                        pool.tensor_tensor(k_rms[:], k_means[:], m.minus_half[:, 0:rows], ALU.pow).then_inc(k_rms_done, 1)
                    elif piece == "qq":
                        pool.wait_ge(prep_kept, h * n_pieces + (pieces.index("qq") + 1))
                        wait_for(pool, exp_done, h * (2 * BATCH) - 2 * BATCH)
                        pool.tensor_tensor(q_scale[:, slot, :], q_means[:], m.minus_half[:, 0:TT],
                                           ALU.pow).then_inc(q_scale_done, 1)
                    elif piece in part_of:
                        n, (high, low, whole) = part_of[piece]
                        first, end = (0, D) if piece in ("a", "wvo") else (int(piece[1]) * BANK, (int(piece[1]) + 1) * BANK)
                        pool.wait_ge(prep_kept, h * n_pieces + (pieces.index(piece) + 1))
                        split(h * n_splits + n,
                              (high[:, slot, first:end], low[:, slot, first:end], whole[:, slot, first:end]))
                        if qk_norm and not (isinstance(h, int) and h == HEADS - 1):
                            split_weights(h + 1, turn + slot, 1 - slot)
                def step(pair, k, head, after, following):
                    for piece in after:
                        prepare(piece, following)

                if qk_norm:
                    split_weights(0, 0, 0)
                walk(pool, prepare, step)


H0 = 16
GROUP = 2
GROUPS = HEADS // GROUP
V0 = 32
SHARES = 4
LAST_KEYS = 16


def small_project_stage(nc, m, dram):
    steps = (TT + BATCH * KT) // 2
    query_steps = TT // 2
    eps = 1e-6
    rows = 2 * HEADS
    common, n_loads = P - LAST_KEYS, 17
    with Stage(nc, m, "l0p") as st:
        wq = st.sbuf("wq", [P, DC, D])
        wkv = st.sbuf("wkv", [CW, 2 * D])
        wkv_last = st.sbuf("wkv_last", [CW, 2 * D])
        bq = st.sbuf("bq", [P, D])
        bkv = st.sbuf("bkv", [P, 2, 2 * D])
        sums = st.sbuf("sums", [P, 2 * HEADS])
        gain = st.sbuf("gain", [P, 5, H0])
        offset = st.sbuf("offset", [P, 5, H0])
        ctx_t = st.sbuf("ctx_t", [CW, BATCH * KEYS])
        ctx_common = st.sbuf("ctx_common", [CW, BATCH, P])
        ctx_last = st.sbuf("ctx_last", [CW, BATCH, P])
        head = st.sbuf("head", [P, 4, rows, H0])
        squares = st.sbuf("squares", [P, 2, rows, H0])
        variance = st.sbuf("variance", [P, 2, rows])
        spread = st.sbuf("spread", [P, 2, rows])
        rstd = st.sbuf("rstd", [P, 2, rows])
        exponent = st.sbuf("exponent", [P, rows])
        parts = st.sbuf("parts", [P, 2, rows, SHARES, H0], F32R)
        project_bank = st.banks("project", 4)
        turn_bank = st.banks("turn", 4)
        (loaded, ctx_loaded, own, centred_done, set_up, cleared, shares_set, projected, head_done, v_done, squares_done,
         variance_done, spread_done, rstd_done, scaled, gained, normed, high_done, low_done, turned, kept) = st.sems(
            "loaded", "ctx_loaded", "own", "centred_done", "set_up", "cleared", "shares_set", "projected", "head_done",
            "v_done", "squares_done", "variance_done", "spread_done", "rstd_done", "scaled", "gained", "normed",
            "high_done", "low_done", "turned", "kept")

        def per_row(a):
            return a.rearrange("p (h a) -> p h a", a=1).broadcast_to([P, a.shape[-1], H0])

        with st.block() as block:

            @block.sync
            def _(sp):
                sp.dma_start(wq[:], dram["wq"].rearrange("(c p) n -> p c n", p=P)).then_inc(loaded, 16)
                sp.dma_start(wkv[:], dram["wkv"]).then_inc(loaded, 16)
                sp.dma_start(wkv_last[:], dram["wkv_last"]).then_inc(loaded, 16)
                sp.dma_start(bq[:], dram["bq"].partition_broadcast(P)).then_inc(loaded, 16)
                sp.dma_start(bkv[:, 0, :], dram["bkv"].partition_broadcast(P)).then_inc(loaded, 16)
                sp.dma_start(bkv[0:common, 1, :], dram["bkv"].partition_broadcast(common)).then_inc(loaded, 16)
                sp.dma_start(bkv[common:P, 1, :], dram["bkv_last"].partition_broadcast(LAST_KEYS)).then_inc(loaded, 16)

            @block.scalar
            def _(act):
                act.dma_start(ctx_t[:], dram["ctx_t"]).then_inc(ctx_loaded, 16)
                for to, q, k, last in ((gain, "qn_w", "kn_w", "kn_dca_w"), (offset, "qn_b", "kn_b", "kn_dca_b")):
                    for n, w in enumerate((q, q, k, k)):
                        act.dma_start(to[:, n, :], dram[w].partition_broadcast(P)).then_inc(loaded, 16)
                    act.dma_start(to[0:common, 4, :], dram[k].partition_broadcast(common)).then_inc(loaded, 16)
                    act.dma_start(to[common:P, 4, :], dram[last].partition_broadcast(LAST_KEYS)).then_inc(loaded, 16)

                def split(s):
                    high = parts[:, s % 2, :, 0:2, :] if s < query_steps else parts[:, s % 2, :, 0:4:2, :]
                    act.wait_ge(normed, s + 1)
                    wait_for(act, turned, s - 1)
                    act.copy(high, head[:, s % 4, :, :].rearrange("p h (a d) -> p h a d", a=1).broadcast_to(
                        [P, rows, 2, H0])).then_inc(high_done, 1)

                def keep(s):
                    act.wait_ge(turned, s + 1)
                    for j in range(2):
                        to, per_batch, at = ((m.q0_t, TT // BATCH, 2 * s + j) if s < query_steps else
                                             (m.k0_t, KT, 2 * s + j - TT))
                        b, n = divmod(at, per_batch)
                        for half in range(2):
                            first = b * GROUPS + half * (GROUPS // 2)
                            last = act.copy(to[:, first:first + GROUPS // 2, n * P:(n + 1) * P],
                                            turn_bank[2 * j + half][:].rearrange("p (g q) -> p g q", g=GROUPS // 2))
                    last.then_inc(kept, 1)

                for s in range(steps + 2):
                    if s < steps:
                        act.wait_ge(head_done, s + 1)
                        wait_for(act, variance_done, s - 1)
                        act.activation(squares[:, s % 2, :, :], head[:, s % 4, :, :], ACT.Square).then_inc(squares_done, 1)
                    if s >= 3:
                        keep(s - 3)
                    if s >= 2:
                        split(s - 2)
                keep(steps - 1)

            @block.gpsimd
            def _(pool):
                pool.memset(exponent[:], -0.5).then_inc(cleared, 1)
                pool.memset(ctx_common[:], 0.0).then_inc(cleared, 1)
                pool.memset(ctx_last[:], 0.0).then_inc(cleared, 1)
                pool.wait_ge(cleared, 3)
                pool.wait_ge(ctx_loaded, 16)
                last_tiles = ctx_t[:].rearrange("c (b n q) -> c b n q", b=BATCH, n=KT)[:, :, KT - 1, :]
                pool.tensor_copy(ctx_common[:, :, 0:common], last_tiles[:, :, 0:common]).then_inc(shares_set, 1)
                pool.tensor_copy(ctx_last[:, :, common:P], last_tiles[:, :, common:P]).then_inc(shares_set, 1)
                for s in range(steps):
                    pool.wait_ge(spread_done, s + 1)
                    wait_for(pool, scaled, s - 1)
                    pool.tensor_tensor(rstd[:, s % 2, :], spread[:, s % 2, :], exponent[:], ALU.pow).then_inc(rstd_done, 1)

            @block.tensor
            def _(pe):
                pe.wait_ge(centred_done, 1)
                pe.wait_ge(shares_set, 2)

                def project(s):
                    wait_for(pe, head_done, s - 1)
                    if s - 2 >= query_steps:
                        pe.wait_ge(v_done, s - 1 - query_steps)
                    for j in range(2):
                        i, bank = 2 * s + j, project_bank[s % 2 * 2 + j]
                        if i < TT:
                            for c in range(DC):
                                last = pe.matmul(bank[:, 0:D], m.x_t[:, c, i * P:(i + 1) * P], wq[:, c, :],
                                                 start=(c == 0), stop=(c == DC - 1))
                        elif (i - TT) % KT == KT - 1:
                            b = (i - TT) // KT
                            pe.matmul(bank[:], ctx_common[:, b, :], wkv[:], start=True, stop=False)
                            last = pe.matmul(bank[:], ctx_last[:, b, :], wkv_last[:], start=False, stop=True)
                        else:
                            last = pe.matmul(bank[:], ctx_t[:, (i - TT) * P:(i - TT + 1) * P], wkv[:], start=True, stop=True)
                    last.then_inc(projected, 1)

                def turn(s):
                    pe.wait_ge(low_done, s + 1)
                    wait_for(pe, kept, s)
                    heads = 2 * GROUPS // 4 * GROUP
                    for n in range(4):
                        for g in range(GROUPS // 2):
                            first = n * heads + g * GROUP
                            last = pe.transpose(turn_bank[n][:, g * P:(g + 1) * P],
                                                parts[:, s % 2, first:first + GROUP, :, :].bitcast(F32).rearrange(
                                                    "p h a d -> p (h a d)"), m.ident[:])
                    last.then_inc(turned, 1)

                project(0)
                for s in range(steps + 2):
                    if s + 1 < steps:
                        project(s + 1)
                    if s >= 2:
                        turn(s - 2)

            @block.vector
            def _(dve):
                links = 0

                def link(instruction):
                    nonlocal links
                    links += 1
                    instruction.then_inc(own, 1)
                    dve.wait_ge(own, links)

                dve.wait_ge(loaded, 16 * (n_loads + 2))
                for w in [wq[:].rearrange("p c (h d) -> p (c h) d", d=H0), bq[:].rearrange("p (h d) -> p h d", d=H0)] + [
                        w.rearrange("p (h a d) -> p h a d", h=HEADS, a=2)[:, :, 0, :]
                        for w in (wkv[:], wkv_last[:], bkv[:, 0, :], bkv[:, 1, :])]:
                    n = w.shape[1]
                    link(dve.tensor_reduce(sums[:, 0:n], w, AX_X, ALU.add))
                    last = dve.scalar_tensor_tensor(w, per_row(sums[:, 0:n]), -1.0 / H0, w, ALU.mult, ALU.add)
                    link(last)
                dve.memset(sums[:], 0.0).then_inc(centred_done, 1)

                def biased(s):
                    for j in range(2):
                        i, bank = 2 * s + j, project_bank[s % 2 * 2 + j]
                        to = head[:, s % 4, j * HEADS:(j + 1) * HEADS, :]
                        if i < TT:
                            last = dve.tensor_tensor(to, bank[:, 0:D].rearrange("p (h d) -> p h d", h=HEADS),
                                                     bq[:].rearrange("p (h d) -> p h d", h=HEADS), ALU.add)
                        else:
                            kinds = [a.rearrange("p (h a d) -> p h a d", h=HEADS, a=2)
                                     for a in (bank[:], bkv[:, int((i - TT) % KT == KT - 1), :])]
                            last = dve.tensor_tensor(to, kinds[0][:, :, 0, :], kinds[1][:, :, 0, :], ALU.add)
                    last.then_inc(head_done, 1)
                    if s >= query_steps:
                        for j in range(2):
                            i, bank = 2 * s + j, project_bank[s % 2 * 2 + j]
                            b, n = divmod(i - TT, KT)
                            kinds = [a.rearrange("p (g h a d) -> p g h a d", g=GROUPS, h=GROUP, a=2)[:, :, :, 1, :]
                                     for a in (bank[:], bkv[:, int(n == KT - 1), :])]
                            last = dve.tensor_tensor(m.v0[:, b * GROUPS:(b + 1) * GROUPS, n, :].rearrange(
                                "p g (h d) -> p g h d", h=GROUP), kinds[0], kinds[1], ALU.add)
                        last.then_inc(v_done, 1)

                def added(s):
                    dve.wait_ge(squares_done, s + 1)
                    dve.tensor_reduce(variance[:, s % 2, :], squares[:, s % 2, :, :], AX_X, ALU.add).then_inc(variance_done, 1)
                    dve.wait_ge(variance_done, s + 1)
                    wait_for(dve, rstd_done, s - 1)
                    dve.tensor_scalar(spread[:, s % 2, :], variance[:, s % 2, :], 1.0 / H0, eps, ALU.mult,
                                      ALU.add).then_inc(spread_done, 1)

                def scale(s):
                    dve.wait_ge(rstd_done, s + 1)
                    h = head[:, s % 4, :, :]
                    dve.tensor_tensor(h, h, per_row(rstd[:, s % 2, :]), ALU.mult).then_inc(scaled, 1)
                    kind = 0 if s < query_steps else 2 + s % 2
                    rows_of = h.rearrange("p (t h) d -> p t h d", t=2)

                    def of_tiles(a):
                        return a[:, kind:kind + 2, :].rearrange("p t (a d) -> p t a d", a=1).broadcast_to([P, 2, HEADS, H0])

                    dve.wait_ge(scaled, s + 1)
                    dve.tensor_tensor(rows_of, rows_of, of_tiles(gain), ALU.mult).then_inc(gained, 1)
                    dve.wait_ge(gained, s + 1)
                    dve.tensor_tensor(rows_of, rows_of, of_tiles(offset), ALU.add).then_inc(normed, 1)

                def split(s):
                    dve.wait_ge(high_done, s + 1)
                    of = parts[:, s % 2, :, :, :]
                    high, low = (of[:, :, 0:2, :], of[:, :, 2:4, :]) if s < query_steps else (of[:, :, 0:4:2, :], of[:, :, 1:4:2, :])
                    dve.tensor_tensor(low, head[:, s % 4, :, :].rearrange("p h (a d) -> p h a d", a=1).broadcast_to(
                        [P, rows, 2, H0]), high.bitcast(F32), ALU.subtract).then_inc(low_done, 1)

                for s in range(steps + 2):
                    if s < steps:
                        dve.wait_ge(projected, s + 1)
                        wait_for(dve, low_done, s - 3)
                        biased(s)
                    if s < steps:
                        added(s)
                    if 1 <= s <= steps:
                        scale(s - 1)
                    if s >= 2:
                        split(s - 2)


def small_attention_stage(nc, m):
    scale = float(H0) ** -0.5
    cut = KEYS - LAST_KEYS
    parts = ((0, cut), (cut, KEYS))
    lag, slots = 4, 4
    turns = BATCH * GROUPS // slots
    width = SHARES * H0
    with Stage(nc, m, "l0a") as st:
        q_t = st.sbuf("q_t", [P, slots, 2 * P], F32R)
        k_t = st.sbuf("k_t", [P, slots, KEYS], F32R)
        v = st.sbuf("v", [P, slots, KT, GROUP, V0])
        top = st.sbuf("top", [P, 2, 2, 2])
        shift = st.sbuf("shift", [P, 2, 2, 2])
        total = st.sbuf("total", [P, 2, 2, 2])
        inverse = st.sbuf("inverse", [P, 2, 2, 2])
        prob = st.sbuf("prob", [P, 4, 2, KEYS])
        prob_t = st.sbuf("prob_t", [P, 2, KT, 2 * P])
        score_bank = st.banks("score", 4)
        turn_bank = st.banks("turn", 2)
        o_bank = st.banks("o", 2)
        (staged, scores_ready, top_done, shift_done, exp_done, inverse_done, prob_done, last_done, turn_ready, pv_ready,
         o_kept, cleared) = st.sems("staged", "scores_ready", "top_done", "shift_done", "exp_done", "inverse_done", "prob_done",
                           "last_done", "turn_ready", "pv_ready", "o_kept", "cleared")
        turn_kept = st.sem("turn_kept")

        def walk(engine, step):
            def four_groups(i, last=False):
                for k in range(slots * GROUP):
                    slot = k // GROUP
                    following = None if last and slot == slots - 1 else (i + (slot + 1) // slots, (slot + 1) % slots)
                    step(i * (slots * GROUP) + k, k, i, following)

            four_groups(0)
            with engine.Fori(1, turns - 1) as i:
                four_groups(i)
            four_groups(turns - 1, True)
            for k in range(lag):
                step(PAIRS + k, k, turns, None)

        def exists(pair, back):
            return not isinstance(pair, int) or 0 <= pair - back < PAIRS

        with st.block() as block:

            @block.gpsimd
            def _(pool):
                def stage(turn, slot):
                    group = turn * slots + slot
                    wait_for(pool, pv_ready, turn * (slots * GROUP) + (slot - slots + 1) * GROUP)
                    pool.tensor_copy(q_t[:, slot, :], m.q0_t[:, group, :]).then_inc(staged, 1)
                    pool.tensor_copy(k_t[:, slot, :], m.k0_t[:, group, :]).then_inc(staged, 1)
                    pool.tensor_copy(v[:, slot, :, :, 0:H0], m.v0[:, group, :, :].rearrange(
                        "p n (j d) -> p n j d", j=GROUP)).then_inc(staged, 1)

                def step(pair, k, turn, following):
                    if exists(pair, 1):
                        at = (k - 1) % 2
                        pool.wait_ge(inverse_done, pair)
                        last_keys = prob[:, (k - 1) % 4, :, cut:]
                        pool.tensor_tensor(last_keys, last_keys, inverse[:, at, :, 1:2].broadcast_to([P, 2, LAST_KEYS]),
                                           ALU.mult).then_inc(last_done, 1)
                    if exists(pair, 0) and k % GROUP == 0 and following is not None:
                        stage(*following)

                pool.memset(v[:], 0.0).then_inc(cleared, 1)
                pool.wait_ge(cleared, 1)
                stage(0, 0)
                walk(pool, step)

            @block.tensor
            def _(pe):
                def step(pair, k, turn, following):
                    if exists(pair, 0):
                        slot, j = k // GROUP, k % GROUP
                        if j == 0:
                            pe.wait_ge(staged, turn * (3 * slots) + (3 * slot + 3))
                        rows = slice(width * j, width * (j + 1))
                        for q in range(2):
                            wait_for(pe, exp_done, pair * 2 + (q - 3))
                            pe.matmul(score_bank[k % 2 * 2 + q][:], q_t[rows, slot, q * P:(q + 1) * P], k_t[rows, slot, :],
                                      start=True, stop=True).then_inc(scores_ready, 1)
                    if exists(pair, 4):
                        old = (k - 4) % (slots * GROUP)
                        slot, j = old // GROUP, old % GROUP
                        quad = slot // 2
                        if old % 4 == 0:
                            wait_for(pe, o_kept, turn * (slots // 2) + ((k - 4) // 4 - 1))
                        pe.wait_ge(turn_kept, pair * 2 - 6)
                        to = old % 4 * V0
                        for n in range(KT):
                            last = pe.matmul(o_bank[quad][to:to + V0, 0:2 * P], v[:, slot, n, j, :], prob_t[:, k % 2, n, :],
                                             start=(n == 0), stop=(n == KT - 1), tile_position=(0, to))
                        last.then_inc(pv_ready, 1)
                    if exists(pair, 2):
                        pe.wait_ge(last_done, pair - 1)
                        for q in range(2):
                            pe.wait_ge(prob_done, pair * 2 + (q - 3))
                            wait_for(pe, turn_kept, pair * 2 + (q - 5))
                            for n in range(KT):
                                last = pe.transpose(turn_bank[q][:, n * P:(n + 1) * P],
                                                    prob[:, (k - 2) % 4, q, n * P:(n + 1) * P], m.ident[:])
                            last.then_inc(turn_ready, 1)

                walk(pe, step)

            @block.scalar
            def _(act):
                def step(pair, k, turn, following):
                    if exists(pair, 3):
                        for q in range(2):
                            act.wait_ge(turn_ready, pair * 2 + (q - 5))
                            wait_for(act, pv_ready, pair - 4)
                            act.copy(prob_t[:, (k - 3) % 2, :, q * P:(q + 1) * P],
                                     turn_bank[q][:].rearrange("p (n t) -> p n t", n=KT)).then_inc(turn_kept, 1)
                    if exists(pair, 0):
                        at = k % 2
                        for q in range(2):
                            act.wait_ge(shift_done, pair + 1)
                            wait_for(act, turn_ready, pair * 2 + (q - 7))
                            wait_for(act, prob_done, pair * 2 - 2)
                            for part, (first, end) in enumerate(parts):
                                last = act.activation(prob[:, k % 4, q, first:end], score_bank[at * 2 + q][:, first:end], ACT.Exp,
                                                      bias=shift[:, at, q, part:part + 1], scale=scale,
                                                      accum_out=total[:, at, q, part:part + 1])
                            last.then_inc(exp_done, 1)
                    if exists(pair, 4) and (k - 4) % 4 == 3:
                        back = (k - 4) // 4
                        act.wait_ge(pv_ready, pair - 3)
                        act.copy(m.o0[:, turn * (slots // 2) + back, :], o_bank[back % 2][:, 0:2 * P]).then_inc(o_kept, 1)

                walk(act, step)

            @block.vector
            def _(dve):
                def step(pair, k, turn, following):
                    if exists(pair, 0):
                        at = k % 2
                        for q in range(2):
                            dve.wait_ge(scores_ready, pair * 2 + (q + 1))
                            for part, (first, end) in enumerate(parts):
                                last = dve.tensor_reduce(top[:, at, q, part:part + 1], score_bank[at * 2 + q][:, first:end],
                                                         AX_X, ALU.max)
                        last.then_inc(top_done, 1)
                        wait_for(dve, exp_done, pair * 2 - 2)
                        dve.wait_ge(top_done, pair + 1)
                        dve.tensor_scalar(shift[:, at, :, :], top[:, at, :, :], -scale, None, ALU.mult).then_inc(shift_done, 1)
                    if exists(pair, 1):
                        at = (k - 1) % 2
                        wait_for(dve, last_done, pair - 2)
                        dve.wait_ge(exp_done, pair * 2)
                        dve.reciprocal(inverse[:, at, :, :], total[:, at, :, :]).then_inc(inverse_done, 1)
                        dve.wait_ge(inverse_done, pair)
                        for q in range(2):
                            common = prob[:, (k - 1) % 4, q, 0:cut]
                            dve.tensor_scalar(common, common, inverse[:, at, q, 0:1], None, ALU.mult).then_inc(prob_done, 1)

                walk(dve, step)


def small_output_stage(nc, m, dram):
    quads = HEADS // 4
    with Stage(nc, m, "l0o") as st:
        wo = st.sbuf("wo", [P, quads, D])
        bo = st.sbuf("bo", [P, D])
        y_bank = st.banks("y", 2)
        wo_loaded, bo_loaded, y_ready, x_added, biased = st.sems("wo_loaded", "bo_loaded", "y_ready", "x_added", "biased")

        with st.block() as block:

            @block.sync
            def _(sp):
                sp.dma_start(wo[:], dram["wo"].rearrange("c p n -> p c n")).then_inc(wo_loaded, 16)
                sp.dma_start(bo[:], dram["bo"].partition_broadcast(P)).then_inc(bo_loaded, 16)

            @block.tensor
            def _(pe):
                pe.wait_ge(wo_loaded, 16)
                for t in range(TT):
                    b, q = divmod(t, TT // BATCH)
                    wait_for(pe, x_added, t - 1)
                    for c in range(quads):
                        last = pe.matmul(y_bank[t % 2][:, 0:D], m.o0[:, b * quads + c, q * P:(q + 1) * P], wo[:, c, :],
                                         start=(c == 0), stop=(c == quads - 1))
                    last.then_inc(y_ready, 1)

            @block.gpsimd
            def _(pool):
                pool.wait_ge(bo_loaded, 16)
                for t in range(TT):
                    pool.tensor_tensor(m.x[:, t, :], m.x[:, t, :], bo[:], ALU.add).then_inc(biased, 1)

            @block.vector
            def _(dve):
                for t in range(TT):
                    dve.wait_ge(biased, t + 1)
                    dve.wait_ge(y_ready, t + 1)
                    dve.tensor_tensor(m.x[:, t, :], m.x[:, t, :], y_bank[t % 2][:, 0:D], ALU.add).then_inc(x_added, 1)


def small_attention(nc, m, dram):
    with ExitStack() as stack:
        m.small_heads(stack)
        small_project_stage(nc, m, dram)
        small_attention_stage(nc, m)
        small_output_stage(nc, m, dram)


HIDDEN0 = 1024


def sparse_ffn_stage(nc, m, dram):
    halves = HIDDEN0 // BANK
    chunks = HIDDEN0 // P
    fours = HIDDEN0 // 4
    lag = 1
    with Stage(nc, m, "l0f") as st:
        wg = st.sbuf("wg", [P, DC, HIDDEN0])
        wu = st.sbuf("wu", [P, DC, HIDDEN0])
        wd = st.sbuf("wd", [P, chunks, D])
        x_t = st.sbuf("x_t", [P, 2, DC, P])
        gate = st.sbuf("gate", [P, 2, HIDDEN0])
        h = st.sbuf("h", [P, 2, HIDDEN0])
        size = st.sbuf("size", [P, HIDDEN0])
        beats_near = st.sbuf("beats_near", [P, fours, 2], BF16)
        beats_far = st.sbuf("beats_far", [P, fours, 2], BF16)
        beats_across = st.sbuf("beats_across", [P, fours, 2], BF16)
        front = st.sbuf("front", [P, fours, 2], BF16)
        back = st.sbuf("back", [P, fours, 2], BF16)
        wins = st.sbuf("wins", [P, fours, 4], BF16)
        kept = st.sbuf("kept", [P, 2, HIDDEN0])
        h_t = st.sbuf("h_t", [P, 2, chunks, P])
        gate_bank = st.banks("gate", halves)
        up_bank = st.banks("up", halves)
        turn_bank = st.banks("turn", 2)
        y_bank = st.banks("y", 2)
        (loaded, staged, gate_ready, up_ready, gate_done, h_done, size_done, near_done, far_done, across_done, front_done, back_done,
         wins_done, kept_done, turned, turn_kept, y_ready, x_added) = st.sems(
            "loaded", "staged", "gate_ready", "up_ready", "gate_done", "h_done", "size_done", "near_done", "far_done", "across_done",
            "front_done", "back_done", "wins_done", "kept_done", "turned", "turn_kept", "y_ready", "x_added")

        def walk(engine, step):
            for k in range(2):
                step(k, k)
            with engine.Fori(1, TT // 2) as i:
                for k in range(2):
                    step(i * 2 + k, k)
            for k in range(lag):
                step(TT + k, k)

        def exists(t, behind):
            return not isinstance(t, int) or 0 <= t - behind < TT

        with st.block() as block:

            @block.sync
            def _(sp):
                sp.dma_start(wg[:], dram["w_gate"].rearrange("(c p) n -> p c n", p=P)).then_inc(loaded, 16)
                sp.dma_start(wu[:], dram["w_up"].rearrange("(c p) n -> p c n", p=P)).then_inc(loaded, 16)
                sp.dma_start(wd[:], dram["w_down"].rearrange("(c p) n -> p c n", p=P)).then_inc(loaded, 16)

            @block.gpsimd
            def _(pool):
                def step(t, k):
                    if exists(t, 0):
                        wait_for(pool, up_ready, t * halves - halves)
                        pool.tensor_copy(x_t[:, k, :, :], m.x_t[:, :, bass.ds(t * P, P)]).then_inc(staged, 1)

                walk(pool, step)

            @block.tensor
            def _(pe):
                def step(t, k):
                    if exists(t, 0):
                        pe.wait_ge(staged, t + 1)
                        for n in range(halves):
                            columns = slice(n * BANK, (n + 1) * BANK)
                            for bank, w, ready, used in ((gate_bank[n], wg, gate_ready, gate_done),
                                                         (up_bank[n], wu, up_ready, h_done)):
                                wait_for(pe, used, t * halves + (n + 1 - halves))
                                for c in range(DC):
                                    last = pe.matmul(bank[:], x_t[:, k, c, :], w[:, c, columns],
                                                     start=(c == 0), stop=(c == DC - 1))
                                last.then_inc(ready, 1)
                    if exists(t, 1):
                        old = 1 - k
                        for half in range(2):
                            pe.wait_ge(kept_done, t)
                            wait_for(pe, turn_kept, t * 2 + (half - 3))
                            for n in range(chunks // 2):
                                c = half * (chunks // 2) + n
                                last = pe.transpose(turn_bank[half][:, n * P:(n + 1) * P], kept[:, old, c * P:(c + 1) * P],
                                                    m.ident[:])
                            last.then_inc(turned, 1)
                        pe.wait_ge(turn_kept, t * 2)
                        wait_for(pe, x_added, t - 2)
                        for c in range(chunks):
                            last = pe.matmul(y_bank[old][:, 0:D], h_t[:, old, c, :], wd[:, c, :],
                                             start=(c == 0), stop=(c == chunks - 1))
                        last.then_inc(y_ready, 1)

                pe.wait_ge(loaded, 48)
                walk(pe, step)

            @block.scalar
            def _(act):
                def step(t, k):
                    if exists(t, 0):
                        for n in range(halves):
                            act.wait_ge(gate_ready, t * halves + (n + 1))
                            wait_for(act, h_done, t * halves + (n + 1 - 2 * halves))
                            act.activation(gate[:, k, n * BANK:(n + 1) * BANK], gate_bank[n][:], ACT.Silu).then_inc(gate_done, 1)
                        act.wait_ge(h_done, t * halves + halves)
                        wait_for(act, across_done, t * 2)
                        act.activation(size[:], h[:, k, :], ACT.Abs).then_inc(size_done, 1)
                    if exists(t, 1):
                        old = 1 - k
                        for half in range(2):
                            act.wait_ge(turned, t * 2 + (half - 1))
                            wait_for(act, y_ready, t - 2)
                            act.copy(h_t[:, old, half * (chunks // 2):(half + 1) * (chunks // 2), :],
                                     turn_bank[half][:].rearrange("p (n t) -> p n t", n=chunks // 2)).then_inc(turn_kept, 1)

                walk(act, step)

            @block.vector
            def _(dve):
                s4 = size[:].rearrange("p (f e) -> p f e", e=4)

                def step(t, k):
                    if exists(t, 0):
                        for n in range(halves):
                            columns = slice(n * BANK, (n + 1) * BANK)
                            dve.wait_ge(gate_done, t * halves + (n + 1))
                            dve.wait_ge(up_ready, t * halves + (n + 1))
                            wait_for(dve, kept_done, t - 1)
                            dve.tensor_tensor(h[:, k, columns], gate[:, k, columns], up_bank[n][:], ALU.mult).then_inc(h_done, 1)
                        h4 = h[:, k, :].rearrange("p (f e) -> p f e", e=4)
                        k4 = kept[:, k, :].rearrange("p (f e) -> p f e", e=4)
                        dve.wait_ge(size_done, t + 1)
                        wait_for(dve, kept_done, t)
                        dve.tensor_tensor(beats_near[:], s4[:, :, 0:4:2], s4[:, :, 1:4:2], ALU.is_ge).then_inc(near_done, 1)
                        dve.tensor_tensor(beats_far[:], s4[:, :, 0:2], s4[:, :, 2:4], ALU.is_ge).then_inc(far_done, 1)
                        for e in range(2):
                            dve.tensor_tensor(beats_across[:, :, e], s4[:, :, e], s4[:, :, 3 - e], ALU.is_ge).then_inc(across_done, 1)
                        dve.wait_ge(near_done, t + 1)
                        dve.wait_ge(far_done, t + 1)
                        dve.wait_ge(across_done, t * 2 + 2)
                        dve.tensor_tensor(front[:], beats_far[:], beats_across[:], ALU.add).then_inc(front_done, 1)
                        for e in range(2):
                            dve.tensor_tensor(back[:, :, e], beats_far[:, :, e], beats_across[:, :, 1 - e], ALU.add).then_inc(back_done, 1)
                        dve.wait_ge(front_done, t + 1)
                        dve.wait_ge(back_done, t * 2 + 2)
                        dve.tensor_tensor(wins[:, :, 0], front[:, :, 0], beats_near[:, :, 0], ALU.add).then_inc(wins_done, 1)
                        dve.tensor_tensor(wins[:, :, 1], front[:, :, 1], beats_near[:, :, 0], ALU.subtract).then_inc(wins_done, 1)
                        dve.tensor_tensor(wins[:, :, 2], beats_near[:, :, 1], back[:, :, 0], ALU.subtract).then_inc(wins_done, 1)
                        dve.tensor_tensor(wins[:, :, 3], beats_near[:, :, 1], back[:, :, 1], ALU.add).then_inc(wins_done, 1)
                        dve.wait_ge(wins_done, t * 4 + 4)
                        dve.wait_ge(h_done, t * halves + halves)
                        wait_for(dve, turned, t * 2 - 2)
                        for e, (least, test) in enumerate(((2.0, ALU.is_ge), (1.0, ALU.is_ge), (0.0, ALU.is_ge), (1.0, ALU.is_le))):
                            last = dve.scalar_tensor_tensor(k4[:, :, e], wins[:, :, e], least, h4[:, :, e], test, ALU.mult)
                        last.then_inc(kept_done, 1)
                    if exists(t, 1):
                        dve.wait_ge(y_ready, t)
                        dve.tensor_tensor(m.x[:, t - 1, :], m.x[:, t - 1, :], y_bank[1 - k][:, 0:D], ALU.add).then_inc(x_added, 1)

                walk(dve, step)


STEPS1 = 4
HIDDEN1 = 1024


def thought_stage(nc, m, dram):
    eps = 1e-6
    chunks = HIDDEN1 // P
    B = BATCH
    IN_GAMMA, IN_BETA, AGG_B, PN_GAMMA, PN_BETA, D2_B, BC_B = range(7)
    small_names = ("in_gamma", "in_beta", "agg_b", "pn_gamma", "pn_beta", "d2_b", "bc_b")
    GATE_B, OUT_GAMMA, OUT_BETA = range(3)
    wide_names = ("gate_b", "out_gamma", "out_beta")
    with Stage(nc, m, "l1f") as st:
        weights = {"agg_w": st.sbuf("agg_w", [P, DC, D]), "d1_w": st.sbuf("d1_w", [P, DC, HIDDEN1]),
                   "d2_w": st.sbuf("d2_w", [P, chunks, D]), "bc_w": st.sbuf("bc_w", [P, DC, D]),
                   "gate_w": st.sbuf("gate_w", [P, DC, D])}
        d1_b = st.sbuf("d1_b", [P, chunks])
        small = st.sbuf("small", [B, len(small_names), D])
        wide = st.sbuf("wide", [P, len(wide_names), D])
        pick = st.sbuf("pick", [B, B, P])
        last_x = st.sbuf("last_x", [B, D])
        thought = st.sbuf("thought", [B, D])
        stats = st.sbuf("stats", [B, 6])
        moments = st.sbuf("moments", [B, 2])
        spread = st.sbuf("spread", [B, 1])
        rstd = st.sbuf("rstd", [B, 1])
        rows = st.sbuf("rows", [B, D])
        rows_t = st.sbuf("rows_t", [P, DC, B])
        hidden = st.sbuf("hidden", [P, chunks, B])
        active = st.sbuf("active", [P, chunks, B])
        delta = st.sbuf("delta", [B, D])
        said = st.sbuf("said", [P, B, D])
        raw = st.sbuf("raw", [P, TT, D])
        gate = st.sbuf("gate", [P, TT, D])
        out = st.sbuf("out", [P, TT, D])
        out_stats = st.sbuf("out_stats", [P, TT, 6])
        out_moments = st.sbuf("out_moments", [P, TT, 2])
        out_spread = st.sbuf("out_spread", [P, TT])
        out_rstd = st.sbuf("out_rstd", [P, TT])
        turn_bank, = st.banks("turn", 1)
        hidden_bank, = st.banks("hidden", 1)
        row_bank, = st.banks("row", 1)
        said_bank = st.banks("said", 2)
        gate_bank = st.banks("gate", 2)
        n_loads = len(weights) + len(small_names) + len(wide_names) + 2
        (loaded, last_loaded, own, spread_done, rstd_done, rows_set, turned, turn_kept, product_ready, product_read,
         hidden_ready, hidden_set, active_done, said_ready, said_kept, gate_ready, raw_done, gate_done, gated, added, offset_done,
         out_spread_done, out_rstd_done, scaled, gained) = st.sems(
            "loaded", "last_loaded", "own", "spread_done", "rstd_done", "rows_set", "turned", "turn_kept", "product_ready",
            "product_read", "hidden_ready", "hidden_set", "active_done", "said_ready", "said_kept", "gate_ready",
            "raw_done", "gate_done", "gated", "added", "offset_done", "out_spread_done", "out_rstd_done", "scaled", "gained")

        with st.block() as block:

            @block.sync
            def _(sp):
                sp.dma_start(last_x[:], m.x_n[P - 1:P, 1:TT:2, :]).then_inc(last_loaded, 16)
                for name, to in weights.items():
                    sp.dma_start(to[:], dram[name].rearrange("(c p) n -> p c n", p=P)).then_inc(loaded, 16)
                for n, name in enumerate(wide_names):
                    sp.dma_start(wide[:, n, :], dram[name].partition_broadcast(P)).then_inc(loaded, 16)
                for n, name in enumerate(small_names):
                    sp.dma_start(small[:, n, :], dram[name].partition_broadcast(B)).then_inc(loaded, 16)
                sp.dma_start(d1_b[:], dram["d1_b"]).then_inc(loaded, 16)
                sp.dma_start(pick[:], dram["pick"]).then_inc(loaded, 16)

            @block.gpsimd
            def _(pool):
                for n in range(1 + STEPS1):
                    pool.wait_ge(spread_done, n + 1)
                    pool.tensor_tensor(rstd[:], spread[:], m.minus_half[0:B, 0:1], ALU.pow).then_inc(rstd_done, 1)
                pool.wait_ge(said_kept, 2)
                for t in range(TT):
                    pool.wait_ge(gate_done, t + 1)
                    pool.tensor_tensor(gate[:, t, :], gate[:, t, :], said[:, t * B // TT, :], ALU.mult).then_inc(gated, 1)
                pool.wait_ge(out_spread_done, 1)
                pool.tensor_tensor(out_rstd[:], out_spread[:], m.minus_half[:, 0:TT], ALU.pow).then_inc(out_rstd_done, 1)
                for t in range(TT):
                    pool.wait_ge(scaled, t + 1)
                    pool.tensor_tensor(out[:, t, :], out[:, t, :], wide[:, OUT_GAMMA, :], ALU.mult).then_inc(gained, 1)

            @block.tensor
            def _(pe):
                products = 0

                def turn(n):
                    pe.wait_ge(rows_set, n + 1)
                    for c in range(DC):
                        last = pe.transpose(turn_bank[:, c * B:(c + 1) * B], rows[:, c * P:(c + 1) * P], m.ident[0:B, 0:B])
                    last.then_inc(turned, 1)
                    pe.wait_ge(turn_kept, n + 1)

                def project(w):
                    for c in range(DC):
                        last = pe.matmul(row_bank[0:B, 0:D], rows_t[:, c, :], w[:, c, :], start=(c == 0), stop=(c == DC - 1))
                    last.then_inc(product_ready, 1)

                pe.wait_ge(loaded, 16 * n_loads)
                for t in range(TT):
                    wait_for(pe, raw_done, t - 1)
                    for c in range(DC):
                        last = pe.matmul(gate_bank[t % 2][:, 0:D], m.x_t[:, c, t * P:(t + 1) * P], weights["gate_w"][:, c, :],
                                         start=(c == 0), stop=(c == DC - 1))
                    last.then_inc(gate_ready, 1)
                turn(0)
                project(weights["agg_w"])
                for n in range(STEPS1):
                    turn(1 + n)
                    for j in range(chunks):
                        for c in range(DC):
                            last = pe.matmul(hidden_bank[:, j * B:(j + 1) * B], weights["d1_w"][:, c, j * P:(j + 1) * P],
                                             rows_t[:, c, :], start=(c == 0), stop=(c == DC - 1))
                    last.then_inc(hidden_ready, 1)
                    pe.wait_ge(active_done, n + 1)
                    pe.wait_ge(product_read, n + 1)
                    for j in range(chunks):
                        last = pe.matmul(row_bank[0:B, 0:D], active[:, j, :], weights["d2_w"][:, j, :],
                                         start=(j == 0), stop=(j == chunks - 1))
                    last.then_inc(product_ready, 1)
                turn(1 + STEPS1)
                project(weights["bc_w"])
                pe.wait_ge(rows_set, 3 + STEPS1)
                for b in range(B):
                    last = pe.matmul(said_bank[b // 2][:, b % 2 * D:(b % 2 + 1) * D], pick[:, b, :], rows[:], start=True, stop=True)
                last.then_inc(said_ready, 1)

            @block.scalar
            def _(act):
                def keep_turn(n):
                    act.wait_ge(turned, n + 1)
                    act.copy(rows_t[:], turn_bank[:, 0:DC * B].rearrange("p (c b) -> p c b", c=DC)).then_inc(turn_kept, 1)

                for t in range(TT):
                    act.wait_ge(raw_done, t + 1)
                    act.activation(gate[:, t, :], raw[:, t, :], ACT.Sigmoid).then_inc(gate_done, 1)
                keep_turn(0)
                for n in range(STEPS1):
                    keep_turn(1 + n)
                    act.wait_ge(hidden_set, n + 1)
                    act.activation(active[:], hidden[:], ACT.Gelu).then_inc(active_done, 1)
                keep_turn(1 + STEPS1)
                act.wait_ge(said_ready, 1)
                for n in range(2):
                    act.copy(said[:, 2 * n:2 * n + 2, :], said_bank[n][:].rearrange("p (b d) -> p b d", b=2)).then_inc(said_kept, 1)

            @block.vector
            def _(dve):
                links = 0

                def link(instruction):
                    nonlocal links
                    links += 1
                    instruction.then_inc(own, 1)
                    dve.wait_ge(own, links)

                def norm(n, of, gamma, beta):
                    link(dve.bn_stats(stats[:], of[:]))
                    link(dve.bn_aggr(moments[:], stats[:]))
                    dve.tensor_scalar(spread[:], moments[:, 1:2], eps, None, ALU.add).then_inc(spread_done, 1)
                    dve.wait_ge(rstd_done, n + 1)
                    link(dve.tensor_scalar(rows[:], of[:], moments[:, 0:1], rstd[:], ALU.subtract, ALU.mult))
                    link(dve.tensor_tensor(rows[:], rows[:], small[:, gamma, :], ALU.mult))
                    dve.tensor_tensor(rows[:], rows[:], small[:, beta, :], ALU.add).then_inc(rows_set, 1)

                dve.wait_ge(loaded, 16 * n_loads)
                for t in range(TT):
                    dve.wait_ge(gate_ready, t + 1)
                    dve.tensor_tensor(raw[:, t, :], gate_bank[t % 2][:, 0:D], wide[:, GATE_B, :], ALU.add).then_inc(raw_done, 1)
                dve.wait_ge(last_loaded, 16)
                norm(0, last_x, IN_GAMMA, IN_BETA)
                dve.wait_ge(product_ready, 1)
                product = dve.tensor_tensor(thought[:], row_bank[0:B, 0:D], small[:, AGG_B, :], ALU.add)
                product.then_inc(product_read, 1)
                dve.wait_ge(product_read, 1)
                for n in range(STEPS1):
                    norm(1 + n, thought, PN_GAMMA, PN_BETA)
                    dve.wait_ge(hidden_ready, n + 1)
                    dve.tensor_tensor(hidden[:], hidden_bank[:, 0:chunks * B].rearrange("p (j b) -> p j b", j=chunks),
                                      d1_b[:].rearrange("p (j a) -> p j a", a=1).broadcast_to([P, chunks, B]),
                                      ALU.add).then_inc(hidden_set, 1)
                    dve.wait_ge(product_ready, n + 2)
                    dve.tensor_tensor(delta[:], row_bank[0:B, 0:D], small[:, D2_B, :], ALU.add).then_inc(product_read, 1)
                    dve.wait_ge(product_read, n + 2)
                    link(dve.tensor_tensor(thought[:], thought[:], delta[:], ALU.add))
                dve.tensor_copy(rows[:], thought[:]).then_inc(rows_set, 1)
                dve.wait_ge(product_ready, 2 + STEPS1)
                dve.tensor_tensor(rows[:], row_bank[0:B, 0:D], small[:, BC_B, :], ALU.add).then_inc(rows_set, 1)
                for t in range(TT):
                    dve.wait_ge(gated, t + 1)
                    dve.tensor_tensor(out[:, t, :], gate[:, t, :], m.x_n[:, t, :], ALU.add).then_inc(added, 1)
                    dve.wait_ge(added, t + 1)
                    link(dve.bn_stats(out_stats[:, t, :], out[:, t, :]))
                    link(dve.bn_aggr(out_moments[:, t, :], out_stats[:, t, :]))
                dve.tensor_scalar(out_spread[:], out_moments[:, :, 1], eps, None, ALU.add).then_inc(out_spread_done, 1)
                dve.wait_ge(out_rstd_done, 1)
                for t in range(TT):
                    dve.tensor_scalar(out[:, t, :], out[:, t, :], out_moments[:, t, 0:1], out_rstd[:, t:t + 1],
                                      ALU.subtract, ALU.mult).then_inc(scaled, 1)
                for t in range(TT):
                    dve.wait_ge(gained, t + 1)
                    dve.tensor_tensor(raw[:, t, :], out[:, t, :], wide[:, OUT_BETA, :], ALU.add).then_inc(offset_done, 1)
                    dve.wait_ge(offset_done, t + 1)
                    dve.tensor_tensor(m.x[:, t, :], m.x[:, t, :], raw[:, t, :], ALU.add)


def route_stage(nc, m, dram, name, experts, chosen, capacity):
    with Stage(nc, m, name) as st:
        pad = 8 - chosen
        gate_w = st.sbuf("gate_w", [P, DC, experts])
        before = st.sbuf("before", [P, 2, P], BF16)
        before_raw = st.sbuf("before_raw", [P, P])
        top = st.sbuf("top", [P, TT])
        total = st.sbuf("total", [P, TT])
        inverse = st.sbuf("inverse", [P, TT])
        logit = st.sbuf("logit", [P, TT, experts])
        prob = st.sbuf("prob", [P, TT, experts + pad])
        best = st.sbuf("best", [P, TT, 8])
        rest = st.sbuf("rest", [P, TT, experts + pad])
        mask = st.sbuf("mask", [P, TT, experts])
        mask_b = st.sbuf("mask_b", [P, TT, experts], BF16)
        share = st.sbuf("share", [P, TT, experts])
        logit_bank, = st.banks("logit", 1)
        place_bank, = st.banks("place", 1)
        turn_bank = st.banks("turn", 2)
        loaded, logits_ready, own, shifted, exp_done, masked, places_ready, shares_done, turned = st.sems(
            "loaded", "logits_ready", "own", "shifted", "exp_done", "masked", "places_ready", "shares_done", "turned")
        wide = [P, TT, experts]

        def by_tile(a):
            return a.rearrange("p (t a) -> p t a", a=1).broadcast_to(wide)

        with st.block() as block:

            @block.sync
            def _(sp):
                sp.dma_start(gate_w[:], dram["gate_w"].rearrange("(c p) n -> p c n", p=P)).then_inc(loaded, 16)
                sp.dma_start(before_raw[:], dram["before"]).then_inc(loaded, 16)

            @block.tensor
            def _(pe):
                pe.wait_ge(loaded, 32)
                for t in range(TT):
                    for c in range(DC):
                        last = pe.matmul(logit_bank[:, t * experts:(t + 1) * experts], m.x_t[:, c, t * P:(t + 1) * P],
                                         gate_w[:, c, :], start=(c == 0), stop=(c == DC - 1))
                last.then_inc(logits_ready, 1)
                if capacity is not None:
                    pe.wait_ge(masked, 1)
                    for t in range(TT):
                        for s in range(t + 1):
                            last = pe.matmul(place_bank[:, t * experts:(t + 1) * experts], before[:, int(s < t), :],
                                             mask_b[:, s, :], start=(s == 0), stop=(s == t))
                    last.then_inc(places_ready, 1)
                pe.wait_ge(shares_done, 1)
                for t in range(TT):
                    bank, at = turn_bank[t * 2 // TT], t % (TT // 2) * P
                    last = pe.transpose(bank[0:experts, at:at + P], share[:, t, :], m.ident[:])
                last.then_inc(turned, 1)

            @block.scalar
            def _(act):
                act.wait_ge(shifted, 1)
                act.activation(prob[:, :, 0:experts], logit[:], ACT.Exp).then_inc(exp_done, 1)

            @block.vector
            def _(dve):
                links = 0

                def link(instruction):
                    nonlocal links
                    links += 1
                    instruction.then_inc(own, 1)
                    dve.wait_ge(own, links)

                dve.wait_ge(loaded, 32)
                dve.tensor_copy(before[:, 0, :], before_raw[:])
                link(dve.memset(before[:, 1, :], 1.0))
                dve.wait_ge(logits_ready, 1)
                logits = logit_bank[:, 0:TT * experts].rearrange("p (t e) -> p t e", t=TT)
                link(dve.tensor_reduce(top[:], logits, AX_X, ALU.max))
                dve.tensor_tensor(logit[:], logits, by_tile(top[:]), ALU.subtract).then_inc(shifted, 1)
                dve.wait_ge(exp_done, 1)
                p = prob[:, :, 0:experts]
                link(dve.tensor_reduce(total[:], p, AX_X, ALU.add))
                link(dve.reciprocal(inverse[:], total[:]))
                link(dve.tensor_tensor(p, p, by_tile(inverse[:]), ALU.mult))
                for t in range(TT):
                    last = dve.max(best[:, t, :], prob[:, t, 0:experts])
                link(last)
                for n in range(pad):
                    dve.memset(best[:, :, chosen + n], -1.0 - n)
                    last = dve.memset(prob[:, :, experts + n], -1.0 - n)
                if pad:
                    link(last)
                for t in range(TT):
                    last = dve.match_replace(rest[:, t, :], best[:, t, :], prob[:, t, :], -9.0)
                link(last)
                link(dve.tensor_tensor(mask[:], rest[:, :, 0:experts], p, ALU.not_equal))
                link(dve.tensor_tensor(share[:], p, mask[:], ALU.mult))
                dve.tensor_copy(mask_b[:], mask[:]).then_inc(masked, 1)
                link(dve.tensor_reduce(total[:], share[:], AX_X, ALU.add))
                link(dve.reciprocal(inverse[:], total[:]))
                last = dve.tensor_tensor(share[:], share[:], by_tile(inverse[:]), ALU.mult)
                if capacity is not None:
                    link(last)
                    dve.wait_ge(places_ready, 1)
                    places = place_bank[:, 0:TT * experts].rearrange("p (t e) -> p t e", t=TT)
                    last = dve.scalar_tensor_tensor(share[:], places, float(capacity), share[:], ALU.is_lt, ALU.mult)
                last.then_inc(shares_done, 1)
                dve.wait_ge(turned, 1)
                for n in range(2):
                    at = slice(n * BANK, (n + 1) * BANK)
                    last = dve.tensor_copy(m.mix[0:experts, at], turn_bank[n][0:experts, :])
                link(last)
                for n in range(2):
                    at = slice(n * BANK, (n + 1) * BANK)
                    dve.tensor_tensor(m.mix[experts:2 * experts, at], turn_bank[n][0:experts, :], m.mix[0:experts, at].bitcast(F32),
                                      ALU.subtract)


def experts_stage(nc, m, dram, name, experts, tiles, gated, shared):
    halves = TOKENS // BANK
    slots = 4
    width = 2 * D + P + D
    used = width if gated else 2 * D + P
    with Stage(nc, m, name) as st:
        raw = st.sbuf("raw", [P, slots, width])
        high = st.sbuf("high", [P, slots, width], F32R)
        low = st.sbuf("low", [P, slots, width], F32R)
        gate = st.sbuf("gate", [P, halves, BANK])
        upped = st.sbuf("upped", [P, halves, BANK])
        h = st.sbuf("h", [P, halves, BANK])
        h_high = st.sbuf("h_high", [P, 2, TOKENS], F32R)
        h_low = st.sbuf("h_low", [P, 2, TOKENS], F32R)
        y_t = st.sbuf("y_t", [P, DC, TOKENS])
        y_bank = st.banks("y", DC * halves)
        hidden_bank = st.banks("hidden", halves)
        up_bank, mix_bank = st.banks("up", 1) + st.banks("mix", 1)
        w_loaded = [st.sem(f"w_loaded{n}") for n in range(slots)]
        (w_high_done, w_low_done, hidden_ready, up_ready, mix_ready, gate_done, up_done, h_done, high_done, low_done,
         y_ready, y_kept, turned, x_added) = st.sems(
            "w_high_done", "w_low_done", "hidden_ready", "up_ready", "mix_ready", "gate_done", "up_done", "h_done",
            "high_done", "low_done", "y_ready", "y_kept", "turned", "x_added")
        n_tiles = shared + tiles

        def walk(engine, step):
            def four(i):
                for k in range(slots):
                    step(i * slots + (shared + k), (shared + k) % slots, i + (shared + k) // slots, False)

            for j in range(shared):
                step(j, j % slots, j // slots, True)
            four(0)
            with engine.Fori(1, tiles // slots - 1) as i:
                four(i)
            four(tiles // slots - 1)
            step(n_tiles, n_tiles % slots, None, False)

        def exists(j, ahead):
            return not isinstance(j, int) or 0 <= j + ahead < n_tiles

        def w1(of, slot, c):
            return of[:, slot, c * P:(c + 1) * P]

        def w2(of, slot, o):
            return of[:, slot, D + o * P:D + (o + 1) * P]

        def wu(of, slot, c):
            return of[:, slot, 2 * D + P + c * P:2 * D + P + (c + 1) * P]

        def selector(slot):
            return high[0:2 * experts, slot, 2 * D:2 * D + P]

        with st.block() as block:

            @block.sync
            def _(sp):
                def step(j, slot, turn, is_shared):
                    if exists(j, 0):
                        wait_for(sp, w_low_done, j + (1 - slots))
                        if is_shared:
                            sp.dma_start(raw[:, slot, :], dram["shared_w"][j]).then_inc(w_loaded[slot], 16)
                        else:
                            sp.dma_start(raw[:, slot, 0:used], dram["w"][j - shared]).then_inc(w_loaded[slot], 16)

                walk(sp, step)

            @block.tensor
            def _(pe):
                def product(bank, left, right):
                    for c in range(DC):
                        (left_high, left_low), (right_high, right_low) = left(c), right(c)
                        pe.matmul(bank[:], left_high, right_high, start=(c == 0), stop=False)
                        pe.matmul(bank[:], left_high, right_low, start=False, stop=False)
                        last = pe.matmul(bank[:], left_low, right_high, start=False, stop=(c == DC - 1))
                    return last

                def step(j, slot, turn, is_shared):
                    first, final = isinstance(j, int) and j == 1, isinstance(j, int) and j == n_tiles
                    old = (slot - 1) % slots
                    if exists(j, 0):
                        pe.wait_ge(w_low_done, j + 1)
                    for n in range(halves):
                        columns = slice(n * BANK, (n + 1) * BANK)
                        half = j * halves + n

                        def tokens(c):
                            return m.x_high[:, c, columns], m.x_low[:, c, columns]

                        if exists(j, 0):
                            wait_for(pe, gate_done, half - 1)
                            product(hidden_bank[n], lambda c: (w1(high, slot, c), w1(low, slot, c)),
                                    tokens).then_inc(hidden_ready, 1)
                            has_up = gated or is_shared
                            if has_up:
                                wait_for(pe, h_done, half)
                                product(up_bank, lambda c: (wu(high, slot, c), wu(low, slot, c)), tokens).then_inc(up_ready, 1)
                            if not is_shared:
                                after_shared = isinstance(j, int) and j == shared
                                wait_for(pe, h_done, half if gated or after_shared else half - 1)
                                pe.matmul((mix_bank if gated or n == 1 else up_bank)[:], selector(slot),
                                          m.mix[0:2 * experts, columns], start=True, stop=True).then_inc(mix_ready, 1)
                        if exists(j, -1):
                            pe.wait_ge(low_done, half + (1 - halves))
                            at = (slot - 1) % 2
                            for o in range(DC):
                                bank = y_bank[o * halves + n]
                                pe.matmul(bank[:], w2(high, old, o), h_high[:, at, columns], start=first, stop=False,
                                          skip_group_check=True)
                                pe.matmul(bank[:], w2(high, old, o), h_low[:, at, columns], start=False, stop=False,
                                          skip_group_check=True)
                                last = pe.matmul(bank[:], w2(low, old, o), h_high[:, at, columns], start=False, stop=final,
                                                 skip_group_check=True)
                            last.then_inc(y_ready, 1)

                walk(pe, step)
                for t in range(TT):
                    bank = hidden_bank[t % 2]
                    if t == 0:
                        pe.wait_ge(y_kept, DC * halves)
                    wait_for(pe, x_added, t - 1)
                    for o in range(DC):
                        last = pe.transpose(bank[:, o * P:(o + 1) * P], y_t[:, o, t * P:(t + 1) * P], m.ident[:])
                    last.then_inc(turned, 1)

            @block.scalar
            def _(act):
                def split(j, slot, turn, is_shared):
                    n = width if is_shared else used
                    act.wait_ge(w_loaded[slot], turn * 16 + 16)
                    wait_for(act, y_ready, j * halves + (1 - slots) * halves)
                    act.copy(high[:, slot, 0:n], raw[:, slot, 0:n]).then_inc(w_high_done, 1)

                def step(j, slot, turn, is_shared):
                    if exists(j, 0):
                        for n in range(halves):
                            half = j * halves + n
                            act.wait_ge(hidden_ready, half + 1)
                            wait_for(act, h_done, half - 1)
                            act.activation(gate[:, n, :], hidden_bank[n][:], ACT.Silu).then_inc(gate_done, 1)
                    if exists(j, 2):
                        split(j + 2, (slot + 2) % slots, turn + (slot + 2) // slots, isinstance(j, int) and j + 2 < shared)
                    if exists(j, 0):
                        for n in range(halves):
                            half = j * halves + n
                            act.wait_ge(h_done, half + 1)
                            wait_for(act, y_ready, half + (1 - 2 * halves))
                            act.copy(h_high[:, slot % 2, n * BANK:(n + 1) * BANK], h[:, n, :]).then_inc(high_done, 1)

                for j in range(2):
                    split(j, j, 0, j < shared)
                walk(act, step)
                act.wait_ge(y_ready, n_tiles * halves)
                for o in range(DC):
                    for n in range(halves):
                        act.copy(y_t[:, o, n * BANK:(n + 1) * BANK], y_bank[o * halves + n][:]).then_inc(y_kept, 1)

            @block.gpsimd
            def _(pool):
                def step(j, slot, turn, is_shared):
                    if exists(j, 0):
                        pool.wait_ge(w_high_done, j + 1)
                        parts = [slice(0, 2 * D)] + ([slice(2 * D + P, width)] if gated or is_shared else [])
                        for at in parts:
                            last = pool.tensor_tensor(low[:, slot, at], raw[:, slot, at], high[:, slot, at].bitcast(F32),
                                                      ALU.subtract)
                        last.then_inc(w_low_done, 1)

                walk(pool, step)

            @block.vector
            def _(dve):
                def step(j, slot, turn, is_shared):
                    if exists(j, 0):
                        for n in range(halves):
                            half = j * halves + n
                            dve.wait_ge(gate_done, half + 1)
                            wait_for(dve, low_done, half - 1)
                            if is_shared:
                                dve.wait_ge(up_ready, half + 1)
                                dve.tensor_tensor(h[:, n, :], gate[:, n, :], up_bank[:], ALU.mult).then_inc(h_done, 1)
                            elif gated:
                                dve.wait_ge(up_ready, half + 1)
                                dve.tensor_tensor(upped[:, n, :], gate[:, n, :], up_bank[:], ALU.mult).then_inc(up_done, 1)
                                dve.wait_ge(up_done, half + 1)
                                dve.wait_ge(mix_ready, half + 1)
                                dve.tensor_tensor(h[:, n, :], upped[:, n, :], mix_bank[:], ALU.mult).then_inc(h_done, 1)
                            else:
                                dve.wait_ge(mix_ready, half + (1 - shared * halves))
                                dve.tensor_tensor(h[:, n, :], gate[:, n, :], (mix_bank if n else up_bank)[:],
                                                  ALU.mult).then_inc(h_done, 1)
                        for n in range(halves):
                            half = j * halves + n
                            dve.wait_ge(high_done, half + 1)
                            columns = slice(n * BANK, (n + 1) * BANK)
                            dve.tensor_tensor(h_low[:, slot % 2, columns], h[:, n, :],
                                              h_high[:, slot % 2, columns].bitcast(F32), ALU.subtract).then_inc(low_done, 1)

                walk(dve, step)
                for t in range(TT):
                    dve.wait_ge(turned, t + 1)
                    dve.tensor_tensor(m.x[:, t, :], m.x[:, t, :], hidden_bank[t % 2][:, 0:D], ALU.add).then_inc(x_added, 1)


class Memory:

    def __init__(self, nc, stack):
        def sbuf(name, shape, dtype=F32):
            return stack.enter_context(nc.sbuf_tensor(name, shape, dtype))

        self.nc = nc
        self.banks = [stack.enter_context(nc.psum_tensor(f"bank{n}", [P, BANK], F32)) for n in range(8)]
        self.ctx_high = None
        self.used_semaphores = []
        self.x = sbuf("x", [P, TT, D])
        self.ident = sbuf("ident", [P, P])
        self.ones = sbuf("ones", [P, 2])
        self.minus_half = sbuf("minus_half", [P, HEADS])

    def sbuf(self, stack, name, shape, dtype=F32):
        return stack.enter_context(self.nc.sbuf_tensor(name, shape, dtype))

    def context(self, stack):
        self.ctx_high = self.sbuf(stack, "ctx_high", [P, BATCH * KT, CW], F32R)
        self.ctx_low = self.sbuf(stack, "ctx_low", [P, BATCH * KT, CW], F32R)
        self.ctx_t_high = self.sbuf(stack, "ctx_t_high", [CW, BATCH * KEYS], F32R)
        self.ctx_t_low = self.sbuf(stack, "ctx_t_low", [CW, BATCH * KEYS], F32R)

    def tokens(self, stack, name, whole, parts, keep, mix):
        if whole:
            self.x_t = self.sbuf(stack, name + "_x_t", [P, DC, TOKENS])
        if parts:
            self.x_high = self.sbuf(stack, name + "_x_high", [P, DC, TOKENS], F32R)
            self.x_low = self.sbuf(stack, name + "_x_low", [P, DC, TOKENS], F32R)
        if keep:
            self.x_n = self.sbuf(stack, name + "_x_n", [P, TT, D])
        if mix:
            self.mix = self.sbuf(stack, name + "_mix", [P, TOKENS], F32R)

    def small_heads(self, stack):
        self.q0_t = self.sbuf(stack, "q0_t", [P, BATCH * GROUPS, 2 * P], F32R)
        self.k0_t = self.sbuf(stack, "k0_t", [P, BATCH * GROUPS, KEYS], F32R)
        self.v0 = self.sbuf(stack, "v0", [P, BATCH * GROUPS, KT, GROUP * H0])
        self.o0 = self.sbuf(stack, "o0", [P, BATCH * HEADS // 4, 2 * P])


CAPACITY3 = 2 * (TOKENS * 8 // 32)


def build(nc, dram, stages=99):
    def of(prefix):
        return {k[len(prefix):]: v for k, v in dram.items() if k.startswith(prefix)} | {
            k: dram[k] for k in ("mask", "rms", "before", "pick", "ctx_t")}

    with ExitStack() as stack:
        m = Memory(nc, stack)
        load_stage(nc, m, dram)

        def normed(name, *stages, whole=True, parts=True, keep=False, mix=False):
            with ExitStack() as tokens:
                m.tokens(tokens, name, whole, parts, keep, mix)
                norm_stage(nc, m, name, whole, parts, keep)
                for stage, *arguments in stages:
                    stage(nc, m, *arguments)

        def context():
            m.context(stack)
            context_stage(nc, m, dram)

        order = [
            lambda: normed("l0n", (small_attention, of("l0a_")), parts=False),
            lambda: normed("l0g", (sparse_ffn_stage, of("l0f_")), parts=False),
            lambda: normed("l1n", (heads_stage, of("l1a_"), "l1a", True), whole=False),
            lambda: normed("l1t", (thought_stage, of("l1f_")), parts=False, keep=True),
            lambda: normed("l2n", (heads_stage, of("l2a_"), "l2a", False), whole=False),
            lambda: normed("l2g", (route_stage, of("l2f_"), "l2r", 64, 6, None),
                           (experts_stage, of("l2f_"), "l2f", 64, 88, False, 3), mix=True),
            lambda: normed("l3n", (heads_stage, of("l3a_"), "l3a", False), whole=False),
            lambda: normed("l3g", (route_stage, of("l3f_"), "l3r", 32, 8, CAPACITY3),
                           (experts_stage, of("l3f_"), "l3f", 32, 24, True, 0), mix=True),
        ]
        chosen = range(len(order)) if stages == 99 else stages
        for n in chosen:
            if n in (2, 4, 6) and m.ctx_high is None:
                context()
            order[n]()
        store_stage(nc, m, dram)


def layouts(i):
    import numpy as _np

    def row_tiles(w):
        return w.reshape(-1, P, w.shape[-1])

    def in_tiles(w):
        return w.reshape(DC, P, -1, P).transpose(2, 1, 0, 3)

    def selectors(experts, width):
        owner = _np.arange(experts * width) // width
        of = (owner[None, :] == _np.arange(experts)[:, None]).astype(_np.float32).reshape(experts, -1, P).transpose(1, 0, 2)
        return _np.concatenate([of, of, _np.zeros((of.shape[0], P - 2 * experts, P), _np.float32)], 1)

    def packed(w1, w2, select, wu):
        return _np.concatenate([w.reshape(w.shape[0], P, -1) for w in (w1, w2, select, wu) if w is not None], 2)

    def heads_in(w):
        return w.reshape(DC, P, HEADS, P).transpose(2, 1, 0, 3).reshape(HEADS, P, DC * P)

    ctx = i["ctx_1024"].reshape(BATCH * KEYS, CW)
    a = {
        "x": i["x"].reshape(TOKENS, D), "ctx": ctx, "ctx_t": ctx.T, "mask": i["mask_BxS2_bf1"].reshape(-1).view(_np.uint8),
        "ident": _np.eye(P, dtype=_np.float32), "before": _np.triu(_np.ones((P, P), _np.float32), 1),
        "pick": _np.repeat(_np.eye(BATCH, dtype=_np.float32)[:, :, None], P, 2),
    }
    p = "L0_xattn_"
    a |= {f"l0a_{n}": i[p + w] for n, w in (
        ("wq", "Wq"), ("bq", "bq"), ("bo", "bo"), ("qn_w", "qn_w"), ("qn_b", "qn_b"), ("kn_w", "kn_w"), ("kn_b", "kn_b"),
        ("kn_dca_w", "kn_dca_w"), ("kn_dca_b", "kn_dca_b"))}
    a["l0a_wo"] = _np.pad(i[p + "Wo"].reshape(HEADS // 4, 4, H0, D), ((0, 0), (0, 0), (0, V0 - H0), (0, 0))).reshape(-1, P, D)
    a["l0a_wkv"] = _np.concatenate([i[p + "Wk"], i[p + "Wv"]], 1)
    a["l0a_bkv"] = _np.concatenate([i[p + "bk"], i[p + "bv"]])
    a["l0a_wkv_last"] = i[p + "Wkv_dca"].reshape(CW, 2, HEADS, H0).transpose(0, 2, 1, 3).reshape(CW, 2 * D)
    a["l0a_bkv_last"] = i[p + "bkv_dca"].reshape(2, HEADS, H0).transpose(1, 0, 2).reshape(2 * D)
    a |= {f"l0f_{n}": i["L0_ffn_" + n] for n in ("w_gate", "w_up", "w_down")}
    p = "L1_xattn_"
    a |= {"l1a_wq": heads_in(i[p + "Wq"]), "l1a_wk": i[p + "Wk"].reshape(CW, HEADS, P).transpose(1, 0, 2),
          "l1a_wv_t": row_tiles(i[p + "Wv"].T), "l1a_wo": row_tiles(i[p + "Wo"]),
          "l1a_gq": i[p + "gq"][:, None], "l1a_gk": i[p + "gk"][:, None]}
    a |= {f"l1f_{n}": i["L1_ffn_" + n] for n in ("in_gamma", "in_beta", "agg_w", "agg_b", "pn_gamma", "pn_beta", "d1_w", "d2_w", "d2_b",
                                                "bc_w", "bc_b", "gate_w", "gate_b", "out_gamma", "out_beta")}
    a["l1f_d1_b"] = i["L1_ffn_d1_b"].reshape(-1, P).T
    for n in (2, 3):
        p = f"L{n}_xattn_"
        a |= {f"l{n}a_wq": row_tiles(i[p + "Wq"].T), f"l{n}a_wk": row_tiles(i[p + "Wk"].T), f"l{n}a_wv_t": row_tiles(i[p + "Wv"].T),
              f"l{n}a_wo": row_tiles(i[p + "Wo"])}
    p = "L2_ffn_"
    inner = i[p + "shared_down"].shape[1]
    short = -inner % P
    gate, up = (_np.pad(w.T, ((0, 0), (0, short))) for w in (i[p + "shared_gate_up"][:inner], i[p + "shared_gate_up"][inner:]))
    nothing = _np.zeros((gate.shape[1] // P, P, P), _np.float32)
    a |= {"l2f_gate_w": i[p + "gate_w"].T,
          "l2f_w": packed(in_tiles(i[p + "experts_w1"].reshape(-1, D).T),
                          row_tiles(i[p + "experts_w2"].transpose(0, 2, 1).reshape(-1, D)), selectors(64, 176), None),
          "l2f_shared_w": packed(in_tiles(gate), row_tiles(_np.pad(i[p + "shared_down"].T, ((0, short), (0, 0)))), nothing,
                                 in_tiles(up))}
    p = "L3_ffn_"
    a |= {"l3f_gate_w": i[p + "gate_w"],
          "l3f_w": packed(in_tiles(i[p + "w_gate"].transpose(1, 0, 2).reshape(D, -1)), row_tiles(i[p + "w_down"].reshape(-1, D)),
                          selectors(32, 96), in_tiles(i[p + "w_up"].transpose(1, 0, 2).reshape(D, -1)))}
    return {n: _np.ascontiguousarray(v) for n, v in a.items()}


def kernel(_stages=99, **inputs):
    import numpy as _np
    import concourse.bacc as _bacc
    from concourse.bass_utils import run_bass_kernel_spmd as _run

    arrays = layouts({n: _np.asarray(v) for n, v in inputs.items()})
    nc = _bacc.Bacc("TRN2", target_bir_lowering=False, num_devices=1)
    dram = {n: nc.dram_tensor(f"in_{n}", v.shape, mybir.dt.from_np(v.dtype), kind="ExternalInput").ap() for n, v in arrays.items()}
    dram["rms"] = nc.dram_tensor("rms", (2, BATCH * KT, P), F32, kind="Internal").ap()
    dram["out"] = nc.dram_tensor("out", (TOKENS, D), F32, kind="ExternalOutput").ap()
    build(nc, dram, _stages)
    r = _run(nc, [{f"in_{n}": v for n, v in arrays.items()}], core_ids=[0])
    return r.results[0]["out"].reshape(BATCH, TOKENS // BATCH, D)
```

```python
from contextlib import ExitStack

import concourse.bass as bass
from concourse import mybir
from concourse.alu_op_type import AluOpType as ALU

ACT = mybir.ActivationFunctionType
AX_X = mybir.AxisListType.X
F32 = mybir.dt.float32
F32R = mybir.dt.float32r
BF16 = mybir.dt.bfloat16
U8 = mybir.dt.uint8

P = 128
BATCH = 4
TOKENS = 1024
TT = TOKENS // P
D = 256
DC = D // P
KEYS = 512
KT = KEYS // P
CW = 128
HEADS = 16
BANK = 512
LOWEST = -3.0e38
MASKED = 1.0e30
PAIRS = HEADS * BATCH
AHEAD = 4
RMS_EPS = 1e-5


def wait_for(engine, semaphore, count):
    if not isinstance(count, int) or count > 0:
        engine.wait_ge(semaphore, count)


class Stage:

    def __init__(self, nc, m, name):
        self.nc, self.m, self.name, self.stack, self.free_banks = nc, m, name, ExitStack(), list(m.banks)
        self.semaphores = []

    def __enter__(self):
        return self

    def __exit__(self, *error):
        self.stack.close()
        self.m.used_semaphores = self.semaphores

    def sbuf(self, name, shape, dtype=F32):
        return self.stack.enter_context(self.nc.sbuf_tensor(f"{self.name}_{name}", shape, dtype))

    def banks(self, name, count):
        given, self.free_banks = self.free_banks[:count], self.free_banks[count:]
        assert len(given) == count, name
        return given

    def sem(self, name):
        self.semaphores.append(self.nc.alloc_semaphore(name=f"{self.name}_{name}"))
        return self.semaphores[-1]

    def sems(self, *names):
        return [self.sem(n) for n in names]

    def block(self):
        if self.m.used_semaphores:
            self.nc.clear_and_free_semaphores(self.m.used_semaphores)
        return self.nc.Block()


def load_stage(nc, m, dram):
    with Stage(nc, m, "load") as st:
        loaded, set_up = st.sems("loaded", "set_up")
        with st.block() as block:

            @block.sync
            def _(sp):
                sp.dma_start(m.x[:], dram["x"].rearrange("(t p) d -> p t d", p=P)).then_inc(loaded, 16)
                sp.dma_start(m.ident[:], dram["ident"]).then_inc(loaded, 16)
                sp.wait_ge(loaded, 32)

            @block.gpsimd
            def _(pool):
                pool.memset(m.minus_half[:], -0.5).then_inc(set_up, 1)
                pool.memset(m.ones[:], 1.0).then_inc(set_up, 1)
                pool.wait_ge(set_up, 2)


class Context:

    def __init__(self, st, m, dram):
        self.m, self.dram = m, dram
        self.ctx = st.sbuf("ctx", [P, BATCH * KT, CW])
        self.ctx_t = st.sbuf("ctx_t", [CW, BATCH * KEYS])
        self.loaded, self.high_done = st.sems("ctx_loaded", "ctx_high_done")

    def sync(self, sp):
        sp.dma_start(self.ctx[:], self.dram["ctx"].rearrange("(t p) c -> p t c", p=P)).then_inc(self.loaded, 16)
        sp.dma_start(self.ctx_t[:], self.dram["ctx_t"]).then_inc(self.loaded, 16)

    def gpsimd(self, pool):
        m = self.m
        pool.wait_ge(self.loaded, 32)
        pool.tensor_copy(m.ctx_high[:], self.ctx[:])
        pool.tensor_copy(m.ctx_t_high[:], self.ctx_t[:]).then_inc(self.high_done, 1)
        pool.wait_ge(self.high_done, 1)
        pool.tensor_tensor(m.ctx_low[:], self.ctx[:], m.ctx_high[:].bitcast(F32), ALU.subtract)
        pool.tensor_tensor(m.ctx_t_low[:], self.ctx_t[:], m.ctx_t_high[:].bitcast(F32), ALU.subtract)


class Norm:

    EPS = 1e-5
    SETS = 2

    def __init__(self, st, m, banks, whole=False, parts=False, keep=False):
        self.m, self.banks, self.whole, self.parts, self.keep = m, banks, whole, parts, keep
        self.stats = st.sbuf("norm_stats", [P, TT, 6])
        self.moments = st.sbuf("norm_moments", [P, TT, 2])
        self.spread = st.sbuf("norm_spread", [P, TT])
        self.rstd = st.sbuf("norm_rstd", [P, TT])
        self.slots = TT if keep else 4
        self.xn = m.x_n if keep else st.sbuf("norm_xn", [P, self.slots, D])
        (self.stats_done, self.moments_done, self.spread_done, self.rstd_done, self.xn_done, self.turned, self.high_done,
         self.low_done) = st.sems("norm_stats_done", "norm_moments_done", "norm_spread_done", "norm_rstd_done",
                                  "norm_xn_done", "norm_turned", "norm_high_done", "norm_low_done")
        self.kept = self.low_done if parts else self.high_done

    def ready(self, engine):
        engine.wait_ge(self.kept, TT)

    def set_of(self, n):
        return range(n * TT // self.SETS, (n + 1) * TT // self.SETS)

    def tile(self, t):
        return self.banks[t % 2][:, 0:D].rearrange("p (c q) -> p c q", c=DC)

    def vector(self, dve):
        m = self.m
        for n in range(self.SETS):
            of = self.set_of(n)
            for t in of:
                last = dve.bn_stats(self.stats[:, t, :], m.x[:, t, :])
            last.then_inc(self.stats_done, 1)
            dve.wait_ge(self.stats_done, n + 1)
            for t in of:
                last = dve.bn_aggr(self.moments[:, t, :], self.stats[:, t, :])
            last.then_inc(self.moments_done, 1)
            dve.wait_ge(self.moments_done, n + 1)
            at = slice(of[0], of[-1] + 1)
            dve.tensor_scalar(self.spread[:, at], self.moments[:, at, 1], self.EPS, None, ALU.add).then_inc(self.spread_done, 1)

        def keep_low(t):
            at = slice(t * P, (t + 1) * P)
            dve.wait_ge(self.high_done, t + 1)
            dve.tensor_tensor(m.x_low[:, :, at], self.tile(t), m.x_high[:, :, at].bitcast(F32),
                              ALU.subtract).then_inc(self.low_done, 1)

        for t in range(TT):
            dve.wait_ge(self.rstd_done, t * self.SETS // TT + 1)
            wait_for(dve, self.turned, t + 1 - self.slots)
            dve.tensor_scalar(self.xn[:, t % self.slots, :], m.x[:, t, :], self.moments[:, t, 0:1], self.rstd[:, t:t + 1],
                              ALU.subtract, ALU.mult).then_inc(self.xn_done, 1)
            if self.parts and t >= 2:
                keep_low(t - 2)
        for t in range(TT - 2 if self.parts else TT, TT):
            keep_low(t)

    def gpsimd(self, pool):
        for n in range(self.SETS):
            at = slice(self.set_of(n)[0], self.set_of(n)[-1] + 1)
            pool.wait_ge(self.spread_done, n + 1)
            pool.tensor_tensor(self.rstd[:, at], self.spread[:, at], self.m.minus_half[:, at], ALU.pow).then_inc(self.rstd_done, 1)

    def tensor(self, pe, use=None):
        def use_tile(t):
            if use and t >= 0:
                pe.wait_ge(self.high_done, t + 1)
                use(t)

        for t in range(TT):
            pe.wait_ge(self.xn_done, t + 1)
            wait_for(pe, self.kept, t - 1)
            for c in range(DC):
                last = pe.transpose(self.banks[t % 2][:, c * P:(c + 1) * P], self.xn[:, t % self.slots, c * P:(c + 1) * P],
                                    self.m.ident[:])
            last.then_inc(self.turned, 1)
            use_tile(t - 1)
        use_tile(TT - 1)

    def scalar(self, act):
        m = self.m
        for t in range(TT):
            act.wait_ge(self.turned, t + 1)
            for to in ([m.x_t] if self.whole else []) + ([m.x_high] if self.parts else []):
                last = act.copy(to[:, :, t * P:(t + 1) * P], self.tile(t))
            last.then_inc(self.high_done, 1)


def rms_stage(nc, m, dram, name, weights):
    sets = HEADS * P // BANK
    per_set = HEADS // sets
    key_tiles = BATCH * KT
    units = [("k", g, t) for g in range(sets) for t in range(key_tiles)] + [
        ("q", g, t) for g in range(sets) for t in range(TT)]
    turn_at = sets * key_tiles + 8
    ends = [n for n, u in enumerate(units) if n + 1 == len(units) or units[n + 1][:2] != u[:2]]
    with Stage(nc, m, name) as st:
        wk = st.sbuf("wk", [CW, HEADS * P])
        wq = st.sbuf("wq", [P, DC, HEADS * P])
        wk_high = st.sbuf("wk_high", [CW, HEADS * P], F32R)
        wk_low = st.sbuf("wk_low", [CW, HEADS * P], F32R)
        wq_high = st.sbuf("wq_high", [P, DC, HEADS * P], F32R)
        wq_low = st.sbuf("wq_low", [P, DC, HEADS * P], F32R)
        squares = st.sbuf("squares", [P, 4, BANK])
        k_sums = st.sbuf("k_sums", [P, HEADS, key_tiles])
        q_sums = st.sbuf("q_sums", [P, HEADS, TT])
        k_root = st.sbuf("k_root", [P, HEADS * key_tiles])
        q_root = st.sbuf("q_root", [P, HEADS * TT])
        k_rms = st.sbuf("k_rms", [P, HEADS * key_tiles])
        eps_columns = st.sbuf("eps_columns", [P, 2])
        rms_row = st.sbuf("rms_row", [P, 2, P])
        turn_bank = st.banks("turn", 2)
        unit_bank = st.banks("unit", 4)
        norm = Norm(st, m, turn_bank, parts=True)
        (k_loaded, q_loaded, high_done, low_done, cleared, unit_ready, squared, added, root_done, rms_done, turned, row_kept,
         stored) = st.sems("k_loaded", "q_loaded", "high_done", "low_done", "cleared", "unit_ready", "squared", "added",
                           "root_done", "rms_done", "turned", "row_kept", "stored")

        def set_of(n, k, q):
            kind, g, _ = units[ends[n]]
            count = per_set * (key_tiles if kind == "k" else TT)
            return (k if kind == "k" else q)[:, g * count:(g + 1) * count]

        def sums_of(unit):
            kind, g, t = unit
            return (k_sums if kind == "k" else q_sums)[:, g * per_set:(g + 1) * per_set, t]

        with st.block() as block:

            @block.sync
            def _(sp):
                sp.dma_start(wk[:], dram["wk_all"]).then_inc(k_loaded, 16)
                weights.sync_first(sp)
                for n in range(2):
                    sp.wait_ge(row_kept, n + 1)
                    sp.dma_start(dram["rms"].rearrange("h t p -> (h t) p")[n * P:(n + 1) * P], rms_row[:, n, :]).then_inc(stored, 16)
                sp.wait_ge(stored, 32)

            @block.tensor
            def _(pe):
                norm.tensor(pe)
                norm.ready(pe)
                pe.wait_ge(low_done, 1)
                for n, (kind, g, t) in enumerate(units):
                    if (kind, g, t) == ("q", 0, 0):
                        pe.wait_ge(low_done, 2)
                    wait_for(pe, squared, n - 3)
                    columns = slice(g * BANK, (g + 1) * BANK)
                    rows = slice(t * P, (t + 1) * P)
                    chunks = [((m.ctx_t_high[:, rows], m.ctx_t_low[:, rows]), (wk_high[:, columns], wk_low[:, columns]))
                              ] if kind == "k" else [
                        ((m.x_high[:, c, rows], m.x_low[:, c, rows]), (wq_high[:, c, columns], wq_low[:, c, columns]))
                        for c in range(DC)]
                    bank = unit_bank[n % 4][:]
                    for c, (left, right) in enumerate(chunks):
                        pe.matmul(bank, left[0], right[0], start=(c == 0), stop=False)
                        pe.matmul(bank, left[0], right[1], start=False, stop=False)
                        last = pe.matmul(bank, left[1], right[0], start=False, stop=(c == len(chunks) - 1))
                    last.then_inc(unit_ready, 1)
                    if n == turn_at:
                        pe.wait_ge(rms_done, sets)
                        for half in range(2):
                            pe.transpose(turn_bank[half][:, 0:P], k_rms[:, half * P:(half + 1) * P], m.ident[:]).then_inc(turned, 1)

            @block.scalar
            def _(act):
                act.dma_start(wq[:], dram["wq_all"].rearrange("(c p) n -> p c n", p=P)).then_inc(q_loaded, 16)
                act.wait_ge(k_loaded, 16)
                act.copy(wk_high[:], wk[:]).then_inc(high_done, 1)
                norm.scalar(act)
                act.wait_ge(q_loaded, 16)
                act.copy(wq_high[:], wq[:]).then_inc(high_done, 1)

                def root(n):
                    act.wait_ge(added, ends[n] + 1)
                    is_k = units[ends[n]][0] == "k"
                    act.activation(set_of(n, k_root, q_root), set_of(n, k_sums[:].rearrange("p h t -> p (h t)"),
                                                                     q_sums[:].rearrange("p h t -> p (h t)")), ACT.Sqrt,
                                   bias=eps_columns[:, 0:1] if is_k else eps_columns[:, 1:2],
                                   scale=1.0 / P if is_k else 1.0).then_inc(root_done, 1)

                act.wait_ge(cleared, 2)
                for n in range(len(units)):
                    act.wait_ge(unit_ready, n + 1)
                    wait_for(act, added, n - 3)
                    act.activation(squares[:, n % 4, :], unit_bank[n % 4][:], ACT.Square).then_inc(squared, 1)
                    if n - 2 in ends:
                        root(ends.index(n - 2))
                    if n == turn_at + 2:
                        for half in range(2):
                            act.wait_ge(turned, half + 1)
                            act.copy(rms_row[:, half, :], turn_bank[half][:, 0:P]).then_inc(row_kept, 1)
                root(len(ends) - 1)

            @block.vector
            def _(dve):
                norm.vector(dve)

                def invert(n):
                    dve.wait_ge(root_done, n + 1)
                    dve.reciprocal(set_of(n, k_rms, m.q_rms), set_of(n, k_root, q_root)).then_inc(rms_done, 1)

                for n, unit in enumerate(units):
                    dve.wait_ge(squared, n + 1)
                    dve.tensor_reduce(sums_of(unit), squares[:, n % 4, :].rearrange("p (h d) -> p h d", h=per_set), AX_X,
                                      ALU.add).then_inc(added, 1)
                    if n - 4 in ends:
                        invert(ends.index(n - 4))
                invert(len(ends) - 1)

            @block.gpsimd
            def _(pool):
                pool.memset(eps_columns[:, 0:1], RMS_EPS).then_inc(cleared, 1)
                pool.memset(eps_columns[:, 1:2], RMS_EPS * P).then_inc(cleared, 1)
                norm.gpsimd(pool)
                pool.wait_ge(high_done, 1)
                pool.tensor_tensor(wk_low[:], wk[:], wk_high[:].bitcast(F32), ALU.subtract).then_inc(low_done, 1)
                pool.wait_ge(high_done, 2)
                pool.tensor_tensor(wq_low[:], wq[:], wq_high[:].bitcast(F32), ALU.subtract).then_inc(low_done, 1)


class HeadWeights:

    def __init__(self, st, dram, qk_norm):
        self.dram, self.qk_norm = dram, qk_norm
        self.wq = st.sbuf("wq", [P, 2, D])
        self.wk = st.sbuf("wk", [P, 2, CW])
        self.wv_t = st.sbuf("wv_t", [P, 2, CW])
        self.wo = st.sbuf("wo", [P, 2, D])
        self.loaded = st.sems("w_loaded0", "w_loaded1")
        if qk_norm:
            self.gain = st.sbuf("gain", [P, 2])
            self.gain_loaded = st.sem("gain_loaded")

    def load(self, sp, h, g, slot):
        for to, of, n in ((self.wq, "wq", h), (self.wk, "wk", g), (self.wv_t, "wv_t", g), (self.wo, "wo", h)):
            sp.dma_start(to[:, slot, :], self.dram[of][n]).then_inc(self.loaded[slot], 16)

    def sync_first(self, sp):
        if self.qk_norm:
            sp.dma_start(self.gain[:, 0:1], self.dram["gq"]).then_inc(self.gain_loaded, 16)
            sp.dma_start(self.gain[:, 1:2], self.dram["gk"]).then_inc(self.gain_loaded, 16)
        for h in range(2):
            self.load(sp, h, h if self.qk_norm else 0, h)


def heads_stage(nc, m, dram, name, qk_norm):
    scale = float(P) ** -0.5
    pieces = ["a", "q0", "q1", "wvo"]
    n_pieces = len(pieces)
    with Stage(nc, m, name) as st:
        weights = HeadWeights(st, dram, qk_norm)
        wq, wk, wv_t, wo, w_loaded = weights.wq, weights.wk, weights.wv_t, weights.wo, weights.loaded
        if qk_norm:
            rms_stage(nc, m, dram, name + "r", weights)
        wvo = st.sbuf("wvo", [P, 2, D])
        wvo_high = st.sbuf("wvo_high", [P, 2, D], F32R)
        wvo_low = st.sbuf("wvo_low", [P, 2, D], F32R)
        q_t = st.sbuf("q_t", [P, 2, TOKENS])
        side = st.sbuf("side", [P, 2, BATCH * KEYS])
        valid = st.sbuf("valid", [P, BATCH])
        masked = st.sbuf("masked", [P, 4, KEYS])
        top = st.sbuf("top", [P, 4])
        shift = st.sbuf("shift", [P, 4])
        prob = st.sbuf("prob", [P, 4, KEYS])
        total = st.sbuf("total", [P, 16])
        inverse = st.sbuf("inverse", [P, 4])
        woken = st.sbuf("woken", [P, 1])
        pool_woken = st.sbuf("pool_woken", [P, 1])
        prob_high = st.sbuf("prob_high", [P, 2, KT, 2 * P], F32R)
        prob_low = st.sbuf("prob_low", [P, 2, KT, 2 * P], F32R)
        o_high = st.sbuf("o_high", [P, 2, 2 * P], F32R)
        o_low = st.sbuf("o_low", [P, 2, 2 * P], F32R)
        a_h = st.sbuf("a_h", [P, 2, D])
        a_high = st.sbuf("a_high", [P, 2, D], F32R)
        a_low = st.sbuf("a_low", [P, 2, D], F32R)
        q_high = st.sbuf("q_high", [P, 2, TOKENS], F32R)
        q_low = st.sbuf("q_low", [P, 2, TOKENS], F32R)
        if qk_norm:
            gain, gain_loaded = weights.gain, weights.gain_loaded
            gains = st.sbuf("gains", [P, 1])
            wk_gained = st.sbuf("wk_gained", [P, 2, CW])
            q_scale = st.sbuf("q_scale", [P, 2, TT])
        else:
            mask_u8 = st.sbuf("mask_u8", [P, BATCH * KEYS], U8)
            norm = Norm(st, m, None, parts=True)
        score_bank = st.banks("score", 2)
        turn_bank = st.banks("turn", 2)
        o_bank, = st.banks("o", 1)
        y_bank, = st.banks("y", 1)
        prep_bank = st.banks("prep", 2)
        if not qk_norm:
            norm.banks = turn_bank
        rms_loaded = st.sems("rms_loaded0", "rms_loaded1")
        (side_loaded, scores_ready, top_done, shift_done, exp_done, inverse_done, turn_ready,
         high_done, turn_kept, pv_ready, o_high_done, o_kept, own_high, split_done, y_ready, x_added, prep_ready,
         prep_kept) = st.sems(
            "side_loaded", "scores_ready", "top_done", "shift_done", "exp_done", "inverse_done",
            "turn_ready", "high_done", "turn_kept", "pv_ready", "o_high_done", "o_kept", "own_high", "split_done", "y_ready",
            "x_added", "prep_ready", "prep_kept")
        set_up, gained, q_scale_done = st.sems("set_up", "gained", "q_scale_done")

        def walk(engine, prepare, step, normalise=None):
            def two_heads(i, last=False):
                for k in range(2 * BATCH):
                    after, ahead = [pieces[k % BATCH]], k // BATCH + 1
                    if last and ahead == 2:
                        after = []
                    head = (i * 2 + k // BATCH, i, k // BATCH)
                    following = (i * 2 + ahead, i + ahead // 2, ahead % 2)
                    step(i * (2 * BATCH) + k, k, head, after, following)

            for piece in pieces:
                if piece == "q0" and normalise:
                    normalise(engine)
                prepare(piece, (0, 0, 0))
            two_heads(0)
            with engine.Fori(1, HEADS // 2 - 1) as i:
                two_heads(i)
            two_heads(HEADS // 2 - 1, True)
            for k in range(AHEAD):
                step(PAIRS + k, k, None, [], None)

        def is_head(h, number):
            return isinstance(h, int) and h == number

        parts_of = {"a": (a_high, a_low, a_h), "q0": (q_high, q_low, q_t), "q1": (q_high, q_low, q_t),
                    "wvo": (wvo_high, wvo_low, wvo)}

        def place(piece, slot):
            first, end = (int(piece[1]) * BANK, (int(piece[1]) + 1) * BANK) if piece in ("q0", "q1") else (0, D)
            return (slice(None), slot, slice(first, end)), end - first

        def exists(pair, back):
            return not isinstance(pair, int) or 0 <= pair - back < PAIRS

        with st.block() as block:

            @block.sync
            def _(sp):
                def load_roots(h, slot):
                    wait_for(sp, top_done, h * (2 * BATCH) - 2 * BATCH)
                    sp.dma_start(side[:, slot, :], dram["rms"][h].rearrange("t p -> (t p)").partition_broadcast(P)
                                 ).then_inc(rms_loaded[slot], 16)

                if qk_norm:
                    for h in range(2):
                        load_roots(h, h)
                else:
                    sp.dma_start(mask_u8[:], dram["mask"].partition_broadcast(P)).then_inc(side_loaded, 16)
                    weights.sync_first(sp)
                with sp.Fori(1, HEADS // 2) as i:
                    for slot in range(2):
                        sp.wait_ge(prep_kept, i * (2 * n_pieces) + (slot - 1) * n_pieces)
                        weights.load(sp, i * 2 + slot, i * 2 + slot if qk_norm else i, slot)
                        if qk_norm:
                            load_roots(i * 2 + slot, slot)

            @block.tensor
            def _(pe):
                def product(to, left, right, start, stop):
                    pe.matmul(to, left[0], right[0], start=start, stop=False)
                    pe.matmul(to, left[0], right[1], start=False, stop=False)
                    return pe.matmul(to, left[1], right[0], start=False, stop=stop)

                def normalise(pe):
                    norm.tensor(pe)
                    norm.ready(pe)

                def prepare(piece, head):
                    h, turn, slot = head
                    n = pieces.index(piece)
                    if n == 0:
                        pe.wait_ge(w_loaded[slot], turn * 64 + 64)
                        if qk_norm:
                            pe.wait_ge(gained, h + 1)
                    bank = prep_bank[n % 2]
                    if is_head(h, 0):
                        wait_for(pe, split_done, n - 1)
                    elif is_head(h, 1) and n < 2:
                        pe.wait_ge(split_done, n_pieces - 1 + n)
                    else:
                        pe.wait_ge(prep_kept, h * n_pieces + (n - 1))
                    if piece == "a":
                        for c in range(DC):
                            last = pe.matmul(bank[:, c * P:(c + 1) * P], wq[:, slot, c * P:(c + 1) * P],
                                             (wk_gained if qk_norm else wk)[:, slot, :], start=True, stop=True)
                    elif piece in ("q0", "q1"):
                        chunk = int(piece[1])
                        pe.wait_ge(split_done, h * n_pieces + 1)
                        for c in range(DC):
                            last = product(bank[:], [of[:, slot, c * P:(c + 1) * P] for of in (a_high, a_low)],
                                           [of[:, c, chunk * BANK:(chunk + 1) * BANK] for of in (m.x_high, m.x_low)],
                                           c == 0, c == DC - 1)
                    elif piece == "wvo":
                        last = pe.matmul(bank[:, 0:D], wv_t[:, slot, :], wo[:, slot, :], start=True, stop=True)
                    last.then_inc(prep_ready, 1)

                def step(pair, k, head, after, following):
                    b = k % BATCH
                    if exists(pair, 0):
                        h, _, slot = head
                        if b == 0:
                            pe.wait_ge(prep_kept, h * n_pieces + n_pieces)
                        if b % 2 == 0:
                            pe.wait_ge(split_done, h * n_pieces + (2 + b // 2))
                        keys = slice(b * KEYS, (b + 1) * KEYS)
                        for q in range(2):
                            wait_for(pe, top_done, pair * 2 + (q - 1))
                            at = slice((2 * b + q) * P, (2 * b + q + 1) * P)
                            last = product(score_bank[q][:], (q_high[:, slot, at], q_low[:, slot, at]),
                                           (m.ctx_t_high[:, keys], m.ctx_t_low[:, keys]), True, True)
                            last.then_inc(scores_ready, 1)
                    if exists(pair, 3):
                        pe.wait_ge(turn_kept, pair * 2 - 4)
                        wait_for(pe, o_kept, pair - 3)
                        for n in range(KT):
                            tile = (k - 3) % BATCH * KT + n
                            last = product(o_bank[:, 0:2 * P], (m.ctx_high[:, tile, :], m.ctx_low[:, tile, :]),
                                           (prob_high[:, (k - 3) % 2, n, :], prob_low[:, (k - 3) % 2, n, :]), n == 0, n == KT - 1)
                        last.then_inc(pv_ready, 1)
                    if exists(pair, 4):
                        pe.wait_ge(o_kept, pair - 3)
                        wait_for(pe, x_added, pair * 2 - 8)
                        if k % BATCH == 0:
                            h = HEADS if head is None else head[0]
                            pe.wait_ge(split_done, h * n_pieces)
                        old = (k - 4) // BATCH % 2
                        for q in range(2):
                            at = slice(q * P, (q + 1) * P)
                            last = product(y_bank[:, q * D:(q + 1) * D], [of[:, k % 2, at] for of in (o_high, o_low)],
                                           (wvo_high[:, old, :], wvo_low[:, old, :]), True, True)
                        last.then_inc(y_ready, 1)
                    for piece in after:
                        prepare(piece, following)
                    if exists(pair, 1):
                        for q in range(2):
                            pe.wait_ge(exp_done, pair * 2 + (q - 1))
                            wait_for(pe, turn_kept, pair * 2 + (q - 3))
                            for n in range(KT):
                                last = pe.transpose(turn_bank[q][:, n * P:(n + 1) * P],
                                                    prob[:, (2 * k - 2 + q) % 4, n * P:(n + 1) * P], m.ident[:])
                            last.then_inc(turn_ready, 1)

                walk(pe, prepare, step, None if qk_norm else normalise)

            @block.scalar
            def _(act):
                def prepare(piece, head):
                    h, turn, slot = head
                    n = pieces.index(piece)
                    bank = prep_bank[n % 2]
                    if is_head(h, 0) and piece == "wvo" and not qk_norm:
                        act.wait_ge(set_up, 1)
                    act.wait_ge(prep_ready, h * n_pieces + (n + 1))
                    high, _, whole = parts_of[piece]
                    at, width = place(piece, slot)
                    act.copy((high if is_head(h, 0) else whole)[at], bank[:, 0:width]).then_inc(prep_kept, 1)

                def step(pair, k, head, after, following):
                    if exists(pair, 2):
                        for q in range(2):
                            act.wait_ge(turn_ready, pair * 2 + (q - 3))
                            wait_for(act, pv_ready, pair - 3)
                            act.copy(prob_high[:, k % 2, :, q * P:(q + 1) * P],
                                     turn_bank[q][:].rearrange("p (n t) -> p n t", n=KT)).then_inc(high_done, 1)
                    if exists(pair, 0):
                        h, _, slot = head
                        for q in range(2):
                            unit, t = (2 * k + q) % 4, 2 * (k % BATCH) + q
                            act.wait_ge(shift_done, pair * 2 + (q + 1))
                            wait_for(act, turn_ready, pair * 2 + (q - 3))
                            wait_for(act, inverse_done, pair - 7)
                            act.activation(prob[:, unit, :], masked[:, unit, :], ACT.Exp, bias=shift[:, unit:unit + 1],
                                           scale=q_scale[:, slot, t:t + 1] if qk_norm else scale,
                                           accum_out=total[:, 2 * (k % 8) + q:2 * (k % 8) + q + 1]).then_inc(exp_done, 1)
                    if exists(pair, 3):
                        act.wait_ge(pv_ready, pair - 2)
                        wait_for(act, y_ready, pair - 4)
                        of = (k - 3) % BATCH
                        if qk_norm:
                            last = act.copy(o_high[:, (k - 3) % 2, :], o_bank[:, 0:2 * P])
                        else:
                            last = act.activation(o_high[:, (k - 3) % 2, :], o_bank[:, 0:2 * P], ACT.Copy,
                                                  scale=valid[:, of:of + 1])
                        last.then_inc(o_high_done, 1)
                    for piece in after:
                        prepare(piece, following)

                walk(act, prepare, step, None if qk_norm else norm.scalar)

            @block.vector
            def _(dve):
                def prepare(piece, head):
                    h, turn, slot = head
                    if is_head(h, 0):
                        n = pieces.index(piece)
                        high, low, _ = parts_of[piece]
                        at, width = place(piece, slot)
                        dve.wait_ge(prep_kept, n + 1)
                        dve.tensor_tensor(low[at], prep_bank[n % 2][:, 0:width], high[at].bitcast(F32),
                                          ALU.subtract).then_inc(split_done, 1)

                def set_up_masks(dve):
                    dve.wait_ge(side_loaded, 16)
                    dve.tensor_scalar(side[:, 0, :], mask_u8[:], 1.0, MASKED, ALU.subtract, ALU.mult)
                    dve.tensor_reduce(valid[:], mask_u8[:].rearrange("p (b s) -> p b s", b=BATCH), AX_X,
                                      ALU.max).then_inc(set_up, 1)

                def step(pair, k, head, after, following):
                    b = k % BATCH
                    if exists(pair, 0):
                        h, turn, slot = head
                        if qk_norm and b == 0:
                            dve.wait_ge(rms_loaded[slot], turn * 16 + 16)
                            dve.wait_ge(q_scale_done, h + 1)
                        for q in range(2):
                            unit, t = (2 * k + q) % 4, 2 * b + q
                            dve.wait_ge(scores_ready, pair * 2 + (q + 1))
                            wait_for(dve, exp_done, pair * 2 + (q - 3))
                            dve.memset(woken[:], 0.0)
                            dve.tensor_tensor_reduce(masked[:, unit, :], score_bank[q][:],
                                                     side[:, slot if qk_norm else 0, b * KEYS:(b + 1) * KEYS], 1.0, LOWEST,
                                                     ALU.mult if qk_norm else ALU.add, ALU.max,
                                                     top[:, unit:unit + 1]).then_inc(top_done, 1)
                            dve.wait_ge(top_done, pair * 2 + (q + 1))
                            if qk_norm:
                                dve.scalar_tensor_tensor(shift[:, unit:unit + 1], top[:, unit:unit + 1], -1.0,
                                                         q_scale[:, slot, t:t + 1], ALU.mult,
                                                         ALU.mult).then_inc(shift_done, 1)
                            else:
                                dve.tensor_scalar(shift[:, unit:unit + 1], top[:, unit:unit + 1], -scale, None,
                                                  ALU.mult).then_inc(shift_done, 1)
                    if exists(pair, 4):
                        old, at = k % BATCH, k % 2 * 2
                        wait_for(dve, x_added, pair * 2 - 10)
                        dve.wait_ge(exp_done, pair * 2 - 6)
                        dve.reciprocal(inverse[:, at:at + 2], total[:, (k - 4) % 8 * 2:(k - 4) % 8 * 2 + 2]
                                       ).then_inc(inverse_done, 1)
                    if exists(pair, 2):
                        for q in range(2):
                            dve.wait_ge(high_done, pair * 2 + (q - 3))
                            part = (slice(None), k % 2, slice(None), slice(q * P, (q + 1) * P))
                            dve.tensor_tensor(prob_low[part], turn_bank[q][:].rearrange("p (n t) -> p n t", n=KT),
                                              prob_high[part].bitcast(F32), ALU.subtract).then_inc(turn_kept, 1)
                    if exists(pair, 3):
                        dve.wait_ge(o_high_done, pair - 2)
                        held, of = (k - 3) % 2, (k - 3) % BATCH
                        high = o_high[:, held, :].bitcast(F32)
                        if qk_norm:
                            last = dve.tensor_tensor(o_low[:, held, :], o_bank[:, 0:2 * P], high, ALU.subtract)
                        else:
                            last = dve.scalar_tensor_tensor(o_low[:, held, :], o_bank[:, 0:2 * P], valid[:, of:of + 1], high,
                                                            ALU.mult, ALU.subtract)
                        last.then_inc(o_kept, 1)
                    if exists(pair, 4):
                        dve.wait_ge(y_ready, pair - 3)
                        dve.wait_ge(inverse_done, pair - 3)
                        for q in range(2):
                            tile = m.x[:, 2 * old + q, :]
                            dve.scalar_tensor_tensor(tile, y_bank[:, q * D:(q + 1) * D], inverse[:, at + q:at + q + 1], tile,
                                                     ALU.mult, ALU.add).then_inc(x_added, 1)

                if qk_norm:
                    dve.wait_ge(gain_loaded, 32)
                    dve.tensor_tensor(gains[:], gain[:, 0:1], gain[:, 1:2], ALU.mult).then_inc(set_up, 1)
                else:
                    norm.vector(dve)
                walk(dve, prepare, step, None if qk_norm else set_up_masks)

            @block.gpsimd
            def _(pool):
                def gain_weights(h, turn, slot):
                    pool.wait_ge(w_loaded[slot], turn * 64 + 64)
                    pool.tensor_tensor(wk_gained[:, slot, :], wk[:, slot, :], gains[:].broadcast_to([P, CW]),
                                       ALU.mult).then_inc(gained, 1)
                    wait_for(pool, exp_done, h * (2 * BATCH) - 2 * BATCH)
                    at = bass.ds(h * TT, TT)
                    pool.tensor_copy(q_scale[:, slot, :], m.q_rms[:, at]).then_inc(q_scale_done, 1)

                def prepare(piece, head):
                    h, turn, slot = head
                    if not is_head(h, 0):
                        number = h * n_pieces + pieces.index(piece)
                        high, low, whole = parts_of[piece]
                        at, _ = place(piece, slot)
                        if is_head(h, 1) and piece == "a":
                            pool.wait_ge(split_done, n_pieces)
                        pool.wait_ge(prep_kept, number + 1)
                        pool.tensor_tensor(pool_woken[:], m.ones[:, 0:1], m.ones[:, 0:1], ALU.mult)
                        pool.tensor_copy(high[at], whole[at]).then_inc(own_high, 1)
                        pool.wait_ge(own_high, number + (1 - n_pieces))
                        pool.tensor_tensor(low[at], whole[at], high[at].bitcast(F32), ALU.subtract).then_inc(split_done, 1)
                    if qk_norm and piece == "wvo" and not is_head(h, HEADS - 1):
                        gain_weights(h + 1, turn + slot, 1 - slot)

                def step(pair, k, head, after, following):
                    for piece in after:
                        prepare(piece, following)

                if qk_norm:
                    pool.wait_ge(set_up, 1)
                    gain_weights(0, 0, 0)
                else:
                    norm.gpsimd(pool)
                walk(pool, prepare, step)


H0 = 16
GROUP = 2
GROUPS = HEADS // GROUP
V0 = 32
SHARES = 4
LAST_KEYS = 16


def small_project_stage(nc, m, dram):
    steps = (TT + BATCH * KT) // 2
    query_steps = TT // 2
    eps = 1e-6
    rows = 2 * HEADS
    common, w_loads, gain_loads = P - LAST_KEYS, 7, 12
    with Stage(nc, m, "l0p") as st:
        wq = st.sbuf("wq", [P, DC, D])
        wkv = st.sbuf("wkv", [CW, 2 * D])
        wkv_last = st.sbuf("wkv_last", [CW, 2 * D])
        bq = st.sbuf("bq", [P, D])
        bkv = st.sbuf("bkv", [P, 2, 2 * D])
        sums = st.sbuf("sums", [P, 2 * HEADS])
        gain = st.sbuf("gain", [P, 5, H0])
        offset = st.sbuf("offset", [P, 5, H0])
        ctx_t = st.sbuf("ctx_t", [CW, BATCH * KEYS])
        ctx_common = st.sbuf("ctx_common", [CW, BATCH, P])
        ctx_last = st.sbuf("ctx_last", [CW, BATCH, P])
        head = st.sbuf("head", [P, 4, rows, H0])
        squares = st.sbuf("squares", [P, 2, rows, H0])
        variance = st.sbuf("variance", [P, 2, rows])
        root = st.sbuf("root", [P, 2, rows])
        rstd = st.sbuf("rstd", [P, 2, rows])
        eps_column = st.sbuf("eps_column", [P, 1])
        parts = st.sbuf("parts", [P, 2, rows, SHARES, H0], F32R)
        project_bank = st.banks("project", 4)
        turn_bank = st.banks("turn", 4)
        norm = Norm(st, m, turn_bank[0:2], whole=True)
        (w_loaded, loaded, ctx_loaded, own, centred_done, cleared, shares_set, projected, head_done, v_done, squares_done,
         variance_done, root_done, rstd_done, scaled, gained, normed, high_done, low_done, turned, kept) = st.sems(
            "w_loaded", "loaded", "ctx_loaded", "own", "centred_done", "cleared", "shares_set", "projected", "head_done",
            "v_done", "squares_done", "variance_done", "root_done", "rstd_done", "scaled", "gained", "normed",
            "high_done", "low_done", "turned", "kept")

        def per_row(a):
            return a.rearrange("p (h a) -> p h a", a=1).broadcast_to([P, a.shape[-1], H0])

        with st.block() as block:

            @block.sync
            def _(sp):
                sp.dma_start(wq[:], dram["wq"].rearrange("(c p) n -> p c n", p=P)).then_inc(w_loaded, 16)
                sp.dma_start(wkv[:], dram["wkv"]).then_inc(w_loaded, 16)
                sp.dma_start(wkv_last[:], dram["wkv_last"]).then_inc(w_loaded, 16)
                sp.dma_start(bq[:], dram["bq"].partition_broadcast(P)).then_inc(w_loaded, 16)
                sp.dma_start(bkv[:, 0, :], dram["bkv"].partition_broadcast(P)).then_inc(w_loaded, 16)
                sp.dma_start(bkv[0:common, 1, :], dram["bkv"].partition_broadcast(common)).then_inc(w_loaded, 16)
                sp.dma_start(bkv[common:P, 1, :], dram["bkv_last"].partition_broadcast(LAST_KEYS)).then_inc(w_loaded, 16)
                for to, q, k, last in ((gain, "qn_w", "kn_w", "kn_dca_w"), (offset, "qn_b", "kn_b", "kn_dca_b")):
                    for n, w in enumerate((q, q, k, k)):
                        sp.dma_start(to[:, n, :], dram[w].partition_broadcast(P)).then_inc(loaded, 16)
                    sp.dma_start(to[0:common, 4, :], dram[k].partition_broadcast(common)).then_inc(loaded, 16)
                    sp.dma_start(to[common:P, 4, :], dram[last].partition_broadcast(LAST_KEYS)).then_inc(loaded, 16)

            @block.scalar
            def _(act):
                act.dma_start(ctx_t[:], dram["ctx_t"]).then_inc(ctx_loaded, 16)
                norm.scalar(act)

                def split(s):
                    high = parts[:, s % 2, :, 0:2, :] if s < query_steps else parts[:, s % 2, :, 0:4:2, :]
                    act.wait_ge(normed, s + 1)
                    wait_for(act, turned, s - 1)
                    act.copy(high, head[:, s % 4, :, :].rearrange("p h (a d) -> p h a d", a=1).broadcast_to(
                        [P, rows, 2, H0])).then_inc(high_done, 1)

                def keep(s):
                    act.wait_ge(turned, s + 1)
                    for j in range(2):
                        to, per_batch, at = ((m.q0_t, TT // BATCH, 2 * s + j) if s < query_steps else
                                             (m.k0_t, KT, 2 * s + j - TT))
                        b, n = divmod(at, per_batch)
                        for half in range(2):
                            first = b * GROUPS + half * (GROUPS // 2)
                            last = act.copy(to[:, first:first + GROUPS // 2, n * P:(n + 1) * P],
                                            turn_bank[2 * j + half][:].rearrange("p (g q) -> p g q", g=GROUPS // 2))
                    last.then_inc(kept, 1)

                act.wait_ge(cleared, 1)
                for s in range(steps + 3):
                    if s < steps:
                        act.wait_ge(head_done, s + 1)
                        wait_for(act, variance_done, s - 1)
                        act.activation(squares[:, s % 2, :, :], head[:, s % 4, :, :], ACT.Square).then_inc(squares_done, 1)
                    if s >= 3:
                        split(s - 3)
                    if s < steps:
                        act.wait_ge(variance_done, s + 1)
                        wait_for(act, rstd_done, s - 1)
                        act.activation(root[:, s % 2, :], variance[:, s % 2, :], ACT.Sqrt, bias=eps_column[:],
                                       scale=1.0 / H0).then_inc(root_done, 1)
                    if s >= 4:
                        keep(s - 4)
                keep(steps - 1)

            @block.gpsimd
            def _(pool):
                pool.memset(eps_column[:], eps).then_inc(cleared, 1)
                pool.memset(ctx_common[:], 0.0).then_inc(cleared, 1)
                pool.memset(ctx_last[:], 0.0).then_inc(cleared, 1)
                norm.gpsimd(pool)
                pool.wait_ge(cleared, 3)
                pool.wait_ge(ctx_loaded, 16)
                last_tiles = ctx_t[:].rearrange("c (b n q) -> c b n q", b=BATCH, n=KT)[:, :, KT - 1, :]
                pool.tensor_copy(ctx_common[:, :, 0:common], last_tiles[:, :, 0:common]).then_inc(shares_set, 1)
                pool.tensor_copy(ctx_last[:, :, common:P], last_tiles[:, :, common:P]).then_inc(shares_set, 1)
                pool.wait_ge(loaded, 16 * gain_loads)
                for s in range(steps):
                    kind = 0 if s < query_steps else 2 + s % 2
                    rows_of = head[:, s % 4, :, :].rearrange("p (t h) d -> p t h d", t=2)

                    def of_tiles(a):
                        return a[:, kind:kind + 2, :].rearrange("p t (a d) -> p t a d", a=1).broadcast_to([P, 2, HEADS, H0])

                    pool.wait_ge(scaled, s + 1)
                    pool.tensor_tensor(rows_of, rows_of, of_tiles(gain), ALU.mult).then_inc(gained, 1)
                    pool.wait_ge(gained, s + 1)
                    pool.tensor_tensor(rows_of, rows_of, of_tiles(offset), ALU.add).then_inc(normed, 1)

            @block.tensor
            def _(pe):
                norm.tensor(pe)
                norm.ready(pe)
                pe.wait_ge(centred_done, 1)
                pe.wait_ge(shares_set, 2)

                def project(s):
                    wait_for(pe, head_done, s - 1)
                    if s - 2 >= query_steps:
                        pe.wait_ge(v_done, s - 1 - query_steps)
                    for j in range(2):
                        i, bank = 2 * s + j, project_bank[s % 2 * 2 + j]
                        if i < TT:
                            for c in range(DC):
                                last = pe.matmul(bank[:, 0:D], m.x_t[:, c, i * P:(i + 1) * P], wq[:, c, :],
                                                 start=(c == 0), stop=(c == DC - 1))
                        elif (i - TT) % KT == KT - 1:
                            b = (i - TT) // KT
                            pe.matmul(bank[:], ctx_common[:, b, :], wkv[:], start=True, stop=False)
                            last = pe.matmul(bank[:], ctx_last[:, b, :], wkv_last[:], start=False, stop=True)
                        else:
                            last = pe.matmul(bank[:], ctx_t[:, (i - TT) * P:(i - TT + 1) * P], wkv[:], start=True, stop=True)
                    last.then_inc(projected, 1)

                def turn(s):
                    pe.wait_ge(low_done, s + 1)
                    wait_for(pe, kept, s)
                    heads = 2 * GROUPS // 4 * GROUP
                    for n in range(4):
                        for g in range(GROUPS // 2):
                            first = n * heads + g * GROUP
                            last = pe.transpose(turn_bank[n][:, g * P:(g + 1) * P],
                                                parts[:, s % 2, first:first + GROUP, :, :].bitcast(F32).rearrange(
                                                    "p h a d -> p (h a d)"), m.ident[:])
                    last.then_inc(turned, 1)

                project(0)
                for s in range(steps + 3):
                    if s + 1 < steps:
                        project(s + 1)
                    if s >= 3:
                        turn(s - 3)

            @block.vector
            def _(dve):
                links = 0

                def link(instruction):
                    nonlocal links
                    links += 1
                    instruction.then_inc(own, 1)
                    dve.wait_ge(own, links)

                norm.vector(dve)
                dve.wait_ge(w_loaded, 16 * w_loads)
                for w in [wq[:].rearrange("p c (h d) -> p (c h) d", d=H0), bq[:].rearrange("p (h d) -> p h d", d=H0)] + [
                        w.rearrange("p (h a d) -> p h a d", h=HEADS, a=2)[:, :, 0, :]
                        for w in (wkv[:], wkv_last[:], bkv[:, 0, :], bkv[:, 1, :])]:
                    n = w.shape[1]
                    link(dve.tensor_reduce(sums[:, 0:n], w, AX_X, ALU.add))
                    last = dve.scalar_tensor_tensor(w, per_row(sums[:, 0:n]), -1.0 / H0, w, ALU.mult, ALU.add)
                    link(last)
                dve.memset(sums[:], 0.0).then_inc(centred_done, 1)

                def biased(s):
                    for j in range(2):
                        i, bank = 2 * s + j, project_bank[s % 2 * 2 + j]
                        to = head[:, s % 4, j * HEADS:(j + 1) * HEADS, :]
                        if i < TT:
                            last = dve.tensor_tensor(to, bank[:, 0:D].rearrange("p (h d) -> p h d", h=HEADS),
                                                     bq[:].rearrange("p (h d) -> p h d", h=HEADS), ALU.add)
                        else:
                            kinds = [a.rearrange("p (h a d) -> p h a d", h=HEADS, a=2)
                                     for a in (bank[:], bkv[:, int((i - TT) % KT == KT - 1), :])]
                            last = dve.tensor_tensor(to, kinds[0][:, :, 0, :], kinds[1][:, :, 0, :], ALU.add)
                    last.then_inc(head_done, 1)
                    if s >= query_steps:
                        for j in range(2):
                            i, bank = 2 * s + j, project_bank[s % 2 * 2 + j]
                            b, n = divmod(i - TT, KT)
                            kinds = [a.rearrange("p (g h a d) -> p g h a d", g=GROUPS, h=GROUP, a=2)[:, :, :, 1, :]
                                     for a in (bank[:], bkv[:, int(n == KT - 1), :])]
                            last = dve.tensor_tensor(m.v0[:, b * GROUPS:(b + 1) * GROUPS, n, :].rearrange(
                                "p g (h d) -> p g h d", h=GROUP), kinds[0], kinds[1], ALU.add)
                        last.then_inc(v_done, 1)

                def added(s):
                    dve.wait_ge(squares_done, s + 1)
                    wait_for(dve, root_done, s - 1)
                    dve.tensor_reduce(variance[:, s % 2, :], squares[:, s % 2, :, :], AX_X, ALU.add).then_inc(variance_done, 1)

                def scale(s):
                    dve.wait_ge(root_done, s + 1)
                    dve.reciprocal(rstd[:, s % 2, :], root[:, s % 2, :]).then_inc(rstd_done, 1)
                    dve.wait_ge(rstd_done, s + 1)
                    h = head[:, s % 4, :, :]
                    dve.tensor_tensor(h, h, per_row(rstd[:, s % 2, :]), ALU.mult).then_inc(scaled, 1)

                def split(s):
                    dve.wait_ge(high_done, s + 1)
                    of = parts[:, s % 2, :, :, :]
                    high, low = (of[:, :, 0:2, :], of[:, :, 2:4, :]) if s < query_steps else (of[:, :, 0:4:2, :], of[:, :, 1:4:2, :])
                    dve.tensor_tensor(low, head[:, s % 4, :, :].rearrange("p h (a d) -> p h a d", a=1).broadcast_to(
                        [P, rows, 2, H0]), high.bitcast(F32), ALU.subtract).then_inc(low_done, 1)

                for s in range(steps + 3):
                    if s < steps:
                        dve.wait_ge(projected, s + 1)
                        wait_for(dve, low_done, s - 3)
                        biased(s)
                    if s < steps:
                        added(s)
                    if 1 <= s <= steps:
                        scale(s - 1)
                    if s >= 3:
                        split(s - 3)


def small_attention_stage(nc, m, output):
    scale = float(H0) ** -0.5
    cut = KEYS - LAST_KEYS
    parts = ((0, cut), (cut, KEYS))
    lag, slots = 5, 4
    turns = BATCH * GROUPS // slots
    width = SHARES * H0
    with Stage(nc, m, "l0a") as st:
        q_t = st.sbuf("q_t", [P, slots, 2 * P], F32R)
        k_t = st.sbuf("k_t", [P, slots, KEYS], F32R)
        v = st.sbuf("v", [P, slots, KT, GROUP, V0])
        top = st.sbuf("top", [P, 4, 2, 2])
        shift = st.sbuf("shift", [P, 4, 2, 2])
        total = st.sbuf("total", [P, 4, 2, 2])
        inverse = st.sbuf("inverse", [P, 4, 2, 2])
        prob = st.sbuf("prob", [P, 4, 2, KEYS])
        prob_t = st.sbuf("prob_t", [P, 2, KT, 2 * P])
        score_bank = st.banks("score", 4)
        turn_bank = st.banks("turn", 2)
        o_bank = st.banks("o", 2)
        (staged, scores_ready, top_done, shift_done, exp_done, inverse_done, prob_done, last_done, turn_ready, pv_ready,
         o_kept, cleared) = st.sems("staged", "scores_ready", "top_done", "shift_done", "exp_done", "inverse_done", "prob_done",
                           "last_done", "turn_ready", "pv_ready", "o_kept", "cleared")
        turn_kept, v_staged = st.sems("turn_kept", "v_staged")

        def walk(engine, step):
            def four_groups(i, last=False):
                for k in range(slots * GROUP):
                    slot = k // GROUP + 2
                    following = None if last and slot >= slots else (i + slot // slots, slot % slots)
                    step(i * (slots * GROUP) + k, k, i, following)

            four_groups(0)
            with engine.Fori(1, turns - 1) as i:
                four_groups(i)
            four_groups(turns - 1, True)
            for k in range(lag):
                step(PAIRS + k, k, turns, None)

        def exists(pair, back):
            return not isinstance(pair, int) or 0 <= pair - back < PAIRS

        with st.block() as block:

            @block.sync
            def _(sp):
                output.load(sp)

            @block.gpsimd
            def _(pool):
                def stage(turn, slot):
                    group = turn * slots + slot
                    wait_for(pool, scores_ready, turn * (slots * GROUP * 2) + (slot - slots + 1) * GROUP * 2)
                    pool.tensor_copy(q_t[:, slot, :], m.q0_t[:, group, :]).then_inc(staged, 1)
                    pool.tensor_copy(k_t[:, slot, :], m.k0_t[:, group, :]).then_inc(staged, 1)

                def stage_v(turn, slot):
                    group = turn * slots + slot
                    wait_for(pool, pv_ready, turn * (slots * GROUP) + (slot - slots + 1) * GROUP)
                    pool.tensor_copy(v[:, slot, :, :, 0:H0], m.v0[:, group, :, :].rearrange(
                        "p n (j d) -> p n j d", j=GROUP)).then_inc(v_staged, 1)

                def step(pair, k, turn, following):
                    if exists(pair, 2):
                        at = (k - 2) % 4
                        pool.wait_ge(inverse_done, pair - 1)
                        last_keys = prob[:, at, :, cut:]
                        pool.tensor_tensor(last_keys, last_keys, inverse[:, at, :, 1:2].broadcast_to([P, 2, LAST_KEYS]),
                                           ALU.mult).then_inc(last_done, 1)
                    if exists(pair, 0) and k % GROUP == 0:
                        stage_v(turn, k // GROUP)
                    elif following is not None:
                        stage(*following)

                pool.memset(v[:], 0.0).then_inc(cleared, 1)
                pool.wait_ge(cleared, 1)
                pool.wait_ge(staged, 4)
                walk(pool, step)

            @block.tensor
            def _(pe):
                def step(pair, k, turn, following):
                    if exists(pair, 0):
                        slot, j = k // GROUP, k % GROUP
                        if j == 0:
                            pe.wait_ge(staged, turn * (2 * slots) + (2 * slot + 2))
                        rows = slice(width * j, width * (j + 1))
                        for q in range(2):
                            wait_for(pe, exp_done, pair * 2 + (q - 3))
                            pe.matmul(score_bank[k % 2 * 2 + q][:], q_t[rows, slot, q * P:(q + 1) * P], k_t[rows, slot, :],
                                      start=True, stop=True).then_inc(scores_ready, 1)
                    if exists(pair, 5):
                        old = (k - 5) % (slots * GROUP)
                        slot, j = old // GROUP, old % GROUP
                        if j == 0:
                            pe.wait_ge(v_staged, turn * slots + ((k - 5) // GROUP + 1))
                        quad = slot // 2
                        if old % 4 == 0:
                            wait_for(pe, o_kept, turn * (slots // 2) + ((k - 5) // 4 - 1))
                        pe.wait_ge(turn_kept, pair * 2 - 8)
                        to = old % 4 * V0
                        for n in range(KT):
                            last = pe.matmul(o_bank[quad][to:to + V0, 0:2 * P], v[:, slot, n, j, :], prob_t[:, (k - 5) % 2, n, :],
                                             start=(n == 0), stop=(n == KT - 1), tile_position=(0, to))
                        last.then_inc(pv_ready, 1)
                    if exists(pair, 3):
                        pe.wait_ge(last_done, pair - 2)
                        for q in range(2):
                            pe.wait_ge(prob_done, pair * 2 + (q - 5))
                            wait_for(pe, turn_kept, pair * 2 + (q - 7))
                            for n in range(KT):
                                last = pe.transpose(turn_bank[q][:, n * P:(n + 1) * P],
                                                    prob[:, (k - 3) % 4, q, n * P:(n + 1) * P], m.ident[:])
                            last.then_inc(turn_ready, 1)

                walk(pe, step)

            @block.scalar
            def _(act):
                def step(pair, k, turn, following):
                    if exists(pair, 4):
                        for q in range(2):
                            act.wait_ge(turn_ready, pair * 2 + (q - 7))
                            wait_for(act, pv_ready, pair - 5)
                            act.copy(prob_t[:, k % 2, :, q * P:(q + 1) * P],
                                     turn_bank[q][:].rearrange("p (n t) -> p n t", n=KT)).then_inc(turn_kept, 1)
                    if exists(pair, 1):
                        at = (k - 1) % 4
                        for q in range(2):
                            act.wait_ge(shift_done, pair)
                            wait_for(act, turn_ready, pair * 2 + (q - 9))
                            wait_for(act, prob_done, pair * 2 - 8)
                            for part, (first, end) in enumerate(parts):
                                last = act.activation(prob[:, at, q, first:end], score_bank[at % 2 * 2 + q][:, first:end], ACT.Exp,
                                                      bias=shift[:, at, q, part:part + 1], scale=scale,
                                                      accum_out=total[:, at, q, part:part + 1])
                            last.then_inc(exp_done, 1)
                    if exists(pair, 5) and (k - 5) % 4 == 3:
                        back = (k - 5) // 4
                        act.wait_ge(pv_ready, pair - 4)
                        act.copy(m.o0[:, turn * (slots // 2) + back, :], o_bank[back % 2][:, 0:2 * P]).then_inc(o_kept, 1)

                walk(act, step)

            @block.vector
            def _(dve):
                def step(pair, k, turn, following):
                    if exists(pair, 0):
                        at = k % 4
                        for q in range(2):
                            dve.wait_ge(scores_ready, pair * 2 + (q + 1))
                            for part, (first, end) in enumerate(parts):
                                last = dve.tensor_reduce(top[:, at, q, part:part + 1], score_bank[k % 2 * 2 + q][:, first:end],
                                                         AX_X, ALU.max)
                        last.then_inc(top_done, 1)
                        wait_for(dve, exp_done, pair * 2 - 6)
                        dve.wait_ge(top_done, pair + 1)
                        dve.tensor_scalar(shift[:, at, :, :], top[:, at, :, :], -scale, None, ALU.mult).then_inc(shift_done, 1)
                    if exists(pair, 2):
                        at = (k - 2) % 4
                        wait_for(dve, last_done, pair - 5)
                        dve.wait_ge(exp_done, pair * 2 - 2)
                        dve.reciprocal(inverse[:, at, :, :], total[:, at, :, :]).then_inc(inverse_done, 1)
                        dve.wait_ge(inverse_done, pair - 1)
                        for q in range(2):
                            common = prob[:, at, q, 0:cut]
                            dve.tensor_scalar(common, common, inverse[:, at, q, 0:1], None, ALU.mult).then_inc(prob_done, 1)

                for group in range(2):
                    dve.tensor_copy(q_t[:, group, :], m.q0_t[:, group, :]).then_inc(staged, 1)
                    dve.tensor_copy(k_t[:, group, :], m.k0_t[:, group, :]).then_inc(staged, 1)
                walk(dve, step)


class OutputWeights:

    def __init__(self, st, dram):
        self.dram = dram
        self.wo = st.sbuf("wo", [P, HEADS // 4, D])
        self.bo = st.sbuf("bo", [P, D])
        self.wo_loaded, self.bo_loaded = st.sems("wo_loaded", "bo_loaded")

    def load(self, sp):
        sp.dma_start(self.wo[:], self.dram["wo"].rearrange("c p n -> p c n")).then_inc(self.wo_loaded, 16)
        sp.dma_start(self.bo[:], self.dram["bo"].partition_broadcast(P)).then_inc(self.bo_loaded, 16)


def small_output_stage(st, m, output):
    quads = HEADS // 4
    y_bank = st.banks("y", 4)
    y_ready, x_added, biased = st.sems("y_ready", "x_added", "biased")

    with st.block() as block:

        @block.tensor
        def _(pe):
            pe.wait_ge(output.wo_loaded, 16)
            for t in range(TT):
                b, q = divmod(t, TT // BATCH)
                wait_for(pe, x_added, t - 3)
                for c in range(quads):
                    last = pe.matmul(y_bank[t % 4][:, 0:D], m.o0[:, b * quads + c, q * P:(q + 1) * P], output.wo[:, c, :],
                                     start=(c == 0), stop=(c == quads - 1))
                last.then_inc(y_ready, 1)

        @block.gpsimd
        def _(pool):
            pool.wait_ge(output.bo_loaded, 16)
            for t in range(TT):
                pool.tensor_tensor(m.x[:, t, :], m.x[:, t, :], output.bo[:], ALU.add).then_inc(biased, 1)

        @block.vector
        def _(dve):
            for t in range(TT):
                dve.wait_ge(biased, t + 1)
                dve.wait_ge(y_ready, t + 1)
                dve.tensor_tensor(m.x[:, t, :], m.x[:, t, :], y_bank[t % 4][:, 0:D], ALU.add).then_inc(x_added, 1)


def small_attention(nc, m, dram):
    with ExitStack() as stack:
        m.small_heads(stack)
        small_project_stage(nc, m, dram)
        st = stack.enter_context(Stage(nc, m, "l0o"))
        output = OutputWeights(st, dram)
        small_attention_stage(nc, m, output)
        small_output_stage(st, m, output)


HIDDEN0 = 1024


def sparse_ffn_stage(nc, m, dram):
    halves = HIDDEN0 // BANK
    chunks = HIDDEN0 // P
    fours = HIDDEN0 // 4
    lag = 2
    with Stage(nc, m, "l0f") as st:
        wg_high = st.sbuf("wg_high", [P, DC, HIDDEN0], F32R)
        wu_high = st.sbuf("wu_high", [P, DC, HIDDEN0], F32R)
        wg_low = st.sbuf("wg_low", [P, DC, HIDDEN0], F32R)
        wu_low = st.sbuf("wu_low", [P, DC, HIDDEN0], F32R)
        wd = st.sbuf("wd", [P, chunks, D])
        x_high = st.sbuf("x_high", [P, 2, DC, P], F32R)
        x_low = st.sbuf("x_low", [P, 2, DC, P], F32R)
        gate = st.sbuf("gate", [P, 2, HIDDEN0])
        h = st.sbuf("h", [P, 2, HIDDEN0])
        size = st.sbuf("size", [P, HIDDEN0])
        beats_near = st.sbuf("beats_near", [P, fours, 2], BF16)
        beats_far = st.sbuf("beats_far", [P, fours, 2], BF16)
        beats_across = st.sbuf("beats_across", [P, fours, 2], BF16)
        front = st.sbuf("front", [P, fours, 2], BF16)
        back = st.sbuf("back", [P, fours, 2], BF16)
        wins = st.sbuf("wins", [P, fours, 4], BF16)
        kept = st.sbuf("kept", [P, 2, HIDDEN0])
        wg, wu = kept, h
        assert DC == 2
        h_t = st.sbuf("h_t", [P, 2, chunks, P])
        gate_bank = st.banks("gate", halves)
        up_bank = st.banks("up", halves)
        turn_bank = st.banks("turn", 2)
        y_bank = st.banks("y", 2)
        norm = Norm(st, m, turn_bank, parts=True)
        context = Context(st, m, dram)
        (gate_loaded, up_loaded, down_loaded, w_high_done, w_low_done, staged, gate_ready, up_ready, gate_done, h_done,
         size_done, near_done, far_done, across_done, front_done, back_done,
         wins_done, kept_done, turned, turn_kept, y_ready, x_added) = st.sems(
            "gate_loaded", "up_loaded", "down_loaded", "w_high_done", "w_low_done", "staged", "gate_ready", "up_ready",
            "gate_done", "h_done", "size_done", "near_done", "far_done", "across_done",
            "front_done", "back_done", "wins_done", "kept_done", "turned", "turn_kept", "y_ready", "x_added")

        def walk(engine, step):
            for t in range(4):
                step(t, t % 2)
            with engine.Fori(2, TT // 2) as i:
                for k in range(2):
                    step(i * 2 + k, k)
            for k in range(lag):
                step(TT + k, k)

        def exists(t, behind):
            return not isinstance(t, int) or 0 <= t - behind < TT

        with st.block() as block:

            @block.sync
            def _(sp):
                sp.dma_start(wg[:], dram["w_gate"].rearrange("(c p) n -> p c n", p=P)).then_inc(gate_loaded, 16)
                sp.dma_start(wu[:], dram["w_up"].rearrange("(c p) n -> p c n", p=P)).then_inc(up_loaded, 16)
                sp.dma_start(wd[:], dram["w_down"].rearrange("(c p) n -> p c n", p=P)).then_inc(down_loaded, 16)
                context.sync(sp)

            @block.gpsimd
            def _(pool):
                def step(t, k):
                    if exists(t, 0):
                        wait_for(pool, up_ready, t * halves - halves)
                        pool.tensor_copy(x_high[:, k, :, :], m.x_high[:, :, bass.ds(t * P, P)]).then_inc(staged, 1)
                        pool.tensor_copy(x_low[:, k, :, :], m.x_low[:, :, bass.ds(t * P, P)]).then_inc(staged, 1)

                norm.gpsimd(pool)
                norm.ready(pool)
                walk(pool, step)
                context.gpsimd(pool)

            @block.tensor
            def _(pe):
                def step(t, k):
                    if exists(t, lag):
                        for half in range(2):
                            pe.wait_ge(kept_done, t - 1)
                            wait_for(pe, turn_kept, t * 2 + (half - 5))
                            for n in range(chunks // 2):
                                c = half * (chunks // 2) + n
                                last = pe.transpose(turn_bank[half][:, n * P:(n + 1) * P], kept[:, k, c * P:(c + 1) * P],
                                                    m.ident[:])
                            last.then_inc(turned, 1)
                    if exists(t, 0):
                        pe.wait_ge(staged, t * 2 + 2)
                        for n in range(halves):
                            columns = slice(n * BANK, (n + 1) * BANK)
                            for bank, w, ready, used in ((gate_bank[n], (wg_high, wg_low), gate_ready, gate_done),
                                                         (up_bank[n], (wu_high, wu_low), up_ready, h_done)):
                                wait_for(pe, used, t * halves + (n + 1 - halves))
                                for c in range(DC):
                                    high, low = w[0][:, c, columns], w[1][:, c, columns]
                                    pe.matmul(bank[:], x_high[:, k, c, :], high, start=(c == 0), stop=False)
                                    pe.matmul(bank[:], x_high[:, k, c, :], low, start=False, stop=False)
                                    last = pe.matmul(bank[:], x_low[:, k, c, :], high, start=False, stop=(c == DC - 1))
                                last.then_inc(ready, 1)
                    if exists(t, lag):
                        pe.wait_ge(turn_kept, t * 2 - 2)
                        wait_for(pe, x_added, t - 3)
                        for c in range(chunks):
                            last = pe.matmul(y_bank[k][:, 0:D], h_t[:, k, c, :], wd[:, c, :],
                                             start=(c == 0), stop=(c == chunks - 1))
                        last.then_inc(y_ready, 1)

                norm.tensor(pe)
                norm.ready(pe)
                pe.wait_ge(w_low_done, 2)
                pe.wait_ge(down_loaded, 16)
                walk(pe, step)

            @block.scalar
            def _(act):
                def step(t, k):
                    if exists(t, lag):
                        for half in range(2):
                            act.wait_ge(turned, t * 2 + (half - 3))
                            wait_for(act, y_ready, t - 3)
                            act.copy(h_t[:, k, half * (chunks // 2):(half + 1) * (chunks // 2), :],
                                     turn_bank[half][:].rearrange("p (n t) -> p n t", n=chunks // 2)).then_inc(turn_kept, 1)
                    if exists(t, 0):
                        for n in range(halves):
                            act.wait_ge(gate_ready, t * halves + (n + 1))
                            wait_for(act, h_done, t * halves + (n + 1 - 2 * halves))
                            act.activation(gate[:, k, n * BANK:(n + 1) * BANK], gate_bank[n][:], ACT.Silu).then_inc(gate_done, 1)
                        act.wait_ge(h_done, t * halves + halves)
                        wait_for(act, across_done, t * 2)
                        act.activation(size[:], h[:, k, :], ACT.Abs).then_inc(size_done, 1)

                norm.scalar(act)
                for of, loaded, to in ((wg, gate_loaded, wg_high), (wu, up_loaded, wu_high)):
                    act.wait_ge(loaded, 16)
                    act.copy(to[:], of[:]).then_inc(w_high_done, 1)
                walk(act, step)

            @block.vector
            def _(dve):
                s4 = size[:].rearrange("p (f e) -> p f e", e=4)

                def step(t, k):
                    if exists(t, 0):
                        for n in range(halves):
                            columns = slice(n * BANK, (n + 1) * BANK)
                            dve.wait_ge(gate_done, t * halves + (n + 1))
                            dve.wait_ge(up_ready, t * halves + (n + 1))
                            wait_for(dve, kept_done, t - 1)
                            dve.tensor_tensor(h[:, k, columns], gate[:, k, columns], up_bank[n][:], ALU.mult).then_inc(h_done, 1)
                        h4 = h[:, k, :].rearrange("p (f e) -> p f e", e=4)
                        k4 = kept[:, k, :].rearrange("p (f e) -> p f e", e=4)
                        dve.wait_ge(size_done, t + 1)
                        wait_for(dve, kept_done, t)
                        dve.tensor_tensor(beats_near[:], s4[:, :, 0:4:2], s4[:, :, 1:4:2], ALU.is_ge).then_inc(near_done, 1)
                        dve.tensor_tensor(beats_far[:], s4[:, :, 0:2], s4[:, :, 2:4], ALU.is_ge).then_inc(far_done, 1)
                        for e in range(2):
                            dve.tensor_tensor(beats_across[:, :, e], s4[:, :, e], s4[:, :, 3 - e], ALU.is_ge).then_inc(across_done, 1)
                        dve.wait_ge(near_done, t + 1)
                        dve.wait_ge(far_done, t + 1)
                        dve.wait_ge(across_done, t * 2 + 2)
                        dve.tensor_tensor(front[:], beats_far[:], beats_across[:], ALU.add).then_inc(front_done, 1)
                        for e in range(2):
                            dve.tensor_tensor(back[:, :, e], beats_far[:, :, e], beats_across[:, :, 1 - e], ALU.add).then_inc(back_done, 1)
                        dve.wait_ge(front_done, t + 1)
                        dve.wait_ge(back_done, t * 2 + 2)
                        dve.tensor_tensor(wins[:, :, 0], front[:, :, 0], beats_near[:, :, 0], ALU.add).then_inc(wins_done, 1)
                        dve.tensor_tensor(wins[:, :, 1], front[:, :, 1], beats_near[:, :, 0], ALU.subtract).then_inc(wins_done, 1)
                        dve.tensor_tensor(wins[:, :, 2], beats_near[:, :, 1], back[:, :, 0], ALU.subtract).then_inc(wins_done, 1)
                        dve.tensor_tensor(wins[:, :, 3], beats_near[:, :, 1], back[:, :, 1], ALU.add).then_inc(wins_done, 1)
                        dve.wait_ge(wins_done, t * 4 + 4)
                        dve.wait_ge(h_done, t * halves + halves)
                        wait_for(dve, turned, t * 2 - 2)
                        for e, (least, test) in enumerate(((2.0, ALU.is_ge), (1.0, ALU.is_ge), (0.0, ALU.is_ge), (1.0, ALU.is_le))):
                            last = dve.scalar_tensor_tensor(k4[:, :, e], wins[:, :, e], least, h4[:, :, e], test, ALU.mult)
                        last.then_inc(kept_done, 1)
                    if exists(t, lag):
                        dve.wait_ge(y_ready, t - 1)
                        dve.tensor_tensor(m.x[:, t - 2, :], m.x[:, t - 2, :], y_bank[k][:, 0:D], ALU.add).then_inc(x_added, 1)

                norm.vector(dve)
                for n, (of, high, low) in enumerate(((wg, wg_high, wg_low), (wu, wu_high, wu_low))):
                    dve.wait_ge(w_high_done, n + 1)
                    dve.tensor_tensor(low[:], of[:], high[:].bitcast(F32), ALU.subtract).then_inc(w_low_done, 1)
                walk(dve, step)


STEPS1 = 4
HIDDEN1 = 1024


def thought_stage(nc, m, dram):
    eps = 1e-6
    chunks = HIDDEN1 // P
    B = BATCH
    IN_GAMMA, IN_BETA, AGG_B, PN_GAMMA, PN_BETA, D2_B, BC_B = range(7)
    small_names = ("in_gamma", "in_beta", "agg_b", "pn_gamma", "pn_beta", "d2_b", "bc_b")
    GATE_B, OUT_GAMMA, OUT_BETA = range(3)
    wide_names = ("gate_b", "out_gamma", "out_beta")
    with Stage(nc, m, "l1f") as st:
        weights = {"agg_w": st.sbuf("agg_w", [P, DC, D]), "d1_w": st.sbuf("d1_w", [P, DC, HIDDEN1]),
                   "d2_w": st.sbuf("d2_w", [P, chunks, D]), "bc_w": st.sbuf("bc_w", [P, DC, D]),
                   "gate_w": st.sbuf("gate_w", [P, DC, D])}
        d1_b = st.sbuf("d1_b", [P, chunks])
        small = st.sbuf("small", [B, len(small_names), D])
        wide = st.sbuf("wide", [P, len(wide_names), D])
        pick = st.sbuf("pick", [B, B, P])
        last_x = st.sbuf("last_x", [B, D])
        thought = st.sbuf("thought", [B, D])
        stats = st.sbuf("stats", [B, 6])
        moments = st.sbuf("moments", [B, 2])
        spread = st.sbuf("spread", [B, 1])
        rstd = st.sbuf("rstd", [B, 1])
        rows = st.sbuf("rows", [B, D])
        rows_t = st.sbuf("rows_t", [P, DC, B])
        hidden = st.sbuf("hidden", [P, chunks, B])
        active = st.sbuf("active", [P, chunks, B])
        delta = st.sbuf("delta", [B, D])
        said = st.sbuf("said", [P, B, D])
        raw = st.sbuf("raw", [P, TT, D])
        gate = st.sbuf("gate", [P, TT, D])
        out = st.sbuf("out", [P, TT, D])
        out_stats = st.sbuf("out_stats", [P, TT, 6])
        out_moments = st.sbuf("out_moments", [P, TT, 2])
        out_spread = st.sbuf("out_spread", [P, TT])
        out_rstd = st.sbuf("out_rstd", [P, TT])
        turn_bank, = st.banks("turn", 1)
        hidden_bank, = st.banks("hidden", 1)
        row_bank, = st.banks("row", 1)
        said_bank = st.banks("said", 2)
        gate_bank = st.banks("gate", 2)
        norm = Norm(st, m, gate_bank, whole=True, keep=True)
        n_loads = len(weights) + len(small_names) + len(wide_names) + 2
        (loaded, last_loaded, own, spread_done, rstd_done, rows_set, turned, turn_kept, product_ready, product_read,
         hidden_ready, hidden_set, active_done, said_ready, said_kept, gate_ready, raw_done, gate_done, gated, offset_done,
         out_spread_done, out_rstd_done, gained) = st.sems(
            "loaded", "last_loaded", "own", "spread_done", "rstd_done", "rows_set", "turned", "turn_kept", "product_ready",
            "product_read", "hidden_ready", "hidden_set", "active_done", "said_ready", "said_kept", "gate_ready",
            "raw_done", "gate_done", "gated", "offset_done", "out_spread_done", "out_rstd_done", "gained")

        def step_tiles(n):
            return range(n * TT // STEPS1, (n + 1) * TT // STEPS1)

        def half(n):
            return slice(n * TT // 2, (n + 1) * TT // 2)

        with st.block() as block:

            @block.sync
            def _(sp):
                for name, to in weights.items():
                    sp.dma_start(to[:], dram[name].rearrange("(c p) n -> p c n", p=P)).then_inc(loaded, 16)
                for n, name in enumerate(wide_names):
                    sp.dma_start(wide[:, n, :], dram[name].partition_broadcast(P)).then_inc(loaded, 16)
                for n, name in enumerate(small_names):
                    sp.dma_start(small[:, n, :], dram[name].partition_broadcast(B)).then_inc(loaded, 16)
                sp.dma_start(d1_b[:], dram["d1_b"]).then_inc(loaded, 16)
                sp.dma_start(pick[:], dram["pick"]).then_inc(loaded, 16)
                sp.wait_ge(norm.xn_done, TT)
                sp.dma_start(last_x[:], m.x_n[P - 1:P, 1:TT:2, :]).then_inc(last_loaded, 16)

            @block.gpsimd
            def _(pool):
                norm.gpsimd(pool)
                for n in range(1 + STEPS1):
                    pool.wait_ge(spread_done, n + 1)
                    pool.tensor_tensor(rstd[:], spread[:], m.minus_half[0:B, 0:1], ALU.pow).then_inc(rstd_done, 1)
                pool.wait_ge(said_kept, 2)
                for t in range(TT):
                    pool.wait_ge(gate_done, t + 1)
                    pool.tensor_tensor(gate[:, t, :], gate[:, t, :], said[:, t * B // TT, :], ALU.mult).then_inc(gated, 1)
                for n in range(2):
                    pool.wait_ge(out_spread_done, n + 1)
                    pool.tensor_tensor(out_rstd[:, half(n)], out_spread[:, half(n)], m.minus_half[:, half(n)],
                                       ALU.pow).then_inc(out_rstd_done, 1)

            @block.tensor
            def _(pe):
                def turn(n):
                    pe.wait_ge(rows_set, n + 1)
                    for c in range(DC):
                        last = pe.transpose(turn_bank[:, c * B:(c + 1) * B], rows[:, c * P:(c + 1) * P], m.ident[0:B, 0:B])
                    last.then_inc(turned, 1)
                    pe.wait_ge(turn_kept, n + 1)

                def project(w):
                    for c in range(DC):
                        last = pe.matmul(row_bank[0:B, 0:D], rows_t[:, c, :], w[:, c, :], start=(c == 0), stop=(c == DC - 1))
                    last.then_inc(product_ready, 1)

                norm.tensor(pe)
                norm.ready(pe)
                pe.wait_ge(loaded, 16 * n_loads)

                def gate_products(of):
                    for t in of:
                        wait_for(pe, raw_done, t - 1)
                        for c in range(DC):
                            last = pe.matmul(gate_bank[t % 2][:, 0:D], m.x_t[:, c, t * P:(t + 1) * P],
                                             weights["gate_w"][:, c, :], start=(c == 0), stop=(c == DC - 1))
                        last.then_inc(gate_ready, 1)

                turn(0)
                project(weights["agg_w"])
                for n in range(STEPS1):
                    turn(1 + n)
                    for j in range(chunks):
                        for c in range(DC):
                            last = pe.matmul(hidden_bank[:, j * B:(j + 1) * B], weights["d1_w"][:, c, j * P:(j + 1) * P],
                                             rows_t[:, c, :], start=(c == 0), stop=(c == DC - 1))
                    last.then_inc(hidden_ready, 1)
                    pe.wait_ge(active_done, n + 1)
                    pe.wait_ge(product_read, n + 1)
                    for j in range(chunks):
                        last = pe.matmul(row_bank[0:B, 0:D], active[:, j, :], weights["d2_w"][:, j, :],
                                         start=(j == 0), stop=(j == chunks - 1))
                    last.then_inc(product_ready, 1)
                    gate_products(step_tiles(n))
                turn(1 + STEPS1)
                project(weights["bc_w"])
                pe.wait_ge(rows_set, 3 + STEPS1)
                for b in range(B):
                    last = pe.matmul(said_bank[b // 2][:, b % 2 * D:(b % 2 + 1) * D], pick[:, b, :], rows[:], start=True, stop=True)
                last.then_inc(said_ready, 1)

            @block.scalar
            def _(act):
                def keep_turn(n):
                    act.wait_ge(turned, n + 1)
                    act.copy(rows_t[:], turn_bank[:, 0:DC * B].rearrange("p (c b) -> p c b", c=DC)).then_inc(turn_kept, 1)

                norm.scalar(act)
                keep_turn(0)
                for n in range(STEPS1):
                    keep_turn(1 + n)
                    act.wait_ge(hidden_set, n + 1)
                    act.activation(active[:], hidden[:], ACT.Gelu).then_inc(active_done, 1)
                keep_turn(1 + STEPS1)
                for t in range(TT):
                    act.wait_ge(raw_done, t + 1)
                    act.activation(gate[:, t, :], raw[:, t, :], ACT.Sigmoid).then_inc(gate_done, 1)

            @block.vector
            def _(dve):
                links = 0

                def link(instruction):
                    nonlocal links
                    links += 1
                    instruction.then_inc(own, 1)
                    dve.wait_ge(own, links)

                def norm_rows(n, of, gamma, beta):
                    link(dve.bn_stats(stats[:], of[:]))
                    link(dve.bn_aggr(moments[:], stats[:]))
                    dve.tensor_scalar(spread[:], moments[:, 1:2], eps, None, ALU.add).then_inc(spread_done, 1)
                    dve.wait_ge(rstd_done, n + 1)
                    link(dve.tensor_scalar(rows[:], of[:], moments[:, 0:1], rstd[:], ALU.subtract, ALU.mult))
                    link(dve.tensor_tensor(rows[:], rows[:], small[:, gamma, :], ALU.mult))
                    dve.tensor_tensor(rows[:], rows[:], small[:, beta, :], ALU.add).then_inc(rows_set, 1)

                norm.vector(dve)
                dve.wait_ge(loaded, 16 * n_loads)

                def gate_sums(of):
                    for t in of:
                        dve.wait_ge(gate_ready, t + 1)
                        dve.tensor_tensor(raw[:, t, :], gate_bank[t % 2][:, 0:D], wide[:, GATE_B, :], ALU.add).then_inc(raw_done, 1)
                        dve.tensor_tensor(m.x[:, t, :], m.x[:, t, :], wide[:, OUT_BETA, :], ALU.add).then_inc(offset_done, 1)

                dve.wait_ge(last_loaded, 16)
                norm_rows(0, last_x, IN_GAMMA, IN_BETA)
                dve.wait_ge(product_ready, 1)
                product = dve.tensor_tensor(thought[:], row_bank[0:B, 0:D], small[:, AGG_B, :], ALU.add)
                product.then_inc(product_read, 1)
                dve.wait_ge(product_read, 1)
                for n in range(STEPS1):
                    norm_rows(1 + n, thought, PN_GAMMA, PN_BETA)
                    if n:
                        gate_sums(step_tiles(n - 1))
                    dve.wait_ge(hidden_ready, n + 1)
                    dve.tensor_tensor(hidden[:], hidden_bank[:, 0:chunks * B].rearrange("p (j b) -> p j b", j=chunks),
                                      d1_b[:].rearrange("p (j a) -> p j a", a=1).broadcast_to([P, chunks, B]),
                                      ALU.add).then_inc(hidden_set, 1)
                    dve.wait_ge(product_ready, n + 2)
                    dve.tensor_tensor(delta[:], row_bank[0:B, 0:D], small[:, D2_B, :], ALU.add).then_inc(product_read, 1)
                    dve.wait_ge(product_read, n + 2)
                    link(dve.tensor_tensor(thought[:], thought[:], delta[:], ALU.add))
                dve.tensor_copy(rows[:], thought[:]).then_inc(rows_set, 1)
                gate_sums(step_tiles(STEPS1 - 1))
                dve.wait_ge(product_ready, 2 + STEPS1)
                dve.tensor_tensor(rows[:], row_bank[0:B, 0:D], small[:, BC_B, :], ALU.add).then_inc(rows_set, 1)
                dve.wait_ge(said_ready, 1)
                for n in range(2):
                    dve.tensor_copy(said[:, 2 * n:2 * n + 2, :],
                                    said_bank[n][:].rearrange("p (b d) -> p b d", b=2)).then_inc(said_kept, 1)
                tiles_of = [range(TT)[half(n)] for n in range(2)]
                for n, tiles in enumerate(tiles_of):
                    for t in tiles:
                        dve.wait_ge(gated, t + 1)
                        last = dve.tensor_tensor(out[:, t, :], gate[:, t, :], m.x_n[:, t, :], ALU.add)
                    link(last)
                    for t in tiles:
                        last = dve.bn_stats(out_stats[:, t, :], out[:, t, :])
                    link(last)
                    for t in tiles:
                        last = dve.bn_aggr(out_moments[:, t, :], out_stats[:, t, :])
                    link(last)
                    dve.tensor_scalar(out_spread[:, half(n)], out_moments[:, half(n), 1], eps, None, ALU.add).then_inc(out_spread_done, 1)
                    for t in tiles:
                        dve.scalar_tensor_tensor(out[:, t, :], out[:, t, :], out_moments[:, t, 0:1], wide[:, OUT_GAMMA, :],
                                                 ALU.subtract, ALU.mult).then_inc(gained, 1)
                for n, tiles in enumerate(tiles_of):
                    dve.wait_ge(out_rstd_done, n + 1)
                    dve.wait_ge(offset_done, (n + 1) * TT // 2)
                    dve.wait_ge(gained, (n + 1) * TT // 2)
                    for t in tiles:
                        dve.scalar_tensor_tensor(m.x[:, t, :], out[:, t, :], out_rstd[:, t:t + 1], m.x[:, t, :], ALU.mult, ALU.add)
def route_stage(nc, m, dram, name, experts, chosen, capacity, weights):
    with Stage(nc, m, name) as st:
        pad = 8 - chosen
        gate_w = st.sbuf("gate_w", [P, DC, experts])
        before = st.sbuf("before", [P, 2, P], BF16)
        before_raw = st.sbuf("before_raw", [P, P])
        top = st.sbuf("top", [P, TT])
        total = st.sbuf("total", [P, TT])
        inverse = st.sbuf("inverse", [P, TT])
        logit = st.sbuf("logit", [P, TT, experts])
        prob = st.sbuf("prob", [P, TT, experts + pad])
        best = st.sbuf("best", [P, TT, 8])
        rest = st.sbuf("rest", [P, TT, experts + pad])
        mask = st.sbuf("mask", [P, TT, experts])
        mask_b = st.sbuf("mask_b", [P, TT, experts], BF16)
        share = st.sbuf("share", [P, TT, experts])
        logit_bank, = st.banks("logit", 1)
        place_bank, = st.banks("place", 1)
        turn_bank = st.banks("turn", 2)
        norm = Norm(st, m, turn_bank, whole=True, parts=True)
        loaded, logits_ready, own, shifted, exp_done, masked, places_ready, shares_done, turned = st.sems(
            "loaded", "logits_ready", "own", "shifted", "exp_done", "masked", "places_ready", "shares_done", "turned")
        wide = [P, TT, experts]

        def by_tile(a):
            return a.rearrange("p (t a) -> p t a", a=1).broadcast_to(wide)

        with st.block() as block:

            @block.sync
            def _(sp):
                sp.dma_start(gate_w[:], dram["gate_w"].rearrange("(c p) n -> p c n", p=P)).then_inc(loaded, 16)
                sp.dma_start(before_raw[:], dram["before"]).then_inc(loaded, 16)
                weights.sync_first(sp)

            @block.tensor
            def _(pe):
                def logits(t):
                    if t == 0:
                        pe.wait_ge(loaded, 32)
                    for c in range(DC):
                        last = pe.matmul(logit_bank[:, t * experts:(t + 1) * experts], m.x_t[:, c, t * P:(t + 1) * P],
                                         gate_w[:, c, :], start=(c == 0), stop=(c == DC - 1))
                    last.then_inc(logits_ready, 1)

                norm.tensor(pe, use=logits)
                norm.ready(pe)
                if capacity is not None:
                    pe.wait_ge(masked, 1)
                    for t in range(TT):
                        for s in range(t + 1):
                            last = pe.matmul(place_bank[:, t * experts:(t + 1) * experts], before[:, int(s < t), :],
                                             mask_b[:, s, :], start=(s == 0), stop=(s == t))
                    last.then_inc(places_ready, 1)
                pe.wait_ge(shares_done, 1)
                for t in range(TT):
                    bank, at = turn_bank[t * 2 // TT], t % (TT // 2) * P
                    last = pe.transpose(bank[0:experts, at:at + P], share[:, t, :], m.ident[:])
                last.then_inc(turned, 1)

            @block.scalar
            def _(act):
                norm.scalar(act)
                act.wait_ge(shifted, 1)
                act.activation(prob[:, :, 0:experts], logit[:], ACT.Exp).then_inc(exp_done, 1)
                weights.scalar_first(act)

            @block.gpsimd
            def _(pool):
                norm.gpsimd(pool)
                weights.gpsimd_first(pool)

            @block.vector
            def _(dve):
                norm.vector(dve)
                links = 0

                def link(instruction):
                    nonlocal links
                    links += 1
                    instruction.then_inc(own, 1)
                    dve.wait_ge(own, links)

                dve.wait_ge(loaded, 32)
                dve.tensor_copy(before[:, 0, :], before_raw[:])
                link(dve.memset(before[:, 1, :], 1.0))
                dve.wait_ge(logits_ready, TT)
                logits = logit_bank[:, 0:TT * experts].rearrange("p (t e) -> p t e", t=TT)
                link(dve.tensor_reduce(top[:], logits, AX_X, ALU.max))
                dve.tensor_tensor(logit[:], logits, by_tile(top[:]), ALU.subtract).then_inc(shifted, 1)
                dve.wait_ge(exp_done, 1)
                p = prob[:, :, 0:experts]
                link(dve.tensor_reduce(total[:], p, AX_X, ALU.add))
                link(dve.reciprocal(inverse[:], total[:]))
                link(dve.tensor_tensor(p, p, by_tile(inverse[:]), ALU.mult))
                for t in range(TT):
                    last = dve.max(best[:, t, :], prob[:, t, 0:experts])
                link(last)
                for n in range(pad):
                    dve.memset(best[:, :, chosen + n], -1.0 - n)
                    last = dve.memset(prob[:, :, experts + n], -1.0 - n)
                if pad:
                    link(last)
                for t in range(TT):
                    last = dve.match_replace(rest[:, t, :], best[:, t, :], prob[:, t, :], -9.0)
                link(last)
                link(dve.tensor_tensor(mask[:], rest[:, :, 0:experts], p, ALU.not_equal))
                link(dve.tensor_tensor(share[:], p, mask[:], ALU.mult))
                dve.tensor_copy(mask_b[:], mask[:]).then_inc(masked, 1)
                link(dve.tensor_reduce(total[:], share[:], AX_X, ALU.add))
                link(dve.reciprocal(inverse[:], total[:]))
                last = dve.tensor_tensor(share[:], share[:], by_tile(inverse[:]), ALU.mult)
                if capacity is not None:
                    link(last)
                    dve.wait_ge(places_ready, 1)
                    places = place_bank[:, 0:TT * experts].rearrange("p (t e) -> p t e", t=TT)
                    last = dve.scalar_tensor_tensor(share[:], places, float(capacity), share[:], ALU.is_lt, ALU.mult)
                last.then_inc(shares_done, 1)
                dve.wait_ge(turned, 1)
                for n in range(2):
                    at = slice(n * BANK, (n + 1) * BANK)
                    last = dve.tensor_copy(m.mix[0:experts, at], turn_bank[n][0:experts, :])
                link(last)
                for n in range(2):
                    at = slice(n * BANK, (n + 1) * BANK)
                    dve.tensor_tensor(m.mix[experts:2 * experts, at], turn_bank[n][0:experts, :], m.mix[0:experts, at].bitcast(F32),
                                      ALU.subtract)


class ExpertWeights:

    SLOTS = 4
    FIRST = 2

    def __init__(self, st, dram, gated, shared):
        width = 2 * D + P + D
        self.dram, self.gated, self.shared, self.width = dram, gated, shared, width
        self.raw = st.sbuf("raw", [P, self.SLOTS, width])
        self.high = st.sbuf("high", [P, self.SLOTS, width], F32R)
        self.low = st.sbuf("low", [P, self.SLOTS, width], F32R)
        self.loaded = [st.sem(f"w_loaded{n}") for n in range(self.SLOTS)]
        self.high_done, self.low_done = st.sems("w_high_done", "w_low_done")

    def used(self, is_shared):
        return self.width if self.gated or is_shared else 2 * D + P

    def load(self, sp, j, slot, is_shared):
        of, n = (self.dram["shared_w"], j) if is_shared else (self.dram["w"], j - self.shared)
        n_columns = self.used(is_shared)
        sp.dma_start(self.raw[:, slot, 0:n_columns], of[n]).then_inc(self.loaded[slot], 16)

    def keep_high(self, act, slot, turn, is_shared):
        n = self.used(is_shared)
        act.wait_ge(self.loaded[slot], turn * 16 + 16)
        act.copy(self.high[:, slot, 0:n], self.raw[:, slot, 0:n]).then_inc(self.high_done, 1)

    def keep_low(self, pool, j, slot, is_shared):
        pool.wait_ge(self.high_done, j + 1)
        parts = [slice(0, 2 * D)] + ([slice(2 * D + P, self.width)] if self.gated or is_shared else [])
        for at in parts:
            last = pool.tensor_tensor(self.low[:, slot, at], self.raw[:, slot, at], self.high[:, slot, at].bitcast(F32),
                                      ALU.subtract)
        last.then_inc(self.low_done, 1)

    def sync_first(self, sp):
        for j in range(self.SLOTS):
            self.load(sp, j, j, j < self.shared)

    def scalar_first(self, act):
        for j in range(self.FIRST):
            self.keep_high(act, j, 0, j < self.shared)

    def gpsimd_first(self, pool):
        for j in range(self.FIRST):
            self.keep_low(pool, j, j, j < self.shared)


def mixture(nc, m, dram, name, experts, chosen, capacity, tiles, gated, shared, out=None):
    with Stage(nc, m, name + "f") as st:
        weights = ExpertWeights(st, dram, gated, shared)
        route_stage(nc, m, dram, name + "r", experts, chosen, capacity, weights)
        experts_stage(st, m, weights, experts, tiles, gated, shared, out)


def experts_stage(st, m, weights, experts, tiles, gated, shared, out):
    halves = TOKENS // BANK
    slots = weights.SLOTS
    high, low = weights.high, weights.low
    gate = st.sbuf("gate", [P, halves, BANK])
    upped = st.sbuf("upped", [P, halves, BANK])
    h = st.sbuf("h", [P, halves, BANK])
    h_high = st.sbuf("h_high", [P, 2, TOKENS], F32R)
    h_low = st.sbuf("h_low", [P, 2, TOKENS], F32R)
    y_t = st.sbuf("y_t", [P, DC, TOKENS])
    y_bank = st.banks("y", DC * halves)
    hidden_bank = st.banks("hidden", halves)
    up_bank, mix_bank = st.banks("up", 1) + st.banks("mix", 1)
    (hidden_ready, up_ready, mix_ready, gate_done, up_done, h_done, high_done, low_done,
     y_ready, act_kept, dve_kept, turned, x_added, stored) = st.sems(
        "hidden_ready", "up_ready", "mix_ready", "gate_done", "up_done", "h_done",
        "high_done", "low_done", "y_ready", "act_kept", "dve_kept", "turned", "x_added", "stored")
    n_tiles = shared + tiles

    def walk(engine, step):
        def four(i):
            for k in range(slots):
                step(i * slots + (shared + k), (shared + k) % slots, i + (shared + k) // slots, False)

        for j in range(shared):
            step(j, j % slots, j // slots, True)
        four(0)
        with engine.Fori(1, tiles // slots - 1) as i:
            four(i)
        four(tiles // slots - 1)
        step(n_tiles, n_tiles % slots, None, False)

    def exists(j, ahead):
        return not isinstance(j, int) or 0 <= j + ahead < n_tiles

    def w1(of, slot, c):
        return of[:, slot, c * P:(c + 1) * P]

    def w2(of, slot, o):
        return of[:, slot, D + o * P:D + (o + 1) * P]

    def wu(of, slot, c):
        return of[:, slot, 2 * D + P + c * P:2 * D + P + (c + 1) * P]

    def selector(slot):
        return high[0:2 * experts, slot, 2 * D:2 * D + P]

    with st.block() as block:

        @block.sync
        def _(sp):
            def step(j, slot, turn, is_shared):
                if exists(j, 0) and not (isinstance(j, int) and j < slots):
                    sp.wait_ge(weights.low_done, j + (1 - slots))
                    weights.load(sp, j, slot, is_shared)

            walk(sp, step)
            if out is not None:
                for n in range(halves):
                    tiles_of = slice(n * TT // halves, (n + 1) * TT // halves)
                    sp.wait_ge(x_added, (n + 1) * TT // halves)
                    sp.dma_start(out.rearrange("(t p) d -> p t d", p=P)[:, tiles_of, :], m.x[:, tiles_of, :]).then_inc(stored, 16)
                sp.wait_ge(stored, halves * 16)

        @block.tensor
        def _(pe):
            def product(bank, left, right):
                for c in range(DC):
                    (left_high, left_low), (right_high, right_low) = left(c), right(c)
                    pe.matmul(bank[:], left_high, right_high, start=(c == 0), stop=False)
                    pe.matmul(bank[:], left_high, right_low, start=False, stop=False)
                    last = pe.matmul(bank[:], left_low, right_high, start=False, stop=(c == DC - 1))
                return last

            def step(j, slot, turn, is_shared):
                first, final = isinstance(j, int) and j == 1, isinstance(j, int) and j == n_tiles
                old = (slot - 1) % slots
                if exists(j, 0):
                    pe.wait_ge(weights.low_done, j + 1)
                for n in range(halves):
                    columns = slice(n * BANK, (n + 1) * BANK)
                    half = j * halves + n

                    def tokens(c):
                        return m.x_high[:, c, columns], m.x_low[:, c, columns]

                    if exists(j, 0):
                        wait_for(pe, gate_done, half - 1)
                        product(hidden_bank[n], lambda c: (w1(high, slot, c), w1(low, slot, c)),
                                tokens).then_inc(hidden_ready, 1)
                        has_up = gated or is_shared
                        if has_up:
                            wait_for(pe, h_done, half)
                            product(up_bank, lambda c: (wu(high, slot, c), wu(low, slot, c)), tokens).then_inc(up_ready, 1)
                        if not is_shared:
                            after_shared = isinstance(j, int) and j == shared
                            wait_for(pe, h_done, half if gated or after_shared else half - 1)
                            pe.matmul((mix_bank if gated or n == 1 else up_bank)[:], selector(slot),
                                      m.mix[0:2 * experts, columns], start=True, stop=True).then_inc(mix_ready, 1)
                    if exists(j, -1):
                        pe.wait_ge(low_done, half + (1 - halves))
                        at = (slot - 1) % 2
                        for o in range(DC):
                            bank = y_bank[o * halves + n]
                            pe.matmul(bank[:], w2(high, old, o), h_high[:, at, columns], start=first, stop=False,
                                      skip_group_check=True)
                            pe.matmul(bank[:], w2(high, old, o), h_low[:, at, columns], start=False, stop=False,
                                      skip_group_check=True)
                            last = pe.matmul(bank[:], w2(low, old, o), h_high[:, at, columns], start=False, stop=final,
                                             skip_group_check=True)
                        last.then_inc(y_ready, 1)

            walk(pe, step)
            for t in range(TT):
                bank = hidden_bank[t % 2]
                if t % (TT // halves) == 0:
                    half = t * halves // TT
                    pe.wait_ge(act_kept, half + 1)
                    pe.wait_ge(dve_kept, half + 1)
                wait_for(pe, x_added, t - 1)
                for o in range(DC):
                    last = pe.transpose(bank[:, o * P:(o + 1) * P], y_t[:, o, t * P:(t + 1) * P], m.ident[:])
                last.then_inc(turned, 1)

        @block.scalar
        def _(act):
            def split(j, slot, turn, is_shared):
                wait_for(act, y_ready, j * halves + (1 - slots) * halves)
                weights.keep_high(act, slot, turn, is_shared)

            def step(j, slot, turn, is_shared):
                if exists(j, 0):
                    for n in range(halves):
                        half = j * halves + n
                        act.wait_ge(hidden_ready, half + 1)
                        wait_for(act, h_done, half - 1)
                        act.activation(gate[:, n, :], hidden_bank[n][:], ACT.Silu).then_inc(gate_done, 1)
                if exists(j, 2):
                    split(j + 2, (slot + 2) % slots, turn + (slot + 2) // slots, isinstance(j, int) and j + 2 < shared)
                if exists(j, 0):
                    for n in range(halves):
                        half = j * halves + n
                        act.wait_ge(h_done, half + 1)
                        wait_for(act, y_ready, half + (1 - 2 * halves))
                        act.copy(h_high[:, slot % 2, n * BANK:(n + 1) * BANK], h[:, n, :]).then_inc(high_done, 1)

            walk(act, step)
            for n in range(halves):
                act.wait_ge(y_ready, (n_tiles - 1) * halves + n + 1)
                act.copy(y_t[:, 0, n * BANK:(n + 1) * BANK], y_bank[n][:]).then_inc(act_kept, 1)

        @block.gpsimd
        def _(pool):
            def step(j, slot, turn, is_shared):
                if exists(j, 0) and not (isinstance(j, int) and j < weights.FIRST):
                    weights.keep_low(pool, j, slot, is_shared)

            walk(pool, step)

        @block.vector
        def _(dve):
            def step(j, slot, turn, is_shared):
                if exists(j, 0):
                    for n in range(halves):
                        half = j * halves + n
                        dve.wait_ge(gate_done, half + 1)
                        wait_for(dve, low_done, half - 1)
                        if is_shared:
                            dve.wait_ge(up_ready, half + 1)
                            dve.tensor_tensor(h[:, n, :], gate[:, n, :], up_bank[:], ALU.mult).then_inc(h_done, 1)
                        elif gated:
                            dve.wait_ge(up_ready, half + 1)
                            dve.tensor_tensor(upped[:, n, :], gate[:, n, :], up_bank[:], ALU.mult).then_inc(up_done, 1)
                            dve.wait_ge(up_done, half + 1)
                            dve.wait_ge(mix_ready, half + 1)
                            dve.tensor_tensor(h[:, n, :], upped[:, n, :], mix_bank[:], ALU.mult).then_inc(h_done, 1)
                        else:
                            dve.wait_ge(mix_ready, half + (1 - shared * halves))
                            dve.tensor_tensor(h[:, n, :], gate[:, n, :], (mix_bank if n else up_bank)[:],
                                              ALU.mult).then_inc(h_done, 1)
                    for n in range(halves):
                        half = j * halves + n
                        dve.wait_ge(high_done, half + 1)
                        columns = slice(n * BANK, (n + 1) * BANK)
                        dve.tensor_tensor(h_low[:, slot % 2, columns], h[:, n, :],
                                          h_high[:, slot % 2, columns].bitcast(F32), ALU.subtract).then_inc(low_done, 1)

            walk(dve, step)
            for n in range(halves):
                dve.wait_ge(y_ready, (n_tiles - 1) * halves + n + 1)
                dve.tensor_copy(y_t[:, 1, n * BANK:(n + 1) * BANK], y_bank[halves + n][:]).then_inc(dve_kept, 1)
            for t in range(TT):
                dve.wait_ge(turned, t + 1)
                dve.tensor_tensor(m.x[:, t, :], m.x[:, t, :], hidden_bank[t % 2][:, 0:D], ALU.add).then_inc(x_added, 1)


class Memory:

    def __init__(self, nc, stack):
        def sbuf(name, shape, dtype=F32):
            return stack.enter_context(nc.sbuf_tensor(name, shape, dtype))

        self.nc = nc
        self.banks = [stack.enter_context(nc.psum_tensor(f"bank{n}", [P, BANK], F32)) for n in range(8)]
        self.used_semaphores = []
        self.x = sbuf("x", [P, TT, D])
        self.ident = sbuf("ident", [P, P])
        self.ones = sbuf("ones", [P, 2])
        self.minus_half = sbuf("minus_half", [P, HEADS])

    def sbuf(self, stack, name, shape, dtype=F32):
        return stack.enter_context(self.nc.sbuf_tensor(name, shape, dtype))

    def context(self, stack):
        self.ctx_high = self.sbuf(stack, "ctx_high", [P, BATCH * KT, CW], F32R)
        self.ctx_low = self.sbuf(stack, "ctx_low", [P, BATCH * KT, CW], F32R)
        self.ctx_t_high = self.sbuf(stack, "ctx_t_high", [CW, BATCH * KEYS], F32R)
        self.ctx_t_low = self.sbuf(stack, "ctx_t_low", [CW, BATCH * KEYS], F32R)

    def tokens(self, stack, name, whole, parts, keep, mix, rms):
        if whole:
            self.x_t = self.sbuf(stack, name + "_x_t", [P, DC, TOKENS])
        if parts:
            self.x_high = self.sbuf(stack, name + "_x_high", [P, DC, TOKENS], F32R)
            self.x_low = self.sbuf(stack, name + "_x_low", [P, DC, TOKENS], F32R)
        if keep:
            self.x_n = self.sbuf(stack, name + "_x_n", [P, TT, D])
        if mix:
            self.mix = self.sbuf(stack, name + "_mix", [P, TOKENS], F32R)
        if rms:
            self.q_rms = self.sbuf(stack, name + "_q_rms", [P, HEADS * TT])

    def small_heads(self, stack):
        self.q0_t = self.sbuf(stack, "q0_t", [P, BATCH * GROUPS, 2 * P], F32R)
        self.k0_t = self.sbuf(stack, "k0_t", [P, BATCH * GROUPS, KEYS], F32R)
        self.v0 = self.sbuf(stack, "v0", [P, BATCH * GROUPS, KT, GROUP * H0])
        self.o0 = self.sbuf(stack, "o0", [P, BATCH * HEADS // 4, 2 * P])


CAPACITY3 = 2 * (TOKENS * 8 // 32)


def build(nc, dram):
    def of(prefix):
        return {k[len(prefix):]: v for k, v in dram.items() if k.startswith(prefix)} | {
            k: dram[k] for k in ("mask", "rms", "before", "pick", "ctx", "ctx_t")}

    with ExitStack() as stack:
        m = Memory(nc, stack)
        load_stage(nc, m, dram)

        def normed(name, *stages, whole=True, parts=True, keep=False, mix=False, rms=False):
            with ExitStack() as tokens:
                m.tokens(tokens, name, whole, parts, keep, mix, rms)
                for stage, *arguments in stages:
                    stage(nc, m, *arguments)

        normed("l0n", (small_attention, of("l0a_")), parts=False)
        m.context(stack)
        normed("l0g", (sparse_ffn_stage, of("l0f_")), whole=False)
        normed("l1n", (heads_stage, of("l1a_"), "l1a", True), whole=False, rms=True)
        normed("l1t", (thought_stage, of("l1f_")), parts=False, keep=True)
        normed("l2n", (heads_stage, of("l2a_"), "l2a", False), whole=False)
        normed("l2g", (mixture, of("l2f_"), "l2", 64, 6, None, 88, False, 3), mix=True)
        normed("l3n", (heads_stage, of("l3a_"), "l3a", False), whole=False)
        normed("l3g", (mixture, of("l3f_"), "l3", 32, 8, CAPACITY3, 24, True, 0, dram["out"]), mix=True)


def layouts(i):
    import numpy as _np

    def row_tiles(w):
        return w.reshape(-1, P, w.shape[-1])

    def in_tiles(w):
        return w.reshape(DC, P, -1, P).transpose(2, 1, 0, 3)

    def selectors(experts, width):
        owner = _np.arange(experts * width) // width
        of = (owner[None, :] == _np.arange(experts)[:, None]).astype(_np.float32).reshape(experts, -1, P).transpose(1, 0, 2)
        return _np.concatenate([of, of, _np.zeros((of.shape[0], P - 2 * experts, P), _np.float32)], 1)

    def packed(w1, w2, select, wu):
        return _np.concatenate([w.reshape(w.shape[0], P, -1) for w in (w1, w2, select, wu) if w is not None], 2)

    ctx = i["ctx_1024"].reshape(BATCH * KEYS, CW)
    a = {
        "x": i["x"].reshape(TOKENS, D), "ctx": ctx, "ctx_t": ctx.T, "mask": i["mask_BxS2_bf1"].reshape(-1).view(_np.uint8),
        "ident": _np.eye(P, dtype=_np.float32), "before": _np.triu(_np.ones((P, P), _np.float32), 1),
        "pick": _np.repeat(_np.eye(BATCH, dtype=_np.float32)[:, :, None], P, 2),
    }
    p = "L0_xattn_"
    a |= {f"l0a_{n}": i[p + w] for n, w in (
        ("wq", "Wq"), ("bq", "bq"), ("bo", "bo"), ("qn_w", "qn_w"), ("qn_b", "qn_b"), ("kn_w", "kn_w"), ("kn_b", "kn_b"),
        ("kn_dca_w", "kn_dca_w"), ("kn_dca_b", "kn_dca_b"))}
    a["l0a_wo"] = _np.pad(i[p + "Wo"].reshape(HEADS // 4, 4, H0, D), ((0, 0), (0, 0), (0, V0 - H0), (0, 0))).reshape(-1, P, D)
    a["l0a_wkv"] = _np.concatenate([i[p + "Wk"], i[p + "Wv"]], 1)
    a["l0a_bkv"] = _np.concatenate([i[p + "bk"], i[p + "bv"]])
    a["l0a_wkv_last"] = i[p + "Wkv_dca"].reshape(CW, 2, HEADS, H0).transpose(0, 2, 1, 3).reshape(CW, 2 * D)
    a["l0a_bkv_last"] = i[p + "bkv_dca"].reshape(2, HEADS, H0).transpose(1, 0, 2).reshape(2 * D)
    a |= {f"l0f_{n}": i["L0_ffn_" + n] for n in ("w_gate", "w_up", "w_down")}
    p = "L1_xattn_"
    a |= {"l1a_wq_all": i[p + "Wq"], "l1a_wk_all": i[p + "Wk"], "l1a_wq": row_tiles(i[p + "Wq"].T), "l1a_wk": row_tiles(i[p + "Wk"].T),
          "l1a_wv_t": row_tiles(i[p + "Wv"].T), "l1a_wo": row_tiles(i[p + "Wo"]),
          "l1a_gq": i[p + "gq"][:, None], "l1a_gk": i[p + "gk"][:, None]}
    a |= {f"l1f_{n}": i["L1_ffn_" + n] for n in ("in_gamma", "in_beta", "agg_w", "agg_b", "pn_gamma", "pn_beta", "d1_w", "d2_w", "d2_b",
                                                "bc_w", "bc_b", "gate_w", "gate_b", "out_gamma", "out_beta")}
    a["l1f_d1_b"] = i["L1_ffn_d1_b"].reshape(-1, P).T
    for n in (2, 3):
        p = f"L{n}_xattn_"
        a |= {f"l{n}a_wq": row_tiles(i[p + "Wq"].T), f"l{n}a_wk": row_tiles(i[p + "Wk"].T), f"l{n}a_wv_t": row_tiles(i[p + "Wv"].T),
              f"l{n}a_wo": row_tiles(i[p + "Wo"])}
    p = "L2_ffn_"
    inner = i[p + "shared_down"].shape[1]
    short = -inner % P
    gate, up = (_np.pad(w.T, ((0, 0), (0, short))) for w in (i[p + "shared_gate_up"][:inner], i[p + "shared_gate_up"][inner:]))
    nothing = _np.zeros((gate.shape[1] // P, P, P), _np.float32)
    a |= {"l2f_gate_w": i[p + "gate_w"].T,
          "l2f_w": packed(in_tiles(i[p + "experts_w1"].reshape(-1, D).T),
                          row_tiles(i[p + "experts_w2"].transpose(0, 2, 1).reshape(-1, D)), selectors(64, 176), None),
          "l2f_shared_w": packed(in_tiles(gate), row_tiles(_np.pad(i[p + "shared_down"].T, ((0, short), (0, 0)))), nothing,
                                 in_tiles(up))}
    p = "L3_ffn_"
    a |= {"l3f_gate_w": i[p + "gate_w"],
          "l3f_w": packed(in_tiles(i[p + "w_gate"].transpose(1, 0, 2).reshape(D, -1)), row_tiles(i[p + "w_down"].reshape(-1, D)),
                          selectors(32, 96), in_tiles(i[p + "w_up"].transpose(1, 0, 2).reshape(D, -1)))}
    return {n: _np.ascontiguousarray(v) for n, v in a.items()}


def kernel(**inputs):
    import numpy as _np
    import concourse.bacc as _bacc
    from concourse.bass_utils import run_bass_kernel_spmd as _run

    arrays = layouts({n: _np.asarray(v) for n, v in inputs.items()})
    nc = _bacc.Bacc("TRN2", target_bir_lowering=False, num_devices=1)
    dram = {n: nc.dram_tensor(f"in_{n}", v.shape, mybir.dt.from_np(v.dtype), kind="ExternalInput").ap() for n, v in arrays.items()}
    dram["rms"] = nc.dram_tensor("rms", (HEADS, BATCH * KT, P), F32, kind="Internal").ap()
    dram["out"] = nc.dram_tensor("out", (TOKENS, D), F32, kind="ExternalOutput").ap()
    build(nc, dram)
    r = _run(nc, [{f"in_{n}": v for n, v in arrays.items()}], core_ids=[0])
    return r.results[0]["out"].reshape(BATCH, TOKENS // BATCH, D)
```
